# Optimizing a Trainium2 kernel written in Bass

```python
import numpy as np
import jax
import jax.numpy as jnp

def _softmax(x, axis=-1):
    return jax.nn.softmax(x, axis=axis)

def _gelu(x):
    return jax.nn.gelu(x, approximate=True)

def _silu(x):
    return jax.nn.silu(x)

def _sigmoid(x):
    return jax.nn.sigmoid(x)

def _layernorm(x, axis=-1, eps=1e-05):
    m = jnp.mean(x, axis=axis, keepdims=True)
    v = jnp.var(x, axis=axis, keepdims=True)
    return (x - m) / jnp.sqrt(v + eps)

def _scatter_add(tgt, idx, src, axis=0):
    return tgt.at[idx].add(src)

def _segment_sum(src, seg, n):
    return jax.ops.segment_sum(src, seg, n)
kernel_name = 'mk_hybrid_d1_jaxref_r4_aa5c6a'

def setup_inputs(seed: int=0):
    np.random.seed(seed)
    _w = jnp.asarray

    def _L0_attn_a_setup():
        import jax, jax.numpy as jnp
        import numpy as np
        B, S, D = (4, 1024, 256)
        CHUNK = 64
        MAX_LR = 0.2
        MIN_DECAY = 0.5
        MAX_NORM = 30.0
        NORM_EPS = 1e-05

        def _forward(x, M_init, eta_w, eta_b, alpha_w, alpha_b, gate_w, gate_b, vg_w1, vg_w2):
            b, s, d = x.shape
            n_ch = s // CHUNK

            def value_gen(y):
                h = jax.nn.silu(y @ vg_w1.T) @ vg_w2.T
                return h + y
            x_chunks = x.reshape(b, n_ch, CHUNK, d).transpose(1, 0, 2, 3)
            M0 = jnp.broadcast_to(M_init, (b, d, d))

            def step(M, chunk):
                eta_tok = jax.nn.sigmoid(chunk @ eta_w + eta_b[0]) * MAX_LR
                alpha_tok = MIN_DECAY + jax.nn.sigmoid(chunk @ alpha_w + alpha_b[0]) * (1.0 - MIN_DECAY)
                eta = eta_tok.mean(axis=1)[:, None, None]
                alpha = alpha_tok.mean(axis=1)[:, None, None]
                outputs = jnp.einsum('bci,boi->bco', chunk, M)
                nrm = jnp.sqrt(jnp.sum(chunk * chunk, axis=-1, keepdims=True))
                keys = chunk / jnp.maximum(nrm, NORM_EPS)
                k_mean = keys.mean(axis=1)
                v_target = value_gen(outputs).mean(axis=1)
                Mk = jnp.einsum('boi,bi->bo', M, k_mean)
                err = v_target - Mk
                update = err[:, :, None] * k_mean[:, None, :]
                M_new = alpha * M + eta * update
                gate = jax.nn.sigmoid(k_mean @ gate_w + gate_b[0])[:, None, None]
                M_new = gate * M_new + (1.0 - gate) * M
                M_norm = jnp.sqrt(jnp.sum(M_new * M_new, axis=(-2, -1), keepdims=True))
                scale = jnp.minimum(MAX_NORM / (M_norm + 1e-06), 1.0)
                return (M_new * scale, outputs)
            M_final, outs = jax.lax.scan(step, M0, x_chunks)
            outs = outs.transpose(1, 0, 2, 3).reshape(b, s, d)
            final_out = value_gen(outs)
            return (final_out, M_final)

        def _reference_tuple_inner(x, M_init, eta_w, eta_b, alpha_w, alpha_b, gate_w, gate_b, vg_w1, vg_w2):
            return _forward(x, M_init, eta_w, eta_b, alpha_w, alpha_b, gate_w, gate_b, vg_w1, vg_w2)
        key = jax.random.key(seed)
        ks = jax.random.split(key, 10)
        return {'x': jax.random.normal(ks[0], (B, S, D), jnp.float32), 'M_init': jax.random.normal(ks[1], (D, D), jnp.float32) * 0.02, 'eta_w': jax.random.normal(ks[2], (D,), jnp.float32) * 0.02, 'eta_b': jax.random.normal(ks[3], (1,), jnp.float32), 'alpha_w': jax.random.normal(ks[4], (D,), jnp.float32) * 0.02, 'alpha_b': jax.random.normal(ks[5], (1,), jnp.float32), 'gate_w': jax.random.normal(ks[6], (D,), jnp.float32) * 0.02, 'gate_b': jax.random.normal(ks[7], (1,), jnp.float32), 'vg_w1': jax.random.normal(ks[8], (D, D), jnp.float32) * 0.02, 'vg_w2': jax.random.normal(ks[9], (D, D), jnp.float32) * 0.02}
    _L0_attn_a_in = _L0_attn_a_setup()

    def _L0_attn_b_setup():
        import jax, jax.numpy as jnp
        import numpy as np
        B, N, D_MODEL, H = (4, 512, 256, 16)
        key = jax.random.key(seed)
        k1, k2, k3 = jax.random.split(key, 3)
        x = jax.random.normal(k1, (B, N, D_MODEL), dtype=jnp.float32)
        Wqkv = jax.random.normal(k2, (3 * D_MODEL, D_MODEL), dtype=jnp.float32) * 0.02
        bqkv = jnp.zeros((3 * D_MODEL,), dtype=jnp.float32)
        Wo = jax.random.normal(k3, (D_MODEL, D_MODEL), dtype=jnp.float32) * 0.02
        bo = jnp.zeros((D_MODEL,), dtype=jnp.float32)
        return {'x': x, 'Wqkv': Wqkv, 'bqkv': bqkv, 'Wo': Wo, 'bo': bo}
    _L0_attn_b_in = _L0_attn_b_setup()

    def _L0_ffn_setup():
        import jax, jax.numpy as jnp
        import numpy as np
        B, S, H = (2, 1024, 256)
        E, K, I = (8, 2, 352)
        key = jax.random.key(seed)
        ks = jax.random.split(key, 9)
        sc = 0.02
        return {'hidden_states': jax.random.normal(ks[0], (B, S, H), jnp.float32), 'gate_w': jax.random.normal(ks[1], (E, H), jnp.float32) * sc, 'w_gate': jax.random.normal(ks[2], (E, H, I), jnp.float32) * sc, 'w_up': jax.random.normal(ks[3], (E, H, I), jnp.float32) * sc, 'w_down': jax.random.normal(ks[4], (E, I, H), jnp.float32) * sc, 'sw_gate': jax.random.normal(ks[5], (H, I), jnp.float32) * sc, 'sw_up': jax.random.normal(ks[6], (H, I), jnp.float32) * sc, 'sw_down': jax.random.normal(ks[7], (I, H), jnp.float32) * sc, 'shared_gate_w': jax.random.normal(ks[8], (1, H), jnp.float32) * sc}
    _L0_ffn_in = _L0_ffn_setup()
    _d = {'L0_attn_a_x': _L0_attn_a_in['x'], 'L0_attn_a_M_init': _L0_attn_a_in['M_init'], 'L0_attn_a_eta_w': _L0_attn_a_in['eta_w'], 'L0_attn_a_eta_b': _L0_attn_a_in['eta_b'], 'L0_attn_a_alpha_w': _L0_attn_a_in['alpha_w'], 'L0_attn_a_alpha_b': _L0_attn_a_in['alpha_b'], 'L0_attn_a_gate_w': _L0_attn_a_in['gate_w'], 'L0_attn_a_gate_b': _L0_attn_a_in['gate_b'], 'L0_attn_a_vg_w1': _L0_attn_a_in['vg_w1'], 'L0_attn_a_vg_w2': _L0_attn_a_in['vg_w2'], 'L0_attn_b_Wqkv': _L0_attn_b_in['Wqkv'], 'L0_attn_b_bqkv': _L0_attn_b_in['bqkv'], 'L0_attn_b_Wo': _L0_attn_b_in['Wo'], 'L0_attn_b_bo': _L0_attn_b_in['bo'], 'L0_ffn_gate_w': _L0_ffn_in['gate_w'], 'L0_ffn_w_gate': _L0_ffn_in['w_gate'], 'L0_ffn_w_up': _L0_ffn_in['w_up'], 'L0_ffn_w_down': _L0_ffn_in['w_down'], 'L0_ffn_sw_gate': _L0_ffn_in['sw_gate'], 'L0_ffn_sw_up': _L0_ffn_in['sw_up'], 'L0_ffn_sw_down': _L0_ffn_in['sw_down'], 'L0_ffn_shared_gate_w': _L0_ffn_in['shared_gate_w']}
    _x0 = _d['L0_attn_a_x']
    _d['L0_attn_a_x'] = jax.random.normal(jax.random.fold_in(jax.random.key(seed), 1), (4, 1024, 256), dtype=_x0.dtype)
    del _x0
    return _d

def reference(L0_attn_a_x, L0_attn_a_M_init, L0_attn_a_eta_w, L0_attn_a_eta_b, L0_attn_a_alpha_w, L0_attn_a_alpha_b, L0_attn_a_gate_w, L0_attn_a_gate_b, L0_attn_a_vg_w1, L0_attn_a_vg_w2, L0_attn_b_Wqkv, L0_attn_b_bqkv, L0_attn_b_Wo, L0_attn_b_bo, L0_ffn_gate_w, L0_ffn_w_gate, L0_ffn_w_up, L0_ffn_w_down, L0_ffn_sw_gate, L0_ffn_sw_up, L0_ffn_sw_down, L0_ffn_shared_gate_w):

    def _L0_attn_a_ref(x, M_init, eta_w, eta_b, alpha_w, alpha_b, gate_w, gate_b, vg_w1, vg_w2):
        import jax, jax.numpy as jnp
        import numpy as np
        B, S, D = (4, 1024, 256)
        CHUNK = 64
        MAX_LR = 0.2
        MIN_DECAY = 0.5
        MAX_NORM = 30.0
        NORM_EPS = 1e-05

        def _forward(x, M_init, eta_w, eta_b, alpha_w, alpha_b, gate_w, gate_b, vg_w1, vg_w2):
            b, s, d = x.shape
            n_ch = s // CHUNK

            def value_gen(y):
                h = jax.nn.silu(y @ vg_w1.T) @ vg_w2.T
                return h + y
            x_chunks = x.reshape(b, n_ch, CHUNK, d).transpose(1, 0, 2, 3)
            M0 = jnp.broadcast_to(M_init, (b, d, d))

            def step(M, chunk):
                eta_tok = jax.nn.sigmoid(chunk @ eta_w + eta_b[0]) * MAX_LR
                alpha_tok = MIN_DECAY + jax.nn.sigmoid(chunk @ alpha_w + alpha_b[0]) * (1.0 - MIN_DECAY)
                eta = eta_tok.mean(axis=1)[:, None, None]
                alpha = alpha_tok.mean(axis=1)[:, None, None]
                outputs = jnp.einsum('bci,boi->bco', chunk, M)
                nrm = jnp.sqrt(jnp.sum(chunk * chunk, axis=-1, keepdims=True))
                keys = chunk / jnp.maximum(nrm, NORM_EPS)
                k_mean = keys.mean(axis=1)
                v_target = value_gen(outputs).mean(axis=1)
                Mk = jnp.einsum('boi,bi->bo', M, k_mean)
                err = v_target - Mk
                update = err[:, :, None] * k_mean[:, None, :]
                M_new = alpha * M + eta * update
                gate = jax.nn.sigmoid(k_mean @ gate_w + gate_b[0])[:, None, None]
                M_new = gate * M_new + (1.0 - gate) * M
                M_norm = jnp.sqrt(jnp.sum(M_new * M_new, axis=(-2, -1), keepdims=True))
                scale = jnp.minimum(MAX_NORM / (M_norm + 1e-06), 1.0)
                return (M_new * scale, outputs)
            M_final, outs = jax.lax.scan(step, M0, x_chunks)
            outs = outs.transpose(1, 0, 2, 3).reshape(b, s, d)
            final_out = value_gen(outs)
            return (final_out, M_final)

        def _reference_tuple_inner(x, M_init, eta_w, eta_b, alpha_w, alpha_b, gate_w, gate_b, vg_w1, vg_w2):
            return _forward(x, M_init, eta_w, eta_b, alpha_w, alpha_b, gate_w, gate_b, vg_w1, vg_w2)
        return _reference_tuple_inner(x, M_init, eta_w, eta_b, alpha_w, alpha_b, gate_w, gate_b, vg_w1, vg_w2)[0]

    def _L0_attn_b_ref(x, Wqkv, bqkv, Wo, bo):
        import jax, jax.numpy as jnp
        import numpy as np
        B, N, D_MODEL, H = (4, 512, 256, 16)
        b, n, _ = x.shape
        qkv = x @ Wqkv.T + bqkv
        qkv = qkv.reshape(b, n, H, -1).transpose(0, 2, 1, 3)
        q, k, v = jnp.split(qkv, 3, axis=-1)
        scale = k.shape[-1] ** 0.5
        scores = jnp.einsum('bhqd,bhkd->bhqk', q, k) / scale
        attn = jax.nn.softmax(scores, axis=-1)
        out = jnp.einsum('bhqk,bhkd->bhqd', attn, v)
        out = out.transpose(0, 2, 1, 3).reshape(b, n, -1)
        return out @ Wo.T + bo

    def _L0_ffn_ref(hidden_states, gate_w, w_gate, w_up, w_down, sw_gate, sw_up, sw_down, shared_gate_w):
        import jax, jax.numpy as jnp
        import numpy as np
        B, S, H = (2, 1024, 256)
        E, K, I = (8, 2, 352)
        b, s, h = hidden_states.shape
        x = hidden_states.reshape(-1, h)
        logits = jnp.einsum('th,eh->te', x, gate_w)
        probs = jax.nn.softmax(logits.astype(jnp.float32), axis=-1)
        topk_w, topk_i = jax.lax.top_k(probs, K)
        topk_w = topk_w / jnp.sum(topk_w, axis=-1, keepdims=True)
        combine = jnp.sum(jax.nn.one_hot(topk_i, E, dtype=topk_w.dtype) * topk_w[..., None], axis=1)
        combine = combine.astype(x.dtype)
        g = jnp.einsum('th,ehi->eti', x, w_gate)
        u = jnp.einsum('th,ehi->eti', x, w_up)
        eo = jnp.einsum('eti,eih->eth', jax.nn.silu(g) * u, w_down)
        out = jnp.einsum('te,eth->th', combine, eo)
        sg = jax.nn.sigmoid(jnp.einsum('th,oh->to', x, shared_gate_w))
        so = jax.nn.silu(x @ sw_gate) * (x @ sw_up) @ sw_down
        out = out + sg * so
        return out.reshape(b, s, h)
    x = L0_attn_a_x
    x = x + _L0_attn_a_ref(_layernorm(x, axis=-1), L0_attn_a_M_init, L0_attn_a_eta_w, L0_attn_a_eta_b, L0_attn_a_alpha_w, L0_attn_a_alpha_b, L0_attn_a_gate_w, L0_attn_a_gate_b, L0_attn_a_vg_w1, L0_attn_a_vg_w2)
    x = x + _L0_ffn_ref(_layernorm(x, axis=-1), L0_ffn_gate_w, L0_ffn_w_gate, L0_ffn_w_up, L0_ffn_w_down, L0_ffn_sw_gate, L0_ffn_sw_up, L0_ffn_sw_down, L0_ffn_shared_gate_w)
    x = x + _L0_attn_b_ref(_layernorm(x, axis=-1), L0_attn_b_Wqkv, L0_attn_b_bqkv, L0_attn_b_Wo, L0_attn_b_bo)
    x = x + _L0_ffn_ref(_layernorm(x, axis=-1), L0_ffn_gate_w, L0_ffn_w_gate, L0_ffn_w_up, L0_ffn_w_down, L0_ffn_sw_gate, L0_ffn_sw_up, L0_ffn_sw_down, L0_ffn_shared_gate_w)
    return x

_drawn_inputs = setup_inputs


def setup_inputs(seed=0):
    import zlib

    import numpy as np

    out = dict(_drawn_inputs(seed))
    spreads = {'L0_attn_b_bqkv': (0.0, 0.268), 'L0_attn_b_bo': (0.0, 0.1)}
    factors = {'L0_attn_a_eta_w': 200.0,
     'L0_attn_a_alpha_w': 79.035,
     'L0_attn_a_gate_w': 200.0,
     'L0_attn_a_vg_w1': 5.482,
     'L0_attn_a_vg_w2': 5.494,
     'L0_attn_b_Wqkv': 8.0,
     'L0_ffn_sw_gate': 2.964,
     'L0_ffn_sw_up': 2.937,
     'L0_ffn_sw_down': 2.933,
     'L0_ffn_shared_gate_w': 8.0}
    for name, (base, spread) in spreads.items():
        noise = np.random.default_rng([zlib.crc32(name.encode()), seed]).standard_normal(out[name].shape)
        drawn = base * np.exp(spread * noise) if base else spread * noise
        out[name] = jnp.asarray(drawn.astype(out[name].dtype))
    for name, factor in factors.items():
        out[name] = (out[name] * factor).astype(out[name].dtype)
    return out
```

```python
import concourse.bass as bass
from concourse import mybir
from contextlib import ExitStack

F32 = mybir.dt.float32
I32 = mybir.dt.int32
U32 = mybir.dt.uint32
BF16 = mybir.dt.bfloat16
ALU = mybir.AluOpType
ACT = mybir.ActivationFunctionType
AX = mybir.AxisListType

P = 128
B, S, D = 4, 1024, 256
TOKENS = B * S
NT = TOKENS // P
KD = D // P
E, TOPK, I = 8, 2, 352
SHARED = E
IP = -(-I // P) * P
KI = IP // P
NB = (TOKENS * TOPK) // P + E
EPS = 1e-5


def new_semaphore(nc, sems, name):
    sems.append(nc.alloc_semaphore(name))
    return sems[-1]


def release(nc, sems):
    nc.clear_and_free_semaphores(sems)
    nc.all_engine_barrier()


def ffn_phase(nc, tag, X, ident, ones, W, weights_loaded, xs, ys, xs_filled, store=None):
    ctx = ExitStack()
    sems = []
    ctx.callback(release, nc, sems)
    with ctx:
        sb = lambda n, s, d=F32: ctx.enter_context(nc.sbuf_tensor(f"{tag}_{n}", s, d))
        sem = lambda n: new_semaphore(nc, sems, f"{tag}_{n}")
        xn_all = sb("xn_all", [P, NT, D])
        src = [sb(f"src{u}", [P, D]) for u in range(2)]
        srcT = [sb(f"srcT{u}", [P, KD, P]) for u in range(2)]
        silu = [sb(f"silu{u}", [P, I]) for u in range(2)]
        hid = [sb(f"hid{u}", [P, IP]) for u in range(2)]
        hidT = [sb(f"hidT{u}", [P, KI, P]) for u in range(2)]
        yb = [sb(f"yb{u}", [P, D]) for u in range(2)]
        GS = 8
        got = sb("got", [P, GS, TOPK, D])
        st = sb("st", [P, NT, 6])
        mv = sb("mv", [P, NT, 2])
        rstd = sb("rstd", [P, NT])
        eps = sb("eps", [P, 1])
        lg = sb("lg", [P, NT, E + 1])
        iota8 = sb("iota8", [P, E])
        upper = sb("upper", [P, P])
        iotab = sb("iotab", [1, NB])
        one256 = sb("one256", [P, NT * E])
        eq = sb("eq", [P, NT, E])
        pk = [sb(f"pk{k}", [P, NT, E]) for k in range(TOPK)]
        mx = [sb(f"mx{k}", [P, NT]) for k in range(TOPK)]
        ix = sb("ix", [P, NT])
        lg2 = sb("lg2", [P, NT, E])
        gap = sb("gap", [P, NT])
        cw = [sb(f"cw{k}", [P, NT]) for k in range(TOPK)]
        sg = sb("sg", [P, NT])
        both = sb("both", [P, NT, E])
        tot = sb("tot", [P, E, NT])
        cum = sb("cum", [P, E, NT])
        exc = sb("exc", [P, E, NT])
        slot = sb("slot", [P, E, NT])
        cnt = sb("cnt", [P, E])
        cnti = sb("cnti", [P, E], I32)
        nblk = sb("nblk", [P, E])
        bend = sb("bend", [P, E])
        base = sb("base", [P, E])
        posf = sb("posf", [P, NT])
        pos = [sb(f"pos{k}", [P, NT], I32) for k in range(TOPK)]
        ble = sb("ble", [1, NB, E])
        bex = sb("bex", [1, NB])
        bexi = sb("bexi", [1, NB], I32)

        ps = [ctx.enter_context(nc.psum_tensor(f"{tag}_ps{i}", [P, 512], F32)) for i in range(8)]
        psT, psH, psG, psU, psD = ps[0], ps[1], ps[2:4], ps[4:6], ps[6:8]
        psL, psR = ps[2], ps[4]

        consts_done = sem("consts_done")
        iota_zeroed = sem("iota_zeroed")
        std_done = sem("std_done")
        var_done = sem("var_done")
        l_src = sem("l_src"); l_T = sem("l_T"); l_srcT = sem("l_srcT"); l_lg = sem("l_lg")
        ms_done = sem("ms_done"); rank_done = sem("rank_done")
        top_done = sem("top_done"); gates_done = sem("gates_done")
        bex_done = sem("bex_done"); pos_done = sem("pos_done")
        scattered = sem("scattered")
        src_ready = sem("src_ready")
        src_loaded = [sem(f"src_loaded{u}") for u in range(2)]
        T_done = sem("T_done"); srcT_ready = sem("srcT_ready")
        g_done = sem("g_done"); u_done = sem("u_done"); silu_done = sem("silu_done")
        hid_ready = sem("hid_ready"); hT_done = sem("hT_done"); hidT_ready = sem("hidT_ready")
        d_done = sem("d_done"); d_used = sem("d_used")
        y_ready = sem("y_ready")
        y_stored = [sem(f"y_stored{u}") for u in range(2)]
        gathered = [sem(f"gathered{s}") for s in range(GS)]
        got_used = sem("got_used")

        NS = NT + NB

        block = ctx.enter_context(nc.Block())

        @block.sync
        def _(sp):
            sp.wait_ge(scattered, 16 * NT * TOPK)
            with sp.Fori(0, NB // 2) as jj:
                for u in range(2):
                    sp.wait_ge(T_done, jj * 2 + (NT + u - 1))
                    sp.dma_start(src[u][:, :], xs.rearrange("(j p) d -> j p d", p=P)[jj * 2 + u]
                                 ).then_inc(src_loaded[u], 16)
            if store is not None:
                out_pt, stored = store
                HN = NT // 4
                for q in range(4):
                    sp.wait_ge(got_used, HN * (q + 1))
                    sp.dma_start(out_pt[:, q * HN:(q + 1) * HN, :], X[:, q * HN:(q + 1) * HN, :]).then_inc(stored, 16)
                sp.wait_ge(stored, 64)

        @block.gpsimd
        def _(pool):
            nc.gpsimd.iota(iota8[:, :], [[1, E]], base=-E, channel_multiplier=0,
                           allow_small_or_imprecise_dtypes=True)
            nc.gpsimd.iota(iotab[:, :], [[1, NB]], base=0, channel_multiplier=0,
                           allow_small_or_imprecise_dtypes=True)
            nc.gpsimd.memset(one256[:, :], 1.0)
            nc.gpsimd.memset(upper[:, :], 1.0).then_inc(iota_zeroed, 1)
            pool.wait_ge(iota_zeroed, 1)
            nc.gpsimd.affine_select(out=upper[:, :], in_=upper[:, :], compare_op=ALU.is_gt, fill=0.0,
                                    base=0, pattern=[[1, P]], channel_multiplier=-1).then_inc(consts_done, 1)
            pool.wait_ge(pos_done, 1)
            pool.wait_ge(xs_filled[0], xs_filled[1])
            for k in range(TOPK):
                for t in range(NT):
                    nc.gpsimd.indirect_dma_start(
                        out=xs, out_offset=bass.IndirectOffsetOnAxis(ap=pos[k][:, t:t + 1].bitcast(U32), axis=0),
                        in_=xn_all[:, t, :], in_offset=None).then_inc(scattered, 16)
            for u in range(2):
                pool.wait_ge(y_stored[u], 16 * (NB // 2))
            for t in range(NT):
                if t >= GS:
                    pool.wait_ge(got_used, t - GS + 1)
                for k in range(TOPK):
                    nc.gpsimd.indirect_dma_start(
                        out=got[:, t % GS, k, :], out_offset=None, in_=ys,
                        in_offset=bass.IndirectOffsetOnAxis(ap=pos[k][:, t:t + 1].bitcast(U32), axis=0)
                    ).then_inc(gathered[t % GS], 16)

        @block.scalar
        def _(act):
            act.wait_ge(var_done, 1)
            nc.scalar.activation(rstd[:, :], mv[:, :, 1], ACT.Sqrt, bias=eps[:, :]).then_inc(std_done, 1)
            nc.scalar.preload_act_table(ACT.Sigmoid)
            with act.Fori(0, NT // 2) as tt:
                for u in range(2):
                    act.wait_ge(l_T, tt * 2 + (u + 1))
                    nc.scalar.copy(srcT[u][:, :, :].rearrange("p k t -> p (k t)"), psT[:, 0:D]).then_inc(l_srcT, 1)
            act.wait_ge(top_done, 1)
            nc.scalar.activation(cw[0][:, :], gap[:, :], ACT.Sigmoid)
            nc.scalar.activation(cw[1][:, :], gap[:, :], ACT.Sigmoid, scale=-1.0)
            nc.scalar.activation(sg[:, :], lg[:, :, E], ACT.Sigmoid).then_inc(gates_done, 1)
            nc.scalar.preload_act_table(ACT.Silu)

            def source_out(n, u):
                act.wait_ge(T_done, n + 1)
                nc.scalar.copy(srcT[u][:, :, :].rearrange("p k t -> p (k t)"), psT[:, 0:D]).then_inc(srcT_ready, 1)

            def silu_step(n, u):
                act.wait_ge(g_done, n + 1)
                nc.scalar.activation(silu[u][:, :], psG[u][:, 0:I], ACT.Silu).then_inc(silu_done, 1)

            def y_out(n, u, first=False):
                act.wait_ge(d_done, n + 1)
                if not first:
                    act.wait_ge(y_stored[u], (n - NT - u) * 8)
                nc.scalar.copy(yb[u][:, :], psD[u][:, 0:D]).then_inc(y_ready, 1)
                act.wait_ge(y_ready, n - (NT - 1))
                act.dma_start(ys.rearrange("(j p) d -> j p d", p=P)[n - NT], yb[u][:, :]).then_inc(y_stored[u], 16)

            source_out(0, 0)
            with act.Fori(0, NT // 2) as tt:
                for u in range(2):
                    silu_step(tt * 2 + u, u)
                    source_out(tt * 2 + (u + 1), 1 - u)
            silu_step(NT, 0)
            source_out(NT + 1, 1)
            silu_step(NT + 1, 1)
            source_out(NT + 2, 0)
            y_out(NT, 0, True)
            silu_step(NT + 2, 0)
            source_out(NT + 3, 1)
            y_out(NT + 1, 1, True)
            with act.Fori(0, NB // 2 - 2) as jj:
                for u in range(2):
                    n = jj * 2 + (NT + 3 + u)
                    silu_step(n, 1 - u)
                    source_out(n + 1, u)
                    y_out(n - 1, u)
            silu_step(NS - 1, 1)
            y_out(NS - 2, 0)
            y_out(NS - 1, 1)

        @block.vector
        def _(dve):
            nc.vector.memset(eps[:, :], EPS)
            for u in range(2):
                nc.vector.memset(hid[u][:, I:IP], 0.0)
            with dve.Fori(0, NT) as t:
                nc.vector.bn_stats(st[:, t, :], X[:, t, :])
            dve.drain()
            for t in range(NT):
                nc.vector.bn_aggr(mv[:, t, :], st[:, t, :])
            dve.drain().then_inc(var_done, 1)
            dve.wait_ge(std_done, 1)
            nc.vector.reciprocal(rstd[:, :], rstd[:, :])
            dve.drain()

            def normalise(dst, t):
                return nc.vector.tensor_scalar(dst, X[:, t, :], mv[:, t, 0:1], rstd[:, bass.ds(t, 1)],
                                               ALU.subtract, ALU.mult)

            for t in range(2):
                normalise(src[t][:, :], t).then_inc(l_src, 1)
                normalise(xn_all[:, t, :], t)
            with dve.Fori(1, NT // 2) as tt:
                for u in range(2):
                    dve.wait_ge(l_T, tt * 2 + (u - 1))
                    normalise(src[u][:, :], tt * 2 + u).then_inc(l_src, 1)
                    normalise(xn_all[:, tt * 2 + u, :], tt * 2 + u)
            dve.wait_ge(l_lg, 1)
            dve.wait_ge(consts_done, 1)
            nc.vector.tensor_copy(lg[:, :, :].rearrange("p t e -> p (t e)"), psL[:, 0:NT * (E + 1)])
            dve.drain()
            over_e = lambda v: v[:, :, None].to_broadcast([P, NT, E])
            index = iota8[:, None, :].to_broadcast([P, NT, E])
            for k in range(TOPK):
                at = lg[:, :, 0:E] if k == 0 else lg2[:, :, :]
                nc.vector.tensor_reduce(mx[k][:, :], at, AX.X, ALU.max)
                dve.drain()
                nc.vector.tensor_tensor(eq[:, :, :], at, over_e(mx[k]), ALU.is_equal)
                dve.drain()
                nc.vector.tensor_tensor(eq[:, :, :], eq[:, :, :], index, ALU.mult)
                dve.drain()
                nc.vector.tensor_reduce(ix[:, :], eq[:, :, :], AX.X, ALU.min)
                dve.drain()
                nc.vector.tensor_tensor(pk[k][:, :, :], index, over_e(ix), ALU.is_equal)
                dve.drain()
                if k == 0:
                    nc.vector.scalar_tensor_tensor(lg2[:, :, :], pk[0][:, :, :], -3.0e38, lg[:, :, 0:E],
                                                   ALU.mult, ALU.add)
                    dve.drain()
            nc.vector.tensor_tensor(both[:, :, :], pk[0][:, :, :], pk[1][:, :, :], ALU.add).then_inc(ms_done, 1)
            nc.vector.tensor_tensor(gap[:, :], mx[0][:, :], mx[1][:, :], ALU.subtract).then_inc(top_done, 1)
            dve.wait_ge(rank_done, 1)
            by_e = lambda ap: ap.rearrange("p (t e) -> p e t", e=E)
            flat = lambda v: v[:, :, :].rearrange("p e t -> p (e t)")
            nc.vector.tensor_copy(tot[:, :, :], by_e(psR[:, NT * E:2 * NT * E]))
            dve.drain()
            nc.vector.tensor_tensor_scan(flat(cum), one256[:, :], flat(tot), 0.0, ALU.mult, ALU.add)
            dve.drain()
            nc.vector.tensor_tensor(exc[:, :, :], cum[:, :, :], tot[:, :, :], ALU.subtract)
            dve.drain()
            nc.vector.tensor_tensor(cnt[:, :], cum[:, :, NT - 1], exc[:, :, 0], ALU.subtract)
            dve.drain()
            nc.vector.tensor_scalar(cnti[:, :], cnt[:, :], float(P - 1), None, ALU.add)
            dve.drain()
            nc.vector.tensor_scalar(cnti[:, :], cnti[:, :], P.bit_length() - 1, None, ALU.arith_shift_right)
            dve.drain()
            nc.vector.tensor_copy(nblk[:, :], cnti[:, :])
            dve.drain()
            nc.vector.tensor_tensor_scan(bend[:, :], one256[:, 0:E], nblk[:, :], 0.0, ALU.mult, ALU.add)
            dve.drain()
            nc.vector.tensor_tensor(base[:, :], bend[:, :], nblk[:, :], ALU.subtract)
            dve.drain()
            nc.vector.scalar_tensor_tensor(base[:, :], base[:, :], float(P), exc[:, :, 0], ALU.mult, ALU.subtract)
            nc.vector.tensor_tensor(ble[:, :, :], bend[0:1, None, :].to_broadcast([1, NB, E]),
                                    iotab[:, :, None].to_broadcast([1, NB, E]), ALU.is_le)
            dve.drain()
            nc.vector.tensor_reduce(bex[:, :], ble[:, :, :], AX.X, ALU.add)
            nc.vector.tensor_tensor(slot[:, :, :], exc[:, :, :],
                                    base[:, :, None].to_broadcast([P, E, NT]), ALU.add)
            dve.drain()
            nc.vector.tensor_scalar(bexi[:, :], bex[:, :], float(E - 1), None, ALU.min).then_inc(bex_done, 1)
            nc.vector.tensor_tensor(slot[:, :, :], slot[:, :, :], by_e(psR[:, 0:NT * E]), ALU.add)
            dve.drain()
            for k in range(TOPK):
                nc.vector.tensor_tensor(eq[:, :, :], pk[k][:, :, :], slot[:, :, :].rearrange("p e t -> p t e"), ALU.mult)
                dve.drain()
                nc.vector.tensor_reduce(posf[:, :], eq[:, :, :], AX.X, ALU.add)
                dve.drain()
                last = nc.vector.tensor_copy(pos[k][:, :], posf[:, :])
            last.then_inc(pos_done, 1)

            def hidden(n, u):
                dve.wait_ge(u_done, n + 1)
                dve.wait_ge(silu_done, n + 1)
                nc.vector.tensor_tensor(hid[u][:, 0:I], silu[u][:, :], psU[u][:, 0:I], ALU.mult).then_inc(hid_ready, 1)

            def hidden_out(n, u):
                dve.wait_ge(hT_done, n + 1)
                nc.vector.tensor_copy(hidT[u][:, :, :].rearrange("p k t -> p (k t)"), psH[:, 0:IP]).then_inc(hidT_ready, 1)

            def add_shared(n, u):
                dve.wait_ge(d_done, n + 1)
                nc.vector.scalar_tensor_tensor(X[:, n, :], psD[u][:, 0:D], sg[:, bass.ds(n, 1)], X[:, n, :],
                                               ALU.mult, ALU.add).then_inc(d_used, 1)

            def source(n, u):
                dve.wait_ge(T_done, n - 1)
                normalise(src[u][:, :], n).then_inc(src_ready, 1)

            dve.wait_ge(gates_done, 1)
            normalise(src[0][:, :], 0).then_inc(src_ready, 1)
            normalise(src[1][:, :], 1).then_inc(src_ready, 1)
            hidden(0, 0)
            with dve.Fori(0, NT // 2 - 1) as tt:
                for u in range(2):
                    n = tt * 2 + u
                    source(n + 2, u)
                    hidden_out(n, u)
                    hidden(n + 1, 1 - u)
                    add_shared(n, u)
            hidden_out(NT - 2, 0)
            hidden(NT - 1, 1)
            add_shared(NT - 2, 0)
            hidden_out(NT - 1, 1)
            hidden(NT, 0)
            add_shared(NT - 1, 1)
            with dve.Fori(0, NB // 2 - 1) as jj:
                for u in range(2):
                    n = jj * 2 + (NT + u)
                    hidden_out(n, u)
                    hidden(n + 1, 1 - u)
            hidden_out(NS - 2, 0)
            hidden(NS - 1, 1)
            hidden_out(NS - 1, 1)
            for t0 in range(0, NT, GS // 2):
                tiles = range(t0, t0 + GS // 2)
                for t in tiles:
                    dve.wait_ge(gathered[t % GS], 16 * TOPK * (t // GS + 1))
                    nc.vector.scalar_tensor_tensor(X[:, t, :], got[:, t % GS, 0, :], cw[0][:, t:t + 1], X[:, t, :],
                                                   ALU.mult, ALU.add)
                dve.drain()
                for t in tiles:
                    nc.vector.scalar_tensor_tensor(X[:, t, :], got[:, t % GS, 1, :], cw[1][:, t:t + 1], X[:, t, :],
                                                   ALU.mult, ALU.add).then_inc(got_used, 1)

        @block.tensor
        def _(pe):
            def transpose_rows(u):
                for k in range(KD):
                    last = nc.tensor.transpose(psT[:, k * P:(k + 1) * P], src[u][:, k * P:(k + 1) * P], ident[:, :])
                return last

            pe.wait_ge(weights_loaded[0], weights_loaded[1])
            with pe.Fori(0, NT // 2) as tt:
                for u in range(2):
                    t = tt * 2 + u
                    pe.wait_ge(l_src, t + 1)
                    transpose_rows(u).then_inc(l_T, 1)
                    pe.wait_ge(l_srcT, t + 1)
                    for k in range(KD):
                        last = nc.tensor.matmul(psL[:, bass.ds(t * (E + 1), E + 1)], srcT[u][:, k, :],
                                                W["router"][:, k, :], start=(k == 0), stop=(k == KD - 1))
            pe.drain().then_inc(l_lg, 1)
            pe.wait_ge(ms_done, 1)
            msf = both[:, :, :].rearrange("p t e -> p (t e)")
            nc.tensor.matmul(psR[:, 0:NT * E], upper[:, :], msf, start=True, stop=True)
            nc.tensor.matmul(psR[:, NT * E:2 * NT * E], ones[:, :], msf, start=True, stop=True).then_inc(rank_done, 1)

            def rows_in(n, u, routed):
                if routed:
                    pe.wait_ge(src_loaded[u], (n - NT - u) * 8 + 16)
                else:
                    pe.wait_ge(src_ready, n + 1)
                pe.wait_ge(srcT_ready, n)
                transpose_rows(u).then_inc(T_done, 1)

            def gate_up(n, u, e, first=False):
                pe.wait_ge(srcT_ready, n + 1)
                if not first:
                    pe.wait_ge(hid_ready, n - 1)
                for half, (bank, done) in enumerate(((psG, g_done), (psU, u_done))):
                    for k in range(KD):
                        last = nc.tensor.matmul(bank[u][:, 0:I], srcT[u][:, k, :],
                                                W["gate_up"][:, k, e, half * I:(half + 1) * I],
                                                start=(k == 0), stop=(k == KD - 1))
                    last.then_inc(done, 1)

            def hidden_T(n, u, first=False):
                pe.wait_ge(hid_ready, n + 1)
                if not first:
                    pe.wait_ge(hidT_ready, n)
                for k in range(KI):
                    last = nc.tensor.transpose(psH[:, k * P:(k + 1) * P], hid[u][:, k * P:(k + 1) * P], ident[:, :])
                last.then_inc(hT_done, 1)

            def down(n, u, e, used):
                pe.wait_ge(hidT_ready, n + 1)
                if used is not None:
                    pe.wait_ge(*used)
                for k in range(KI):
                    last = nc.tensor.matmul(psD[u][:, 0:D], hidT[u][:, k, :], W["down"][:, k, e, :],
                                            start=(k == 0), stop=(k == KI - 1))
                last.then_inc(d_done, 1)

            pe.wait_ge(src_ready, 1)
            transpose_rows(0).then_inc(T_done, 1)
            gate_up(0, 0, SHARED, True)
            rows_in(1, 1, False)
            hidden_T(0, 0, True)
            gate_up(1, 1, SHARED, True)
            rows_in(2, 0, False)
            down(0, 0, SHARED, None)
            hidden_T(1, 1)
            gate_up(2, 0, SHARED)
            rows_in(3, 1, False)
            down(1, 1, SHARED, None)
            with pe.Fori(1, NT // 2 - 1) as tt:
                for u in range(2):
                    n = tt * 2 + (1 + u)
                    hidden_T(n - 1, u)
                    gate_up(n, 1 - u, SHARED)
                    rows_in(n + 1, u, False)
                    down(n - 1, u, SHARED, (d_used, n - 2))
            n = NT - 1
            hidden_T(n - 1, 0)
            gate_up(n, 1, SHARED)
            rows_in(n + 1, 0, True)
            down(n - 1, 0, SHARED, (d_used, n - 2))
            pe.wait_ge(bex_done, 1)
            expert = lambda j: pe.value_load(bexi[0:1, bass.ds(j, 1)], min_val=0, max_val=E - 1)
            hidden_T(n, 1)
            gate_up(NT, 0, expert(0))
            rows_in(NT + 1, 1, True)
            down(n, 1, SHARED, (d_used, n - 1))
            hidden_T(NT, 0)
            gate_up(NT + 1, 1, expert(1))
            rows_in(NT + 2, 0, True)
            down(NT, 0, expert(0), (d_used, NT - 1))
            hidden_T(NT + 1, 1)
            gate_up(NT + 2, 0, expert(2))
            rows_in(NT + 3, 1, True)
            down(NT + 1, 1, expert(1), (d_used, NT))
            with pe.Fori(0, NB // 2 - 2) as jj:
                for u in range(2):
                    j = jj * 2 + (3 + u)
                    n = j + NT
                    hidden_T(n - 1, u)
                    gate_up(n, 1 - u, expert(j))
                    rows_in(n + 1, u, True)
                    down(n - 1, u, expert(j - 1), (y_ready, j - 2))
            hidden_T(NS - 2, 0)
            gate_up(NS - 1, 1, expert(NB - 1))
            down(NS - 2, 0, expert(NB - 2), (y_ready, NB - 3))
            hidden_T(NS - 1, 1)
            down(NS - 1, 1, expert(NB - 1), (y_ready, NB - 2))


CHUNK = 64
NC = S // CHUNK
HALVES = P // CHUNK
XC = CHUNK + 2
ROWS = NC * B
MAX_LR, MIN_DECAY, MAX_NORM, NORM_EPS = 0.2, 0.5, 30.0, 1e-5


def memory_phase(nc, tag, X, ident, ones, m0T, w1T, w2T, weights_loaded, rates_w, rates_b, gate_w, gate_b):
    ctx = ExitStack()
    sems = []
    ctx.callback(release, nc, sems)
    with ctx:
        sb = lambda n, s, d=F32: ctx.enter_context(nc.sbuf_tensor(f"{tag}_{n}", s, d))
        sem = lambda n: new_semaphore(nc, sems, f"{tag}_{n}")
        xT = sb("xT", [P, KD, NC, B, XC])
        km = sb("km", [P, KD, NC, B])
        G = sb("G", [P, NC, B, XC])
        xn = [sb(f"xn{u}", [P, D]) for u in range(2)]
        st = sb("st", [P, NT, 6]); mv = sb("mv", [P, NT, 2]); rstd = sb("rstd", [P, NT]); eps = sb("eps", [P, 1])
        ss = sb("ss", [P, NT]); nrm = sb("nrm", [P, NT])
        half = sb("half", [P, HALVES])
        mean_w = sb("mean_w", [P, NT, 2 * HALVES])
        seq = sb("seq", [ROWS, B])
        gwb = sb("gwb", [P, KD, P])
        esel = sb("esel", [2, 2, P])
        sig = [sb(f"sig{u}", [2, B, XC]) for u in range(2)]
        ea = sb("ea", [2, NC, B])
        kk2 = sb("kk2", [P, KD, ROWS]); kks = sb("kks", [P, ROWS])
        m0n = sb("m0n", [P, 1])
        gate = sb("gate", [P, NC, B]); dec = sb("dec", [P, NC, B]); cdec = sb("cdec", [P, NC, B])
        beta = sb("beta", [P, NC, B]); boc = sb("boc", [P, NC, B]); rc = sb("rc", [P, NC, B])
        c2 = sb("c2", [P, NC, B]); coef = sb("coef", [P, NC, 2, B]); kk = sb("kk", [P, NC, B])
        A = sb("A", [P, B]); n2 = sb("n2", [P, B]); n2c = sb("n2c", [P, B]); cA = sb("cA", [P, B])
        f = sb("f", [P, B]); rA = sb("rA", [P, B]); t2 = sb("t2", [P, 2, B]); root = sb("root", [P, B]); scl = sb("scl", [P, B])
        halfpow = sb("halfpow", [P, B])
        w2s = sb("w2s", [P, KD, D])
        ET = sb("ET", [P, KD, NC, B]); Erow = sb("Erow", [P, D])
        y = [sb(f"y{q}", [P, KD, B, HALVES, CHUNK]) for q in range(2)]
        ye = [sb(f"ye{v}", [P, KD, B, 2]) for v in range(2)]
        h = [sb(f"h{q}", [P, KD, B, HALVES, CHUNK]) for q in range(2)]
        hs = sb("hs", [P, KD, B])
        e = sb("e", [P, KD, B]); prod = sb("prod", [P, KD, 2, B]); prods = sb("prods", [P, 2, B])

        ps = [ctx.enter_context(nc.psum_tensor(f"{tag}_ps{i}", [P, 512], F32)) for i in range(8)]
        psO = [ps[0:2], ps[2:4]]; psU = ps[4:6]; psE = ps[6]; psF = ps[7]
        psT, psM, psA, psG, psK = ps[0:2], ps[2], ps[3:5], ps[5:7], ps[7]

        consts = sem("consts"); var_done = sem("var_done"); std_done = sem("std_done")
        ss_done = sem("ss_done"); nrm_done = sem("nrm_done"); meanw_done = sem("meanw_done")
        n_ready = sem("n_ready"); T_done = sem("T_done"); xT_ready = sem("xT_ready"); mean_done = sem("mean_done")
        xc_ready = sem("xc_ready"); ea_done = sem("ea_done"); sig_ready = sem("sig_ready"); ea_ready = sem("ea_ready")
        G_done = sem("G_done"); G_ready = sem("G_ready"); kk_ready = sem("kk_ready"); sc_done = sem("sc_done")
        gate_ready = sem("gate_ready"); start_ready = sem("start_ready")
        o_done = sem("o_done"); y_ready = sem("y_ready"); u_done = sem("u_done"); h_ready = sem("h_ready")
        hs_ready = sem("hs_ready"); e_done = sem("e_done"); ET_ready = sem("ET_ready"); ER_done = sem("ER_done")
        Erow_ready = sem("Erow_ready"); prods_ready = sem("prods_ready"); pq_done = sem("pq_done")
        n2_ready = sem("n2_ready"); root_ready = sem("root_ready"); f_done = sem("f_done"); f_used = sem("f_used")
        cz = sem("cz")

        block = ctx.enter_context(nc.Block())

        @block.gpsimd
        def _(pool):
            nc.gpsimd.memset(G[:, :, :, :], 0.0)
            nc.gpsimd.memset(ET[:, :, :, :], 0.0)
            nc.gpsimd.memset(Erow[:, :], 0.0)
            nc.gpsimd.memset(halfpow[:, :], 0.5)
            nc.gpsimd.memset(half[:, :], 0.0)
            nc.gpsimd.memset(esel[:, 0, :], MAX_LR / CHUNK)
            nc.gpsimd.memset(esel[:, 1, :], (1.0 - MIN_DECAY) / CHUNK).then_inc(cz, 1)
            pool.wait_ge(cz, 1)
            nc.gpsimd.memset(half[0:CHUNK, 0:1], 1.0 / CHUNK)
            nc.gpsimd.memset(half[CHUNK:P, 1:2], 1.0 / CHUNK)
            nc.gpsimd.affine_select(out=esel[:, 0, :], in_=esel[:, 0, :], compare_op=ALU.is_equal, fill=0.0,
                                    base=0, pattern=[[0, P]], channel_multiplier=1)
            nc.gpsimd.affine_select(out=esel[:, 1, :], in_=esel[:, 1, :], compare_op=ALU.is_equal, fill=0.0,
                                    base=-1, pattern=[[0, P]], channel_multiplier=1).then_inc(consts, 1)
            with pool.Fori(0, NC) as t:
                pool.wait_ge(n2_ready, t + 1)
                nc.gpsimd.tensor_tensor(root[:, :], n2[:, :], halfpow[:, :], ALU.pow).then_inc(root_ready, 1)

        @block.scalar
        def _(act):
            act.wait_ge(var_done, 1)
            nc.scalar.activation(rstd[:, :], mv[:, :, 1], ACT.Sqrt, bias=eps[:, :]).then_inc(std_done, 1)
            act.wait_ge(ss_done, 1)
            nc.scalar.sqrt(nrm[:, :], ss[:, :]).then_inc(nrm_done, 1)
            nc.scalar.preload_act_table(ACT.Sigmoid)
            with act.Fori(0, B) as b:
                with act.Fori(0, NT // B // 2) as cc:
                    for u in range(2):
                        act.wait_ge(T_done, b * (NT // B) + cc * 2 + (u + 1))
                        for k in range(KD):
                            last = nc.scalar.copy(xT[:, k, bass.ds(cc * 4 + 2 * u, HALVES), b, 0:CHUNK],
                                                  psT[u][:, k * P:(k + 1) * P].rearrange("p (c s) -> p c s", c=HALVES))
                        last.then_inc(xT_ready, 1)
            act.wait_ge(sc_done, 1)
            nc.scalar.activation(gate[:, :, :].rearrange("p t b -> p (t b)"), psK[:, 0:ROWS], ACT.Sigmoid,
                                 bias=gate_b[:, :]).then_inc(gate_ready, 1)

            def rates(t, u):
                act.wait_ge(ea_done, t + 1)
                nc.scalar.activation(sig[u][:, :, :].rearrange("p b c -> p (b c)"), psA[u][0:2, 0:B * XC],
                                     ACT.Sigmoid, bias=rates_b[:, :]).then_inc(sig_ready, 1)

            for u in range(2):
                rates(u, u)
            with act.Fori(1, NC // 2) as tt:
                for u in range(2):
                    act.wait_ge(ea_ready, tt * 2 + (u - 1))
                    rates(tt * 2 + u, u)
            nc.scalar.preload_act_table(ACT.Silu)
            with act.Fori(0, NC // 4) as tq:
                for v in range(4):
                    t = tq * 4 + v
                    for j in range(KD):
                        act.wait_ge(u_done, t * KD + (j + 1))
                        nc.scalar.activation(h[v // 2][:, j, :, v % 2, :],
                                             psU[j][:, 0:B * CHUNK].rearrange("p (b s) -> p b s", b=B),
                                             ACT.Silu).then_inc(h_ready, 1)
                    act.wait_ge(ER_done, t + 1)
                    nc.scalar.copy(Erow[0:ROWS, :], psE[0:ROWS, D:2 * D]).then_inc(Erow_ready, 1)

        @block.vector
        def _(dve):
            nc.vector.memset(eps[:, :], EPS)
            with dve.Fori(0, NT) as t:
                nc.vector.bn_stats(st[:, t, :], X[:, t, :])
            dve.drain()
            for t in range(NT):
                nc.vector.bn_aggr(mv[:, t, :], st[:, t, :])
            dve.drain().then_inc(var_done, 1)
            dve.wait_ge(std_done, 1)
            nc.vector.reciprocal(rstd[:, :], rstd[:, :])
            dve.drain()
            nc.vector.tensor_tensor(ss[:, :], mv[:, :, 1], rstd[:, :], ALU.mult)
            dve.drain()
            nc.vector.tensor_tensor(ss[:, :], ss[:, :], rstd[:, :], ALU.mult)
            dve.drain()
            nc.vector.tensor_scalar(ss[:, :], ss[:, :], float(D), NORM_EPS ** 2, ALU.mult, ALU.max).then_inc(ss_done, 1)

            def normalise(b, i, u):
                t = b * (NT // B) + i
                nc.vector.tensor_scalar(xn[u][:, :], X[:, t, :], mv[:, t, 0:1], rstd[:, bass.ds(t, 1)],
                                        ALU.subtract, ALU.mult).then_inc(n_ready, 1)

            for u in range(2):
                normalise(0, u, u)
            dve.wait_ge(nrm_done, 1)
            nc.vector.reciprocal(nrm[:, :], nrm[:, :])
            dve.wait_ge(consts, 1)
            dve.drain()
            nc.vector.tensor_tensor(mean_w[:, :, 0:HALVES], nrm[:, :, None].to_broadcast([P, NT, HALVES]),
                                    half[:, None, :].to_broadcast([P, NT, HALVES]), ALU.mult)
            nc.vector.tensor_copy(mean_w[:, :, HALVES:], half[:, None, :].to_broadcast([P, NT, HALVES])).then_inc(meanw_done, 1)
            TB = NT // B
            for i in range(2, TB):
                dve.wait_ge(mean_done, i - 1)
                normalise(0, i, i % 2)
            with dve.Fori(1, B) as b:
                with dve.Fori(0, TB // 2) as cc:
                    for u in range(2):
                        dve.wait_ge(mean_done, b * TB + cc * 2 + (u - 1))
                        normalise(b, cc * 2 + u, u)
            dve.wait_ge(*weights_loaded)
            for k in range(KD):
                nc.vector.tensor_copy(gwb[:, k, :], gate_w[:, k:k + 1].to_broadcast([P, P]))
            nc.vector.tensor_scalar(w2s[:, :, :], w2T[:, :, :], 1.0 / CHUNK, None, ALU.mult)
            nc.vector.tensor_reduce(seq[:, :], ident[0:ROWS, 0:ROWS].rearrange("p (t b) -> p b t", b=B), AX.X, ALU.add)
            flat0 = m0T[:, :, :].rearrange("p k o -> p (k o)")
            squares = h[0][:, :, :, :, :].rearrange("p k b c s -> p (k b c s)")[:, 0:KD * D]
            nc.vector.scalar_tensor_tensor(squares, flat0, 1.0, flat0, ALU.mult, ALU.mult, accum_out=m0n[:, :])
            dve.wait_ge(mean_done, NT)
            dve.wait_ge(xT_ready, NT)
            for k in range(KD):
                means = psM[:, k * NT * 4:(k + 1) * NT * 4].rearrange("p (b i c) -> p b i c", b=B, c=2 * HALVES)
                tb = lambda v: v.rearrange("p (i c) b -> p b i c", c=HALVES)
                for b in range(B):
                    nc.vector.tensor_copy(tb(km[:, k, :, :])[:, b], means[:, b, :, 0:HALVES])
                    nc.vector.tensor_copy(tb(xT[:, k, :, :, CHUNK])[:, b], means[:, b, :, 0:HALVES])
            dve.drain()
            for k in range(KD):
                means = psM[:, k * NT * 4:(k + 1) * NT * 4].rearrange("p (b i c) -> p b i c", b=B, c=2 * HALVES)
                for b in range(B):
                    nc.vector.tensor_tensor(tb(xT[:, k, :, :, CHUNK + 1])[:, b], means[:, b, :, HALVES:],
                                            tb(km[:, k, :, :])[:, b], ALU.subtract)
            kmf = km[:, :, :, :].rearrange("p k t b -> p k (t b)")
            nc.vector.tensor_tensor(kk2[:, :, :], kmf, kmf, ALU.mult)
            dve.drain().then_inc(xc_ready, 1)
            nc.vector.tensor_tensor(kks[:, :], kk2[:, 0, :], kk2[:, 1, :], ALU.add).then_inc(kk_ready, 1)
            with dve.Fori(0, NC // 2) as tt:
                for u in range(2):
                    t = tt * 2 + u
                    dve.wait_ge(G_done, t + 1)
                    nc.vector.tensor_tensor(G[0:ROWS, t, :, :], psG[u][0:ROWS, 0:B * XC].rearrange("p (b c) -> p b c", b=B),
                                            seq[:, :, None].to_broadcast([ROWS, B, XC]), ALU.mult).then_inc(G_ready, 1)
                    dve.wait_ge(sig_ready, t + 1)
                    nc.vector.tensor_reduce(ea[:, t, :], sig[u][:, :, 0:CHUNK], AX.X, ALU.add).then_inc(ea_ready, 1)
            dve.wait_ge(gate_ready, 1)
            dve.wait_ge(sc_done, 2)
            fl = lambda v: v[:, :, :].rearrange("p t b -> p (t b)")
            nc.vector.tensor_copy(fl(kk), psK[:, ROWS:2 * ROWS])
            nc.vector.tensor_copy(n2[:, :], psK[:, 2 * ROWS:2 * ROWS + 1].to_broadcast([P, B]))
            nc.vector.tensor_tensor(fl(beta), psK[:, 256:256 + ROWS], fl(gate), ALU.mult)
            nc.vector.tensor_scalar(fl(dec), psK[:, 256 + ROWS:256 + 2 * ROWS], MIN_DECAY - 1.0, None, ALU.add)
            dve.drain()
            nc.vector.tensor_tensor(fl(cdec), fl(dec), fl(gate), ALU.mult)
            dve.drain()
            nc.vector.tensor_scalar(fl(dec), fl(cdec), 1.0, None, ALU.add)
            dve.drain()
            nc.vector.reciprocal(fl(rc), fl(dec))
            nc.vector.tensor_tensor(fl(c2), fl(dec), fl(dec), ALU.mult)
            nc.vector.scalar_tensor_tensor(coef[:, :, 0, :], dec[:, :, :], 2.0, beta[:, :, :], ALU.mult, ALU.mult)
            nc.vector.tensor_tensor(fl(gate), fl(beta), fl(beta), ALU.mult)
            dve.drain()
            nc.vector.tensor_tensor(fl(boc), fl(beta), fl(rc), ALU.mult)
            nc.vector.tensor_tensor(coef[:, :, 1, :], gate[:, :, :], kk[:, :, :], ALU.mult)
            nc.vector.memset(A[:, :], 1.0)
            nc.vector.memset(rA[:, :], 1.0)
            dve.drain().then_inc(start_ready, 1)

            def step(tq, v, no_result):
                t = tq * 4 + v
                q, c = v // 2, v % 2
                for o in range(KD):
                    dve.wait_ge(o_done, t * KD + (o + 1))
                    out = psO[v % 2][o][:, 0:B * XC].rearrange("p (b c) -> p b c", b=B)
                    nc.vector.tensor_tensor(y[q][:, o, :, c, :], out[:, :, 0:CHUNK],
                                            A[:, :, None].to_broadcast([P, B, CHUNK]), ALU.mult)
                    nc.vector.tensor_tensor(ye[v % 2][:, o, :, :], out[:, :, CHUNK:],
                                            A[:, :, None].to_broadcast([P, B, 2]), ALU.mult).then_inc(y_ready, 1)
                nc.vector.tensor_tensor(f[:, :], boc[:, t, :], rA[:, :], ALU.mult)
                nc.vector.tensor_tensor(n2c[:, :], c2[:, t, :], n2[:, :], ALU.mult)
                nc.vector.tensor_tensor(cA[:, :], dec[:, t, :], A[:, :], ALU.mult)
                for j in range(KD):
                    dve.wait_ge(h_ready, t * KD + (j + 1))
                    nc.vector.tensor_reduce(hs[:, j, :], h[q][:, j, :, c, :], AX.X, ALU.add).then_inc(hs_ready, 1)
                if not no_result:
                    result(tq, v, 0)
                dve.wait_ge(e_done, t + 1)
                nc.vector.tensor_tensor(e[:, :, :], psE[:, 0:KD * B].rearrange("p (k b) -> p k b", k=KD),
                                        ye[v % 2][:, :, :, 1], ALU.add)
                dve.drain()
                nc.vector.tensor_tensor(ET[:, :, t, :], e[:, :, :], f[:, None, :].to_broadcast([P, KD, B]),
                                        ALU.mult).then_inc(ET_ready, 1)
                nc.vector.tensor_tensor(prod[:, :, 0, :], e[:, :, :], ye[v % 2][:, :, :, 0], ALU.mult)
                nc.vector.tensor_tensor(prod[:, :, 1, :], e[:, :, :], e[:, :, :], ALU.mult)
                dve.drain()
                nc.vector.tensor_tensor(prods[:, :, :], prod[:, 0, :, :], prod[:, 1, :, :], ALU.add).then_inc(prods_ready, 1)
                if not no_result:
                    result(tq, v, 1)
                dve.wait_ge(pq_done, t + 1)
                nc.vector.tensor_tensor(t2[:, :, :], coef[:, t, :, :], psU[1][:, 256:256 + 2 * B].rearrange("p (q b) -> p q b", q=2),
                                        ALU.mult)
                dve.drain()
                nc.vector.tensor_tensor(n2c[:, :], n2c[:, :], t2[:, 0, :], ALU.add)
                dve.drain()
                nc.vector.tensor_tensor(n2c[:, :], n2c[:, :], t2[:, 1, :], ALU.add)
                dve.drain()
                nc.vector.tensor_scalar(n2[:, :], n2c[:, :], 0.0, None, ALU.max).then_inc(n2_ready, 1)
                dve.wait_ge(root_ready, t + 1)
                nc.vector.tensor_scalar(scl[:, :], root[:, :], 1e-6, None, ALU.add)
                dve.drain()
                nc.vector.reciprocal(scl[:, :], scl[:, :])
                dve.drain()
                nc.vector.tensor_scalar(scl[:, :], scl[:, :], MAX_NORM, 1.0, ALU.mult, ALU.min)
                dve.drain()
                nc.vector.tensor_tensor(A[:, :], cA[:, :], scl[:, :], ALU.mult)
                nc.vector.tensor_tensor(n2[:, :], n2[:, :], scl[:, :], ALU.mult)
                dve.drain()
                nc.vector.reciprocal(rA[:, :], A[:, :])
                nc.vector.tensor_tensor(n2[:, :], n2[:, :], scl[:, :], ALU.mult)
                dve.drain()

            def result(tq, v, i):
                pair = tq * 2 + (0 if v >= 2 else -1)
                b = v % 2 * 2 + i
                dve.wait_ge(f_done, tq * 8 + (v - 2) * 2 + (i + 1))
                nc.vector.tensor_tensor(X[:, pair + b * (NT // B), :], X[:, pair + b * (NT // B), :], psF[:, 0:D],
                                        ALU.add).then_inc(f_used, 1)

            for v in range(4):
                step(0, v, v < 2)
            with dve.Fori(1, NC // 4) as tq:
                for v in range(4):
                    step(tq, v, False)
            for v in range(2):
                for i in range(2):
                    result(NC // 4, v, i)

        @block.tensor
        def _(pe):
            TB = NT // B
            pe.wait_ge(meanw_done, 1)

            def rows_in(b, i, u, first=False):
                t = b * TB + i
                pe.wait_ge(n_ready, t + 1)
                if not first:
                    pe.wait_ge(xT_ready, t - 1)
                for k in range(KD):
                    last = nc.tensor.transpose(psT[u][:, k * P:(k + 1) * P], xn[u][:, k * P:(k + 1) * P], ident[:, :])
                last.then_inc(T_done, 1)
                for k in range(KD):
                    last = nc.tensor.matmul(psM[:, bass.ds((t + k * NT) * 4, 4)], xn[u][:, k * P:(k + 1) * P],
                                            mean_w[:, t, :], start=True, stop=True)
                last.then_inc(mean_done, 1)

            for i in range(TB):
                rows_in(0, i, i % 2, i < 2)
            with pe.Fori(1, B) as b:
                with pe.Fori(0, TB // 2) as cc:
                    for u in range(2):
                        rows_in(b, cc * 2 + u, u)
            pe.wait_ge(xc_ready, 1)
            kmf = [km[:, k, :, :].rearrange("p t b -> p (t b)") for k in range(KD)]
            for k in range(KD):
                last = nc.tensor.matmul(psK[:, 0:ROWS], gwb[:, k, :], kmf[k], start=(k == 0), stop=(k == KD - 1))
            pe.wait_ge(kk_ready, 1)
            nc.tensor.matmul(psK[:, ROWS:2 * ROWS], ones[:, :], kks[:, :], start=True, stop=True)
            nc.tensor.matmul(psK[:, 2 * ROWS:2 * ROWS + 1], ones[:, :], m0n[:, :], start=True, stop=True).then_inc(sc_done, 1)

            def rates_and_products(t, u, first):
                if not first:
                    pe.wait_ge(sig_ready, t - 1)
                    pe.wait_ge(G_ready, t - 1)
                for k in range(KD):
                    xk = xT[:, k, t, :, :].rearrange("p b c -> p (b c)")
                    last = nc.tensor.matmul(psA[u][0:2, 0:B * XC], rates_w[:, k, :], xk, start=(k == 0), stop=(k == KD - 1))
                last.then_inc(ea_done, 1)
                for k in range(KD):
                    xk = xT[:, k, t, :, :].rearrange("p b c -> p (b c)")
                    last = nc.tensor.matmul(psG[u][0:ROWS, 0:B * XC], kmf[k], xk, start=(k == 0), stop=(k == KD - 1))
                last.then_inc(G_done, 1)

            for u in range(2):
                rates_and_products(u, u, True)
            with pe.Fori(1, NC // 2) as tt:
                for u in range(2):
                    rates_and_products(tt * 2 + u, u, False)
            pe.wait_ge(ea_ready, NC)
            pe.wait_ge(gate_ready, 1)
            for i in range(2):
                last = nc.tensor.matmul(psK[:, 256 + i * ROWS:256 + (i + 1) * ROWS], esel[:, i, :],
                                        ea[:, :, :].rearrange("p t b -> p (t b)"), start=True, stop=True)
            last.then_inc(sc_done, 1)
            pe.wait_ge(start_ready, 1)
            pe.wait_ge(G_ready, NC)

            def first_memory(t, v, o):
                for k in range(KD):
                    nc.tensor.matmul(psO[v % 2][o][:, 0:B * XC], m0T[:, k, o * P:(o + 1) * P],
                                     xT[:, k, t, :, :].rearrange("p b c -> p (b c)"), start=(k == 0), stop=False)

            def result(tq, v, i):
                q = 0 if v >= 2 else 1
                b = v % 2 * 2 + i
                count = tq * 8 + (v - 2) * 2 + i
                if not (isinstance(tq, int) and tq == 0 and v == 2 and i == 0):
                    pe.wait_ge(f_used, count)
                for k in range(KD):
                    nc.tensor.matmul(psF[:, 0:D], h[q][:, k, b, :, :].rearrange("p c s -> p (c s)"), w2T[:, k, :],
                                     start=(k == 0), stop=False, skip_group_check=True)
                for o in range(KD):
                    last = nc.tensor.matmul(psF[:, o * P:(o + 1) * P], y[q][:, o, b, :, :].rearrange("p c s -> p (c s)"),
                                            ident[:, :], start=False, stop=(o == KD - 1), skip_group_check=True)
                last.then_inc(f_done, 1)

            def step(tq, v, no_result, first=False, last_step=False):
                t = tq * 4 + v
                q, c = v // 2, v % 2
                if not first:
                    pe.wait_ge(Erow_ready, t)
                for o in range(KD):
                    nc.tensor.matmul(psO[v % 2][o][:, 0:B * XC], Erow[:, o * P:(o + 1) * P],
                                     G[:, t, :, :].rearrange("p b c -> p (b c)"), start=False, stop=True).then_inc(o_done, 1)
                if not last_step:
                    if not first:
                        pe.wait_ge(y_ready, t * KD)
                    first_memory(t + 1, v + 1, 0)
                pe.wait_ge(y_ready, t * KD + KD)
                if not first:
                    pe.wait_ge(n2_ready, t)
                for j in range(KD):
                    for o in range(KD):
                        last = nc.tensor.matmul(psU[j][:, 0:B * CHUNK], w1T[:, o, j * P:(j + 1) * P],
                                                y[q][:, o, :, c, :], start=(o == 0), stop=(o == KD - 1))
                    last.then_inc(u_done, 1)
                if not last_step:
                    first_memory(t + 1, v + 1, 1)
                if not no_result:
                    result(tq, v, 0)
                pe.wait_ge(hs_ready, t * KD + KD)
                for o in range(KD):
                    for j in range(KD):
                        last = nc.tensor.matmul(psE[:, o * B:(o + 1) * B], w2s[:, j, o * P:(o + 1) * P], hs[:, j, :],
                                                start=(j == 0), stop=(j == KD - 1))
                last.then_inc(e_done, 1)
                if not no_result:
                    result(tq, v, 1)
                pe.wait_ge(ET_ready, t + 1)
                for o in range(KD):
                    last = nc.tensor.matmul(psE[0:ROWS, D + o * P:D + (o + 1) * P], ET[:, o, :, :].rearrange("p t b -> p (t b)"),
                                            ident[:, :], start=True, stop=True)
                last.then_inc(ER_done, 1)
                pe.wait_ge(prods_ready, t + 1)
                nc.tensor.matmul(psU[1][:, 256:256 + 2 * B], ones[:, :], prods[:, :, :].rearrange("p q b -> p (q b)"),
                                 start=True, stop=True).then_inc(pq_done, 1)

            for o in range(KD):
                first_memory(0, 0, o)
            for v in range(4):
                step(0, v, v < 2, v == 0)
            with pe.Fori(1, NC // 4 - 1) as tq:
                for v in range(4):
                    step(tq, v, False)
            for v in range(4):
                step(NC // 4 - 1, v, False, False, v == 3)
            for v in range(2):
                for i in range(2):
                    result(NC // 4, v, i)


HEADS, HD = 16, 16
GROUP = 4
NG = HEADS // GROUP
CT = 4
CW = CT * P
NCH = TOKENS // CW
QT = S // P
HALF = 512
Q_PARTS = [0, 0, 0, 1, 1, 2]
K_PARTS = [0, 1, 2, 0, 1, 0]
KROWS = len(Q_PARTS) * HD
MROWS = KROWS + 3
VC = HD + 1


def qkv_phase(nc, tag, X, ident, wqk, wv, bqk, bv, bo, weights_loaded, qk_d, v_d):
    ctx = ExitStack()
    sems = []
    ctx.callback(release, nc, sems)
    with ctx:
        sb = lambda n, s, d=F32: ctx.enter_context(nc.sbuf_tensor(f"{tag}_{n}", s, d))
        sem = lambda n: new_semaphore(nc, sems, f"{tag}_{n}")
        xn = [sb(f"xn{j}", [P, D]) for j in range(CT)]
        xT = [sb(f"xT{u}", [P, KD, CW]) for u in range(2)]
        st = sb("st", [P, NT, 6]); mv = sb("mv", [P, NT, 2]); rstd = sb("rstd", [P, NT]); eps = sb("eps", [P, 1])
        NM = 2 * KD
        parts = [[sb(f"parts{u}{m}", [P, 3, CW], BF16) for m in range(NM)] for u in range(2)]
        rest = [[sb(f"rest{u}{m}", [P, CW]) for m in range(NM)] for u in range(2)]
        vt = [[sb(f"vt{u}{j}", [P, HEADS, VC]) for j in range(CT)] for u in range(2)]
        ps = [ctx.enter_context(nc.psum_tensor(f"{tag}_ps{i}", [P, 512], F32)) for i in range(8)]
        psT, psQ, psV = ps[0:2], ps[2:6], ps[6:8]

        var_done = sem("var_done"); std_done = sem("std_done")
        n_ready = sem("n_ready"); T_done = sem("T_done"); xT_ready = sem("xT_ready")
        qk_done = sem("qk_done"); hi_ready = sem("hi_ready"); rest_ready = sem("rest_ready")
        mid_ready = sem("mid_ready"); lo_ready = sem("lo_ready")
        v_done = sem("v_done"); v_ready = sem("v_ready")
        parts_stored = [sem(f"parts_stored{u}") for u in range(2)]
        v_stored = [sem(f"v_stored{u}") for u in range(2)]

        block = ctx.enter_context(nc.Block())

        @block.sync
        def _(sp):
            with sp.Fori(0, NCH // 2) as cc:
                for u in range(2):
                    for m in range(NM):
                        sp.wait_ge(lo_ready, cc * (2 * NM) + (u * NM + m + 1))
                        sp.dma_start(qk_d[m // KD, :, cc, (m % KD) * P:(m % KD + 1) * P, u * CW:(u + 1) * CW]
                                     .rearrange("s p t -> p s t"), parts[u][m][:, :, :]).then_inc(parts_stored[u], 16)
                    for j in range(CT):
                        sp.wait_ge(v_ready, cc * (2 * CT) + (u * CT + j + 1))
                        sp.dma_start(v_d[cc, :, :, u * CT + j, :].rearrange("g p c -> p g c"),
                                     vt[u][j][:, :, :].rearrange("p (g h) c -> p g (h c)", g=NG)).then_inc(v_stored[u], 16)
            for u in range(2):
                sp.wait_ge(parts_stored[u], 16 * NM * (NCH // 2))
                sp.wait_ge(v_stored[u], 16 * CT * (NCH // 2))

        @block.gpsimd
        def _(pool):
            pool.wait_ge(*weights_loaded)
            with pool.Fori(0, NCH // 2) as cc:
                for u in range(2):
                    for m in range(NM):
                        pool.wait_ge(mid_ready, cc * (2 * NM) + (u * NM + m + 1))
                        nc.gpsimd.tensor_tensor(parts[u][m][:, 2, :], rest[u][m][:, :], parts[u][m][:, 1, :],
                                                ALU.subtract).then_inc(lo_ready, 1)
                    for j in range(CT):
                        pool.wait_ge(n_ready, cc * (2 * CT) + (u * CT + j + 1))
                        t = cc * (2 * CT) + (u * CT + j)
                        nc.gpsimd.tensor_tensor(X[:, t, :], X[:, t, :], bo[:, :], ALU.add)

        @block.scalar
        def _(act):
            act.wait_ge(var_done, 1)
            nc.scalar.activation(rstd[:, :], mv[:, :, 1], ACT.Sqrt, bias=eps[:, :]).then_inc(std_done, 1)

            def rows_out(c, u):
                act.wait_ge(T_done, c + 1)
                for k in range(KD):
                    last = nc.scalar.copy(xT[u][:, k, :], psT[k][:, :])
                last.then_inc(xT_ready, 1)

            def high(c, u, m):
                act.wait_ge(qk_done, c * NM + (m + 1))
                nc.scalar.activation(parts[u][m][:, 0, :], psQ[m][:, :], ACT.Identity,
                                     bias=bqk[:, m:m + 1]).then_inc(hi_ready, 1)

            rows_out(0, 0)
            act.wait_ge(*weights_loaded)
            for u in range(2):
                for m in range(NM):
                    high(u, u, m)
                rows_out(u + 1, 1 - u)
            with act.Fori(1, NCH // 2 - 1) as cc:
                for u in range(2):
                    act.wait_ge(parts_stored[u], cc * (16 * NM))
                    for m in range(NM):
                        high(cc * 2 + u, u, m)
                    rows_out(cc * 2 + (u + 1), 1 - u)
            for u in range(2):
                act.wait_ge(parts_stored[u], (NCH // 2 - 1) * 16 * NM)
                for m in range(NM):
                    high(NCH - 2 + u, u, m)
                if u == 0:
                    rows_out(NCH - 1, 1)

        @block.vector
        def _(dve):
            nc.vector.memset(eps[:, :], EPS)
            for u in range(2):
                for j in range(CT):
                    nc.vector.memset(vt[u][j][:, :, HD:VC], 1.0)
            with dve.Fori(0, NT) as t:
                nc.vector.bn_stats(st[:, t, :], X[:, t, :])
            dve.drain()
            for t in range(NT):
                nc.vector.bn_aggr(mv[:, t, :], st[:, t, :])
            dve.drain().then_inc(var_done, 1)
            dve.wait_ge(std_done, 1)
            nc.vector.reciprocal(rstd[:, :], rstd[:, :])
            dve.drain()

            def rows(c):
                for j in range(CT):
                    t = c * CT + j
                    nc.vector.tensor_scalar(xn[j][:, :], X[:, t, :], mv[:, t, 0:1], rstd[:, bass.ds(t, 1)],
                                            ALU.subtract, ALU.mult).then_inc(n_ready, 1)

            def chunk(c, u, stored=None, more=True):
                if more:
                    dve.wait_ge(T_done, c + 1)
                    rows(c + 1)
                if stored is not None:
                    dve.wait_ge(parts_stored[u], stored * 16 * NM)
                    dve.wait_ge(v_stored[u], stored * 16 * CT)
                for m in range(NM):
                    dve.wait_ge(hi_ready, c * NM + (m + 1))
                    nc.vector.scalar_tensor_tensor(rest[u][m][:, :], psQ[m][:, :], bqk[:, m:m + 1],
                                                   parts[u][m][:, 0, :], ALU.add, ALU.subtract).then_inc(rest_ready, 1)
                    dve.wait_ge(rest_ready, c * NM + (m + 1))
                    nc.vector.tensor_copy(parts[u][m][:, 1, :], rest[u][m][:, :]).then_inc(mid_ready, 1)
                for j in range(CT):
                    dve.wait_ge(v_done, c * CT + (j + 1))
                    nc.vector.tensor_tensor(vt[u][j][:, :, 0:HD],
                                            psV[j % 2][:, 0:D].rearrange("p (h d) -> p h d", d=HD),
                                            bv[:, :].rearrange("p (h d) -> p h d", d=HD), ALU.add).then_inc(v_ready, 1)

            rows(0)
            dve.wait_ge(*weights_loaded)
            chunk(0, 0)
            chunk(1, 1)
            with dve.Fori(1, NCH // 2 - 1) as cc:
                for u in range(2):
                    chunk(cc * 2 + u, u, cc)
            chunk(NCH - 2, 0, NCH // 2 - 1)
            chunk(NCH - 1, 1, NCH // 2 - 1, False)

        @block.tensor
        def _(pe):
            def rows_in(c, first=False):
                pe.wait_ge(n_ready, c * CT + CT)
                if not first:
                    pe.wait_ge(xT_ready, c)
                for k in range(KD):
                    for j in range(CT):
                        last = nc.tensor.transpose(psT[k][:, j * P:(j + 1) * P], xn[j][:, k * P:(k + 1) * P], ident[:, :])
                last.then_inc(T_done, 1)

            def chunk(c, u, first=False, more=True):
                pe.wait_ge(xT_ready, c + 1)
                for m in range(NM):
                    if not first:
                        pe.wait_ge(rest_ready, c * NM + (m + 1 - NM))
                    for k in range(KD):
                        last = nc.tensor.matmul(psQ[m][:, :], wqk[:, k, m * P:(m + 1) * P], xT[u][:, k, :],
                                                start=(k == 0), stop=(k == KD - 1))
                    last.then_inc(qk_done, 1)
                if more:
                    rows_in(c + 1)
                for j in range(CT):
                    if not (first and j < 2):
                        pe.wait_ge(v_ready, c * CT + (j - 1))
                    for k in range(KD):
                        last = nc.tensor.matmul(psV[j % 2][:, 0:D], xT[u][:, k, j * P:(j + 1) * P], wv[:, k, :],
                                                start=(k == 0), stop=(k == KD - 1))
                    last.then_inc(v_done, 1)

            rows_in(0, True)
            pe.wait_ge(*weights_loaded)
            chunk(0, 0, True)
            chunk(1, 1)
            with pe.Fori(1, NCH // 2 - 1) as cc:
                for u in range(2):
                    chunk(cc * 2 + u, u)
            chunk(NCH - 2, 0)
            chunk(NCH - 1, 1, False, False)


def scores_phase(nc, tag, ident, identb, qk_d, v_d, o_d):
    ctx = ExitStack()
    sems = []
    ctx.callback(release, nc, sems)
    with ctx:
        sb = lambda n, s, d=F32: ctx.enter_context(nc.sbuf_tensor(f"{tag}_{n}", s, d))
        sem = lambda n: new_semaphore(nc, sems, f"{tag}_{n}")
        qs = [sb(f"qs{g}", [MROWS, GROUP, S], BF16) for g in range(NG)]
        ks = [sb(f"ks{g}", [MROWS, GROUP, S], BF16) for g in range(NG)]
        va = [sb(f"va{g}", [P, QT, GROUP * VC]) for g in range(NG)]
        pt = [[sb(f"pt{v}{h}", [P, 2, HALF]) for h in range(2)] for v in range(2)]
        SUB = 2 * QT * GROUP
        mxh = sb("mxh", [P, QT, GROUP, 2])
        mx = sb("mx", [P, QT * GROUP])
        zeros = sb("zeros", [P, QT * GROUP])
        mxr = sb("mxr", [P, QT * GROUP])
        mx3 = sb("mx3", [P, QT, GROUP, 3], BF16)
        mxT = [sb(f"mxT{v}", [GROUP * 3, S], BF16) for v in range(2)]
        osb = [sb(f"osb{h}", [P, HALF]) for h in range(2)]
        rden = [sb(f"rden{h}", [P, QT // 2, GROUP]) for h in range(2)]
        ot = [sb(f"ot{h}", [P, QT // 2, GROUP, HD]) for h in range(2)]
        psS = [ctx.enter_context(nc.psum_tensor(f"{tag}_psS{h}", [P, HALF], F32)) for h in range(2)]
        psE = [ctx.enter_context(nc.psum_tensor(f"{tag}_psE{h}", [P, 2, HALF], F32)) for h in range(2)]
        psO = ctx.enter_context(nc.psum_tensor(f"{tag}_psO", [P, HALF], F32))
        psX = ctx.enter_context(nc.psum_tensor(f"{tag}_psX", [P, HALF], F32))

        rows_ready = sem("rows_ready"); psO_cleared = sem("psO_cleared")
        loaded = [sem(f"loaded{g}") for g in range(NG)]
        v_loaded = [sem(f"v_loaded{g}") for g in range(NG)]
        sub_done = sem("sub_done"); sub_used = sem("sub_used")
        mx_found = sem("mx_found"); mx_ready = sem("mx_ready"); mxT_done = sem("mxT_done"); mxT_ready = sem("mxT_ready")
        mx_rows = [sem(f"mx_rows{g}") for g in range(NG)]
        e_done = sem("e_done"); p_ready = sem("p_ready"); pv_done = sem("pv_done")
        o_ready = sem("o_ready"); oT_done = sem("oT_done"); ot_ready = sem("ot_ready")
        o_stored = [sem(f"o_stored{h}") for h in range(2)]

        SLOTS = 2 * QT
        SHARE = SUB // SLOTS
        LEAD = 4
        EARLY = 4
        following = lambda b, g: (b, g + 1) if g + 1 < NG else (b + 1, 0)

        def taken_along(b, g, s):
            nb, ng = following(b, g)
            first = (s + LEAD) % SLOTS * SHARE
            if s >= SLOTS - LEAD:
                nb, ng = following(nb, ng)
            return nb, ng, range(first, first + SHARE)

        MAX_T = (SLOTS - LEAD, SLOTS - LEAD + 1)
        in_range = lambda b, g: not (isinstance(b, int) and b >= B)
        before = lambda b, g, n: b * (NG * n) + g * n

        block = ctx.enter_context(nc.Block())

        @block.sync
        def _(sp):
            def load(b, g):
                for dst, w, parts in ((qs, 0, Q_PARTS), (ks, 1, K_PARTS)):
                    for i, part in enumerate(parts):
                        sp.dma_start(dst[g][i * HD:(i + 1) * HD, :, :],
                                     qk_d[w, part, b, g * GROUP * HD:(g + 1) * GROUP * HD, :]
                                     .rearrange("(r d) t -> d r t", d=HD)).then_inc(loaded[g], 16)
                sp.dma_start(va[g][:, :, :], v_d[b, g, :, :, :]).then_inc(v_loaded[g], 16)

            def max_rows(b, g):
                sp.wait_ge(mxT_ready, before(b, g, 2) + 2)
                for r in range(GROUP):
                    sp.dma_start(qs[g][KROWS:MROWS, r, :], mxT[g % 2][r * 3:(r + 1) * 3, :]).then_inc(mx_rows[g], 16)

            def results(b, g, h):
                sp.wait_ge(ot_ready, before(b, g, 2) + (h + 2))
                sp.dma_start(o_d[b, h * QT // 2:(h + 1) * QT // 2, :, g * GROUP * HD:(g + 1) * GROUP * HD]
                             .rearrange("t p c -> p t c"),
                             ot[h][:, :, :, :].rearrange("p t r c -> p t (r c)")).then_inc(o_stored[h], 16)

            def group(b, g, last):
                results(b, g, 0)
                if not (last and g == NG - 1):
                    max_rows(*following(b, g))
                if not last:
                    sp.wait_ge(pv_done, before(b, g, SLOTS) + SLOTS)
                    load(b + 1, g)
                results(b, g, 1)

            for h in range(2):
                sp.sem_inc(o_stored[h], 16)
            for g in range(NG):
                load(0, g)
            max_rows(0, 0)
            with sp.Fori(0, B - 1) as b:
                for g in range(NG):
                    group(b, g, False)
            for g in range(NG):
                group(B - 1, g, True)
            for h in range(2):
                sp.wait_ge(o_stored[h], 16 * (B * NG + 1))

        @block.gpsimd
        def _(pool):
            nc.gpsimd.memset(zeros[:, :], 0.0).then_inc(rows_ready, 1)
            pool.wait_ge(rows_ready, 1)
            for g in range(NG):
                nc.gpsimd.memset(ks[g][KROWS:MROWS, :, :], -1.0).then_inc(rows_ready, 1)
                pool.wait_ge(rows_ready, g + 2)

            def maximum_parts(b, g):
                pool.wait_ge(mx_found, before(b, g, 1) + 1)
                part = lambda i: mx3[:, :, :, i].rearrange("p q r -> p (q r)")
                nc.gpsimd.tensor_tensor(part(0), mx[:, :], zeros[:, :], ALU.add)
                pool.drain()
                nc.gpsimd.tensor_tensor(mxr[:, :], mx[:, :], part(0), ALU.subtract)
                pool.drain()
                nc.gpsimd.tensor_copy(part(1), mxr[:, :])
                pool.drain()
                nc.gpsimd.tensor_tensor(part(2), mxr[:, :], part(1), ALU.subtract).then_inc(mx_ready, 1)

            maximum_parts(0, 0)
            with pool.Fori(0, B - 1) as b:
                for g in range(NG):
                    maximum_parts(*following(b, g))
            for g in range(NG - 1):
                maximum_parts(B - 1, g + 1)

        @block.scalar
        def _(act):
            nc.scalar.preload_act_table(ACT.Exp)

            def exps(b, g, s, h, first=False):
                act.wait_ge(e_done, before(b, g, 2 * SLOTS) + (2 * s + h + 1))
                if not first:
                    act.wait_ge(pv_done, before(b, g, SLOTS) + (s - 1))
                nc.scalar.activation(pt[s % 2][h][:, :, :], psE[h][:, :, :], ACT.Exp,
                                     scale=HD ** -0.5).then_inc(p_ready, 1)

            def sums_out(b, g, h):
                act.wait_ge(pv_done, before(b, g, SLOTS) + (h + 1) * QT)
                nc.scalar.copy(osb[h][:, :], psO[:, :]).then_inc(o_ready, 1)

            def maxima_out(b, g, v):
                act.wait_ge(mxT_done, before(b, g, 2) + (v + 1))
                nc.scalar.copy(mxT[g % 2][:, v * HALF:(v + 1) * HALF], psX[0:GROUP * 3, :]).then_inc(mxT_ready, 1)

            def slots(b, g, which, first=False, last=False):
                for s in which:
                    if s == 1 and not first:
                        sums_out(*(b, g - 1) if g else (b - 1, NG - 1), 1)
                    if s == QT + 1:
                        sums_out(b, g, 0)
                    exps(b, g, s, 0, first and s < 2)
                    exps(b, g, s, 1, first and s < 2)
                    if s in MAX_T and not last:
                        maxima_out(*following(b, g), MAX_T.index(s))

            for v in range(2):
                maxima_out(0, 0, v)
            slots(0, 0, range(EARLY), first=True)
            with act.Fori(0, B - 1) as b:
                for g in range(NG):
                    slots(b, g, range(EARLY, SLOTS))
                    slots(*following(b, g), range(EARLY))
            for g in range(NG):
                slots(B - 1, g, range(EARLY, SLOTS), last=g == NG - 1)
                if g + 1 < NG:
                    slots(B - 1, g + 1, range(EARLY))
            sums_out(B - 1, NG - 1, 1)

        @block.vector
        def _(dve):
            nc.vector.memset(psO[:, :], 0.0).then_inc(psO_cleared, 1)
            dve.sem_inc(ot_ready, 1)

            def maxima(b, g, which):
                for v in which:
                    dve.wait_ge(sub_done, before(b, g, SUB) + (v + 1))
                    nc.vector.tensor_reduce(mxh[:, v // 8, v // 2 % GROUP, v % 2:v % 2 + 1], psS[v % 2][:, :], AX.X,
                                            ALU.max).then_inc(sub_used, 1)

            def group_maxima(b, g, first=False):
                dve.drain()
                if not first:
                    dve.wait_ge(mx_ready, before(b, g, 1))
                halves = mxh[:, :, :, :].rearrange("p q r h -> p (q r) h")
                nc.vector.tensor_tensor(mx[:, :], halves[:, :, 0], halves[:, :, 1], ALU.max).then_inc(mx_found, 1)

            def divide(b, g, h):
                dve.wait_ge(oT_done, before(b, g, 2) + (h + 1))
                view = psX[:, :].rearrange("p (t r c) -> p t r c", r=GROUP, c=32)
                nc.vector.reciprocal(rden[h][:, :, :], view[:, :, :, HD])
                dve.drain()
                dve.wait_ge(o_stored[h], before(b, g, 16) + 16)
                nc.vector.tensor_tensor(ot[h][:, :, :, :].rearrange("p t r c -> p (t r) c"),
                                        psX[:, :].rearrange("p (t c) -> p t c", c=32)[:, :, 0:HD],
                                        rden[h][:, :, :].rearrange("p t r -> p (t r)")[:, :, None]
                                        .to_broadcast([P, QT // 2 * GROUP, HD]), ALU.mult).then_inc(ot_ready, 1)

            def slots(b, g, which, first=False, last=False):
                for s in which:
                    nb, ng, which_max = taken_along(b, g, s)
                    if in_range(nb, ng):
                        maxima(nb, ng, which_max)
                        if s == SLOTS - LEAD - 1:
                            group_maxima(nb, ng)
                    if s == 3 and not first:
                        divide(*(b, g - 1) if g else (b - 1, NG - 1), 1)
                    if s == QT + 3:
                        divide(b, g, 0)

            maxima(0, 0, range(SUB))
            group_maxima(0, 0, True)
            maxima(0, 1, range(LEAD * SHARE))
            slots(0, 0, range(EARLY), first=True)
            with dve.Fori(0, B - 1) as b:
                for g in range(NG):
                    slots(b, g, range(EARLY, SLOTS))
                    slots(*following(b, g), range(EARLY))
            for g in range(NG):
                slots(B - 1, g, range(EARLY, SLOTS), last=g == NG - 1)
                if g + 1 < NG:
                    slots(B - 1, g + 1, range(EARLY), last=g + 1 == NG - 1)
            divide(B - 1, NG - 1, 1)

        @block.tensor
        def _(pe):
            def maxima(b, g, which, first=False):
                for v in which:
                    if not (first and v < 2):
                        pe.wait_ge(sub_used, before(b, g, SUB) + (v - 1))
                    nc.tensor.matmul(psS[v % 2][:, :], qs[g][0:KROWS, v // 2 % GROUP, v // 8 * P:(v // 8 + 1) * P],
                                     ks[g][0:KROWS, v // 2 % GROUP, v % 2 * HALF:(v % 2 + 1) * HALF],
                                     start=True, stop=True).then_inc(sub_done, 1)

            def scores(b, g, s, r, first=False):
                half, kt = divmod(s, QT)
                if r % 2 == 0 and not first:
                    pe.wait_ge(p_ready, before(b, g, 2 * SLOTS) + (2 * s + r // 2 - 1))
                product = nc.tensor.matmul(psE[r // 2][:, r % 2, :], ks[g][0:MROWS, r, kt * P:(kt + 1) * P],
                                           qs[g][0:MROWS, r, half * HALF:(half + 1) * HALF], start=True, stop=True)
                if r % 2 == 1:
                    product.then_inc(e_done, 1)

            def sums(b, g, s, c, first=False):
                half, kt = divmod(s, QT)
                if c == 0:
                    pe.wait_ge(p_ready, before(b, g, 2 * SLOTS) + (2 * s + 2))
                    if s == 0:
                        pe.wait_ge(v_loaded[g], b * 16 + 16)
                    if kt == 0 and not first:
                        pe.wait_ge(o_ready, before(b, g, 2) + half)
                cols = slice(c * HALF // 2, (c + 1) * HALF // 2)
                for r in range(GROUP):
                    last = nc.tensor.matmul(psO[32 * r:32 * r + VC, cols], va[g][:, kt, r * VC:(r + 1) * VC],
                                            pt[s % 2][r // 2][:, r % 2, cols], start=(kt == 0 and c == 0),
                                            stop=(kt == QT - 1 and c == 1), tile_position=(0, 32 * r),
                                            skip_group_check=True)
                if c == 1:
                    last.then_inc(pv_done, 1)

            def maxima_T(b, g, v, psX_free):
                pe.wait_ge(mx_ready, before(b, g, 1) + 1)
                if psX_free is not None:
                    pe.wait_ge(*psX_free)
                for q in range(QT // 2):
                    last = nc.tensor.matmul(psX[0:GROUP * 3, q * P:(q + 1) * P],
                                            mx3[:, v * (QT // 2) + q, :, :].rearrange("p r c -> p (r c)"),
                                            identb[:, :], start=True, stop=True)
                last.then_inc(mxT_done, 1)

            def sums_T(b, g, h, psX_free):
                pe.wait_ge(o_ready, before(b, g, 2) + (h + 1))
                pe.wait_ge(*psX_free)
                for q in range(QT // 2):
                    last = nc.tensor.transpose(psX[:, q * P:(q + 1) * P], osb[h][:, q * P:(q + 1) * P], ident[:, :])
                last.then_inc(oT_done, 1)

            def slots(b, g, which, first=False, last=False):
                nb, ng = following(b, g)
                pb, pg = (b, g - 1) if g else (b - 1, NG - 1)
                for s in which:
                    mb, mg, which_max = taken_along(b, g, s)
                    some = which_max if in_range(mb, mg) else ()
                    if s == 0:
                        pe.wait_ge(mx_rows[g], b * (16 * GROUP) + 16 * GROUP)
                    if s == SLOTS - LEAD and some:
                        pe.wait_ge(loaded[mg], mb * (16 * 12) + 16 * 12)
                    scores(b, g, s, 0, first and s == 0)
                    maxima(mb, mg, some[0:1])
                    if s >= 2:
                        sums(b, g, s - 2, 1)
                    elif not first:
                        sums(pb, pg, SLOTS - 2 + s, 1)
                    maxima(mb, mg, some[1:2])
                    for r in (1, 2):
                        scores(b, g, s, r, first and s == 0)
                    maxima(mb, mg, some[2:3])
                    if s >= 1:
                        sums(b, g, s - 1, 0, first and s == 1)
                    elif not first:
                        sums(pb, pg, SLOTS - 1, 0)
                    maxima(mb, mg, some[3:4])
                    scores(b, g, s, 3)
                    if s == 2 and not first:
                        sums_T(pb, pg, 1, (mxT_ready, before(b, g, 2) + 2))
                    if s == QT + 2:
                        sums_T(b, g, 0, (ot_ready, before(b, g, 2) + 1))
                    if s in MAX_T and not last:
                        v = MAX_T.index(s)
                        maxima_T(nb, ng, v, (mxT_ready, before(nb, ng, 2) + 1) if v else
                                 (ot_ready, before(b, g, 2) + 2))

            pe.wait_ge(loaded[0], 16 * 12)
            maxima(0, 0, range(SUB), first=True)
            maxima_T(0, 0, 0, None)
            maxima_T(0, 0, 1, (mxT_ready, 1))
            pe.wait_ge(loaded[1], 16 * 12)
            maxima(0, 1, range(LEAD * SHARE))
            pe.wait_ge(rows_ready, NG + 1)
            pe.wait_ge(psO_cleared, 1)
            slots(0, 0, range(EARLY), first=True)
            with pe.Fori(0, B - 1) as b:
                for g in range(NG):
                    slots(b, g, range(EARLY, SLOTS))
                    slots(*following(b, g), range(EARLY))
            for g in range(NG):
                slots(B - 1, g, range(EARLY, SLOTS), last=g == NG - 1)
                if g + 1 < NG:
                    slots(B - 1, g + 1, range(EARLY), last=g + 1 == NG - 1)
            sums(B - 1, NG - 1, SLOTS - 2, 1)
            for c in range(2):
                sums(B - 1, NG - 1, SLOTS - 1, c)
            sums_T(B - 1, NG - 1, 1, (ot_ready, before(B - 1, NG - 1, 2) + 2))


def out_projection_phase(nc, tag, X, ident, wo, weights_loaded, o_d):
    ctx = ExitStack()
    sems = []
    ctx.callback(release, nc, sems)
    with ctx:
        sb = lambda n, s, d=F32: ctx.enter_context(nc.sbuf_tensor(f"{tag}_{n}", s, d))
        sem = lambda n: new_semaphore(nc, sems, f"{tag}_{n}")
        o = [sb(f"o{u}", [P, D]) for u in range(4)]
        oT = [sb(f"oT{u}", [P, KD, P]) for u in range(2)]
        psT = [ctx.enter_context(nc.psum_tensor(f"{tag}_psT{u}", [P, 512], F32)) for u in range(2)]
        psY = [ctx.enter_context(nc.psum_tensor(f"{tag}_psY{u}", [P, 512], F32)) for u in range(2)]
        o_loaded = [sem(f"o_loaded{u}") for u in range(4)]
        T_done = sem("T_done"); oT_ready = sem("oT_ready"); y_done = sem("y_done"); y_used = sem("y_used")
        block = ctx.enter_context(nc.Block())

        @block.sync
        def _(sp):
            rows = o_d.rearrange("b t p c -> (b t) p c")
            for u in range(4):
                sp.dma_start(o[u][:, :], rows[u]).then_inc(o_loaded[u], 16)
            with sp.Fori(1, NT // 4) as tt:
                for u in range(4):
                    sp.wait_ge(T_done, tt * 4 + (u - 3))
                    sp.dma_start(o[u][:, :], rows[tt * 4 + u]).then_inc(o_loaded[u], 16)

        @block.scalar
        def _(act):
            with act.Fori(0, NT // 2) as tt:
                for u in range(2):
                    act.wait_ge(T_done, tt * 2 + (u + 1))
                    nc.scalar.copy(oT[u][:, :, :].rearrange("p k t -> p (k t)"), psT[u][:, 0:D]).then_inc(oT_ready, 1)

        @block.vector
        def _(dve):
            with dve.Fori(0, NT // 2) as tt:
                for u in range(2):
                    t = tt * 2 + u
                    dve.wait_ge(y_done, t + 1)
                    nc.vector.tensor_tensor(X[:, t, :], X[:, t, :], psY[u][:, 0:D], ALU.add).then_inc(y_used, 1)

        @block.tensor
        def _(pe):
            def transposes(t, u, first=False):
                pe.wait_ge(o_loaded[u], (t - u) * 4 + 16)
                if not first:
                    pe.wait_ge(oT_ready, t - 1)
                for k in range(KD):
                    last = nc.tensor.transpose(psT[u % 2][:, k * P:(k + 1) * P], o[u][:, k * P:(k + 1) * P], ident[:, :])
                last.then_inc(T_done, 1)

            def product(t, u, first=False):
                pe.wait_ge(oT_ready, t + 1)
                if not first:
                    pe.wait_ge(y_used, t - 1)
                for k in range(KD):
                    last = nc.tensor.matmul(psY[u % 2][:, 0:D], oT[u % 2][:, k, :], wo[:, k, :],
                                            start=(k == 0), stop=(k == KD - 1))
                last.then_inc(y_done, 1)

            transposes(0, 0, True)
            pe.wait_ge(*weights_loaded)
            for t in range(3):
                transposes(t + 1, t + 1, t == 0)
                product(t, t, t < 2)
            with pe.Fori(0, NT // 4 - 1) as tt:
                for u in range(4):
                    t = tt * 4 + (3 + u)
                    transposes(t + 1, u)
                    product(t, (3 + u) % 4)
            product(NT - 1, 3)


def memory_moe_attention_moe_kernel(nc, x, m0T, w1T, w2T, rates_w, rates_b, gate_w, gate_b,
                                    gate_up, down_a, down_b, router, wqk, wv, wo, bqk, bv, bo, out):
    ctx = ExitStack()
    with ctx:
        def alloc(where, name, shape, dtype=F32):
            return where.enter_context(nc.sbuf_tensor(name, shape, dtype))

        X = alloc(ctx, "X", [P, NT, D])
        ident = alloc(ctx, "ident", [P, P]); identb = alloc(ctx, "identb", [P, P], BF16)
        ones = alloc(ctx, "ones", [P, P]); zero = alloc(ctx, "zero", [P, D])
        W = {"gate_up": alloc(ctx, "W_gate_up", [P, KD, E + 1, 2 * I]), "router": alloc(ctx, "W_router", [P, KD, E + 1])}
        Wqk = alloc(ctx, "Wqk", [P, KD, 2 * D]); Wv = alloc(ctx, "Wv", [P, KD, D])
        Bqk = alloc(ctx, "Bqk", [P, 2 * KD]); Bv = alloc(ctx, "Bv", [P, D]); Bo = alloc(ctx, "Bo", [P, D])
        xs = nc.dram_tensor("sorted_rows", [NB * P, D], F32).ap()
        ys = nc.dram_tensor("expert_rows", [NB * P, D], F32).ap()
        qk_d = nc.dram_tensor("query_key_parts", [2, 3, B, D, S], BF16).ap()
        v_d = nc.dram_tensor("values", [B, NG, P, QT, GROUP * VC], F32).ap()
        o_d = nc.dram_tensor("head_results", [B, QT, P, D], F32).ap()

        sem = lambda n: ctx.enter_context(nc.semaphore(n))
        memory_loaded = sem("memory_loaded"); moe_loaded = sem("moe_loaded"); down_loaded = sem("down_loaded")
        attention_loaded = sem("attention_loaded"); zero_ready = sem("zero_ready"); xs_filled = sem("xs_filled")
        ident_ready = sem("ident_ready"); stored = sem("stored"); wo_loaded = sem("wo_loaded")

        def load_down(sp, down, loaded):
            sp.dma_start(down[:, 0:I // P, :, :], down_a).then_inc(loaded, 16)
            sp.dma_start(down[0:I % P, I // P, :, :], down_b).then_inc(loaded, 16)

        first_half = ExitStack()
        with first_half:
            M0 = alloc(first_half, "M0", [P, KD, D])
            W1 = alloc(first_half, "W1", [P, KD, D]); W2 = alloc(first_half, "W2", [P, KD, D])
            Rw = alloc(first_half, "Rw", [P, KD, 2]); Rb = alloc(first_half, "Rb", [2, 1])
            Gw = alloc(first_half, "Gw", [P, KD]); Gb = alloc(first_half, "Gb", [P, 1])
            W["down"] = alloc(first_half, "W_down1", [P, KI, E + 1, D])

            with nc.Block() as block:
                @block.sync
                def _(sp):
                    sp.dma_start(X[:, :, :], x).then_inc(memory_loaded, 16)
                    for dst, src in ((M0, m0T), (W1, w1T), (W2, w2T), (Rw, rates_w)):
                        sp.dma_start(dst[:, :, :], src).then_inc(memory_loaded, 16)
                    sp.dma_start(Rb[:, :], rates_b).then_inc(memory_loaded, 16)
                    sp.dma_start(Gw[:, :], gate_w).then_inc(memory_loaded, 16)
                    sp.dma_start(Gb[:, :], gate_b.to_broadcast([P, 1])).then_inc(memory_loaded, 16)
                    sp.dma_start(W["router"][:, :, :], router).then_inc(moe_loaded, 16)
                    sp.dma_start(W["gate_up"][:, :, :, :], gate_up).then_inc(moe_loaded, 16)
                    sp.wait_ge(zero_ready, 1)
                    load_down(sp, W["down"], moe_loaded)
                    sp.dma_start(xs.rearrange("(j p) d -> p j d", p=P),
                                 zero[:, None, :].to_broadcast([P, NB, D])).then_inc(xs_filled, 16)
                    for dst, src in ((Wqk, wqk), (Wv, wv)):
                        sp.dma_start(dst[:, :, :], src).then_inc(attention_loaded, 16)
                    sp.dma_start(Bqk[:, :], bqk).then_inc(attention_loaded, 16)
                    sp.dma_start(Bv[:, :], bv.to_broadcast([P, D])).then_inc(attention_loaded, 16)
                    sp.dma_start(Bo[:, :], bo.to_broadcast([P, D])).then_inc(attention_loaded, 16)
                    sp.wait_ge(memory_loaded, 16 * 8)

                @block.vector
                def _(dve):
                    nc.vector.memset(zero[:, :], 0.0)
                    nc.vector.memset(W["down"][I % P:P, I // P, :, :], 0.0)
                    nc.vector.memset(ones[:, :], 1.0)
                    dve.drain().then_inc(zero_ready, 1)

                @block.gpsimd
                def _(pool):
                    nc.gpsimd.memset(ident[:, :], 0.0).then_inc(ident_ready, 1)
                    pool.wait_ge(ident_ready, 1)
                    nc.gpsimd.affine_select(out=ident[:, :], in_=ident[:, :], compare_op=ALU.not_equal, fill=1.0,
                                            base=0, pattern=[[-1, P]], channel_multiplier=1).then_inc(ident_ready, 1)
                    pool.wait_ge(ident_ready, 2)
                    nc.gpsimd.tensor_copy(identb[:, :], ident[:, :])

            memory_phase(nc, "mem", X, ident, ones, M0, W1, W2, (memory_loaded, 16 * 8), Rw, Rb, Gw, Gb)
            ffn_phase(nc, "moe1", X, ident, ones, W, (moe_loaded, 16 * 4), xs, ys, (xs_filled, 16))

        qkv_phase(nc, "qkv", X, ident, Wqk, Wv, Bqk, Bv, Bo, (attention_loaded, 16 * 5), qk_d, v_d)
        scores_phase(nc, "scores", ident, identb, qk_d, v_d, o_d)

        second_half = ExitStack()
        with second_half:
            W["down"] = alloc(second_half, "W_down2", [P, KI, E + 1, D]); Wo = alloc(second_half, "Wo", [P, KD, D])
            with nc.Block() as block:
                @block.vector
                def _(dve):
                    nc.vector.memset(W["down"][I % P:P, I // P, :, :], 0.0)
                    dve.drain().then_inc(zero_ready, 1)

                @block.sync
                def _(sp):
                    sp.dma_start(Wo[:, :, :], wo).then_inc(wo_loaded, 16)
                    sp.wait_ge(zero_ready, 2)
                    load_down(sp, W["down"], down_loaded)
            out_projection_phase(nc, "out", X, ident, Wo, (wo_loaded, 16), o_d)
            ffn_phase(nc, "moe2", X, ident, ones, W, (down_loaded, 16 * 2), xs, ys, (xs_filled, 16), (out, stored))


def kernel(**inputs):
    import numpy as np
    import concourse.bacc as bacc
    from concourse.bass_utils import run_bass_kernel_spmd

    a = {name: np.asarray(v) for name, v in inputs.items()}
    mem = lambda n: a["L0_attn_a_" + n]
    att = lambda n: a["L0_attn_b_" + n]
    moe = lambda n: a["L0_ffn_" + n]
    tiles = lambda w: w.reshape(-1, P, w.shape[-1]).transpose(1, 0, 2)
    wqkv = att("Wqkv").reshape(HEADS, 3, HD, D)
    bqkv = att("bqkv").reshape(HEADS, 3, HD)
    experts = lambda n: np.concatenate([moe("w_" + n), moe("sw_" + n)[None]])
    gate_up = np.concatenate([experts("gate"), experts("up")], axis=2)
    down = experts("down")
    arrays = {
        "x": mem("x").reshape(NT, P, D).transpose(1, 0, 2),
        "m0T": tiles(mem("M_init").T), "w1T": tiles(mem("vg_w1").T), "w2T": tiles(mem("vg_w2").T),
        "rates_w": tiles(np.stack([mem("eta_w"), mem("alpha_w")], 1)),
        "rates_b": np.concatenate([mem("eta_b"), mem("alpha_b")]).reshape(2, 1),
        "gate_w": mem("gate_w").reshape(KD, P).T, "gate_b": mem("gate_b").reshape(1, 1),
        "gate_up": gate_up.reshape(E + 1, KD, P, 2 * I).transpose(2, 1, 0, 3),
        "down_a": down[:, :I // P * P].reshape(E + 1, I // P, P, D).transpose(2, 1, 0, 3),
        "down_b": down[:, I // P * P:].transpose(1, 0, 2),
        "router": tiles(np.concatenate([moe("gate_w"), moe("shared_gate_w")]).T),
        "wqk": tiles(wqkv[:, 0:2].transpose(3, 1, 0, 2).reshape(D, 2 * D)),
        "wv": tiles(wqkv[:, 2].transpose(2, 0, 1).reshape(D, D)), "wo": tiles(att("Wo").T),
        "bqk": bqkv[:, 0:2].transpose(1, 0, 2).reshape(2 * KD, P).T,
        "bv": bqkv[:, 2].reshape(1, D), "bo": att("bo").reshape(1, D),
    }
    nc = bacc.Bacc("TRN2", target_bir_lowering=False, num_devices=1)
    feeds, args = {}, []
    for name, v in arrays.items():
        v = np.ascontiguousarray(v)
        feeds[f"in_{name}_dram"] = v
        args.append(nc.dram_tensor(f"in_{name}_dram", v.shape, mybir.dt.from_np(v.dtype), kind="ExternalInput").ap())
    args.append(nc.dram_tensor("out_0_dram", (P, NT, D), F32, kind="ExternalOutput").ap())
    memory_moe_attention_moe_kernel(nc, *args)
    r = run_bass_kernel_spmd(nc, [feeds], core_ids=[0])
    return r.results[0]["out_0_dram"].transpose(1, 0, 2).reshape(B, S, D)
```

```python
import concourse.bass as bass
from concourse import mybir
from contextlib import ExitStack

F32 = mybir.dt.float32
I32 = mybir.dt.int32
U32 = mybir.dt.uint32
BF16 = mybir.dt.bfloat16
ALU = mybir.AluOpType
ACT = mybir.ActivationFunctionType
AX = mybir.AxisListType

P = 128
B, S, D = 4, 1024, 256
TOKENS = B * S
NT = TOKENS // P
KD = D // P
E, TOPK, I = 8, 2, 352
SHARED = E
IP = -(-I // P) * P
KI = IP // P
NB = (TOKENS * TOPK) // P + E
SLOTS_ALL = NB * P
ROWS_ALL = TOPK * TOKENS
SRC = 6
AHEAD = 4
NA = 16
PIECE = 8
NS = NT + NB
EPS = 1e-5


def new_semaphore(nc, sems, name):
    sems.append(nc.alloc_semaphore(name))
    return sems[-1]


def release(nc, sems):
    nc.clear_and_free_semaphores(sems)
    nc.all_engine_barrier()


def ffn_phase(nc, tag, X, stats, ident, ones, W, weights_loaded, xn_d, ys, store=None):
    ctx = ExitStack()
    sems = []
    ctx.callback(release, nc, sems)
    with ctx:
        sb = lambda n, s, d=F32: ctx.enter_context(nc.sbuf_tensor(f"{tag}_{n}", s, d))
        sem = lambda n: new_semaphore(nc, sems, f"{tag}_{n}")
        src = [sb(f"src{u}", [P, D]) for u in range(SRC)]
        srcT = [sb(f"srcT{u}", [P, KD, P]) for u in range(2)]
        silu = [sb(f"silu{u}", [P, I]) for u in range(2)]
        hid = [sb(f"hid{u}", [P, IP]) for u in range(2)]
        hidT = [sb(f"hidT{u}", [P, KI, P]) for u in range(2)]
        yb = [sb(f"yb{u}", [P, D]) for u in range(2)]
        GS = 4
        got = sb("got", [P, GS, TOPK, D])
        mv = sb("mv", [P, NT, 2])
        rstd = sb("rstd", [P, NT])
        eps = sb("eps", [P, 1])
        lg = sb("lg", [P, NT, E + 1])
        iota8 = sb("iota8", [P, E])
        upper = sb("upper", [P, P])
        iotab = sb("iotab", [1, NB])
        one256 = sb("one256", [P, NT * E])
        eq = sb("eq", [P, NT, E])
        pk = [sb(f"pk{k}", [P, NT, E]) for k in range(TOPK)]
        mx = [sb(f"mx{k}", [P, NT]) for k in range(TOPK)]
        ix = sb("ix", [P, NT])
        lg2 = sb("lg2", [P, NT, E])
        gap = sb("gap", [P, NT])
        cw = [sb(f"cw{k}", [P, NT]) for k in range(TOPK)]
        sg = sb("sg", [P, NT])
        both = sb("both", [P, NT, E])
        tot = sb("tot", [P, E, NT])
        cum = sb("cum", [P, E, NT])
        exc = sb("exc", [P, E, NT])
        slot = sb("slot", [P, E, NT])
        cnt = sb("cnt", [P, E])
        cnti = sb("cnti", [P, E], I32)
        nblk = sb("nblk", [P, E])
        bend = sb("bend", [P, E])
        base = sb("base", [P, E])
        CH = TOPK * NT
        pos = sb("pos", [P, CH], I32); part_i = sb("part_i", [P, CH], I32)
        pos_p = sb("pos_p", [P, CH], BF16); pos_j = sb("pos_j", [P, CH], BF16)
        posf = sb("posf", [P, CH])
        iota_p = sb("iota_p", [P, P], BF16); iota_j = sb("iota_j", [P, NB], BF16)
        tile1 = sb("tile1", [P, CH], BF16)
        lane = sb("lane", [P, 1])
        dump = sb("dump", [P, NB])
        hot_p = [sb(f"hot_p{u}", [P, PIECE, P], BF16) for u in range(2)]
        hot_j = sb("hot_j", [P, PIECE, NB], BF16)
        hot_id = [sb(f"hot_id{u}", [P, PIECE, 2, NB], BF16) for u in range(2)]
        place = sb("place", [P, NB]); empty = sb("empty", [P, NB])
        slots_i = sb("slots_i", [P, NB, 2], I32)
        now_i = [sb(f"now_i{u}", [P, 2], I32) for u in range(SRC)]
        ble = sb("ble", [1, NB, E])
        bex = sb("bex", [1, NB])
        bexi = sb("bexi", [1, NB], I32)

        ps = [ctx.enter_context(nc.psum_tensor(f"{tag}_ps{i}", [P, 512], F32)) for i in range(8)]
        psT, psH, psG, psU, psD = ps[0], ps[1], ps[2:4], ps[4:6], ps[6]
        psL = ps[2]
        psR = (ps[7][:, 0:NT * E], ps[7][:, NT * E:2 * NT * E])
        psI = ps[7][:, 0:2 * NB]

        consts_done = sem("consts_done"); ones_set = sem("ones_set")
        var_done = sem("var_done"); std_done = sem("std_done"); rstd_ready = sem("rstd_ready")
        l_src = sem("l_src"); l_T = sem("l_T"); l_srcT = sem("l_srcT"); l_lg = sem("l_lg"); lg_ready = sem("lg_ready")
        sg_done = sem("sg_done"); chosen = sem("chosen"); rank_done = sem("rank_done"); cw_done = sem("cw_done")
        bex_done = sem("bex_done"); slots_ready = sem("slots_ready"); inv_ready = sem("inv_ready"); inv_done = sem("inv_done")
        xn_stored = [sem(f"xn_stored{u}") for u in range(AHEAD)]
        due = sem("due")
        src_ready = sem("src_ready")
        src_loaded = [sem(f"src_loaded{u}") for u in range(SRC)]
        T_done = sem("T_done"); srcT_ready = sem("srcT_ready")
        g_done = sem("g_done"); u_done = sem("u_done"); silu_done = sem("silu_done")
        hid_ready = sem("hid_ready"); hT_done = sem("hT_done"); hidT_ready = sem("hidT_ready")
        d_done = sem("d_done"); d_used = sem("d_used")
        y_ready = sem("y_ready")
        y_sent = [sem(f"y_sent{u}") for u in range(SRC)]
        got_loaded = [sem(f"got_loaded{s}") for s in range(GS)]
        got_used = sem("got_used")

        LAST = NA + NB
        kind = lambda n: "shared" if n < NA else "routed" if n < LAST else "late"
        UNROLL = {"shared": 2, "routed": SRC, "late": 2}
        runs = []
        n = 0
        while n < NS:
            k, width = kind(n), UNROLL[kind(n)]
            like = n
            while NA <= n and like + 2 < NS and kind(n - 3) == kind(like + 2) == k:
                like += 1
            times = (like - n) // width
            runs.append((n, times, k))
            n += max(times * width, 1)
        tile = lambda n, k: n if k == "shared" else n - NB
        buffer = lambda n0, u, k: (n0 - NA + u) % SRC if k == "routed" else (n0 + u) % 2

        FOUND = 4 + CH // PIECE + 1
        EARLY = min(NT, 2 * (NT - NA - 2)) // GS * GS

        block = ctx.enter_context(nc.Block())

        @block.sync
        def _(sp):
            results = ys[0:ROWS_ALL, :].rearrange("(k t p) d -> t p k d", k=TOPK, p=P)
            with sp.Fori(0, NT // AHEAD) as tt:
                for u in range(AHEAD):
                    sp.wait_ge(l_src, tt * AHEAD + (u + 1))
                    sp.dma_start(xn_d.rearrange("(t p) d -> t p d", p=P)[tt * AHEAD + u], src[u][:, :]
                                 ).then_inc(xn_stored[u], 16)
            for u in range(SRC):
                sp.wait_ge(y_sent[u], 16 * (NB // SRC))
            for t in range(GS):
                sp.dma_start(got[:, t, :, :], results[t]).then_inc(got_loaded[t], 16)
            with sp.Fori(1, NT // GS) as tt:
                for s in range(GS):
                    sp.wait_ge(got_used, tt * GS + (s - GS + 1))
                    sp.dma_start(got[:, s, :, :], results[tt * GS + s]).then_inc(got_loaded[s], 16)
            if store is not None:
                sp.wait_ge(store[1], 16 * NT // GS)

        @block.gpsimd
        def _(pool):
            nc.gpsimd.iota(iota8[:, :], [[1, E]], base=-E, channel_multiplier=0,
                           allow_small_or_imprecise_dtypes=True)
            nc.gpsimd.iota(iotab[:, :], [[1, NB]], base=0, channel_multiplier=0,
                           allow_small_or_imprecise_dtypes=True)
            nc.gpsimd.memset(one256[:, :], 1.0)
            nc.gpsimd.memset(upper[:, :], 1.0).then_inc(ones_set, 1)
            pool.wait_ge(ones_set, 1)
            nc.gpsimd.affine_select(out=upper[:, :], in_=upper[:, :], compare_op=ALU.is_gt, fill=0.0,
                                    base=0, pattern=[[1, P]], channel_multiplier=-1).then_inc(consts_done, 1)
            nc.gpsimd.iota(iota_p[:, :], [[1, P]], base=0, channel_multiplier=0, allow_small_or_imprecise_dtypes=True)
            nc.gpsimd.iota(iota_j[:, :], [[1, NB]], base=0, channel_multiplier=0, allow_small_or_imprecise_dtypes=True)
            nc.gpsimd.iota(tile1[:, :], [[1, CH]], base=1, channel_multiplier=0, allow_small_or_imprecise_dtypes=True)
            nc.gpsimd.iota(lane[:, :], [[1, 1]], base=0, channel_multiplier=1, allow_small_or_imprecise_dtypes=True)
            nc.gpsimd.iota(dump[:, :], [[P, NB]], base=ROWS_ALL + P, channel_multiplier=1,
                           allow_small_or_imprecise_dtypes=True).then_inc(consts_done, 1)

            def fetch(j, u, free=None):
                if free is not None:
                    pool.wait_ge(y_sent[u], free)
                    pool.sem_inc(due, 1)
                nc.gpsimd.tensor_copy(now_i[u][:, :], slots_i[:, j, :])
                pool.drain()
                nc.gpsimd.indirect_dma_start(
                    out=src[u][:, :], out_offset=None, in_=xn_d,
                    in_offset=bass.IndirectOffsetOnAxis(ap=now_i[u][:, 0:1].bitcast(U32), axis=0)
                ).then_inc(src_loaded[u], 16)

            def send(j, u):
                pool.wait_ge(y_ready, j + 1)
                pool.sem_inc(due, 1)
                nc.gpsimd.indirect_dma_start(
                    out=ys, out_offset=bass.IndirectOffsetOnAxis(ap=now_i[u][:, 1:2].bitcast(U32), axis=0),
                    in_=yb[u % 2][:, :], in_offset=None).then_inc(y_sent[u], 16)

            pool.wait_ge(slots_ready, 1)
            for u in range(AHEAD):
                pool.wait_ge(xn_stored[u], 16 * (NT // AHEAD))
            for j in range(AHEAD):
                if j < 2:
                    pool.wait_ge(T_done, NA - 1 + j)
                fetch(j, j)
            for j in range(SRC):
                fetch(j + AHEAD, (j + AHEAD) % SRC, 16 if j + AHEAD >= SRC else None)
                send(j, j)
            with pool.Fori(1, NB // SRC - 1) as jj:
                for u in range(SRC):
                    fetch(jj * SRC + (u + AHEAD), (u + AHEAD) % SRC, jj * 16 + (16 if u + AHEAD >= SRC else 0))
                    send(jj * SRC + u, u)
            for j in range(NB - SRC, NB):
                if j + AHEAD < NB:
                    fetch(j + AHEAD, (j + AHEAD) % SRC, (j + AHEAD) // SRC * 16)
                send(j, j % SRC)
            if store is not None:
                out_pt, stored = store
                for t in range(0, NT, GS):
                    pool.wait_ge(got_used, t + GS)
                    pool.dma_start(out_pt[:, t:t + GS, :], X[:, t:t + GS, :]).then_inc(stored, 16)

        @block.scalar
        def _(act):
            nc.scalar.preload_act_table(ACT.Sqrt)
            act.wait_ge(var_done, 1)
            nc.scalar.activation(rstd[:, :], mv[:, :, 1], ACT.Sqrt, bias=eps[:, :]).then_inc(std_done, 1)
            nc.scalar.preload_act_table(ACT.Sigmoid)
            with act.Fori(0, NT // 2) as tt:
                for u in range(2):
                    act.wait_ge(l_T, tt * 2 + (u + 1))
                    nc.scalar.copy(srcT[u][:, :, :].rearrange("p k t -> p (k t)"), ps[u][:, 0:D]).then_inc(l_srcT, 1)
            act.wait_ge(lg_ready, 1)
            nc.scalar.activation(sg[:, :], lg[:, :, E], ACT.Sigmoid).then_inc(sg_done, 1)
            nc.scalar.preload_act_table(ACT.Silu)

            def source_out(n, u):
                act.wait_ge(T_done, n + 1)
                nc.scalar.copy(srcT[u][:, :, :].rearrange("p k t -> p (k t)"), psT[:, 0:D]).then_inc(srcT_ready, 1)

            def silu_step(n, u):
                act.wait_ge(g_done, n + 1)
                nc.scalar.activation(silu[u][:, :], psG[u][:, 0:I], ACT.Silu).then_inc(silu_done, 1)

            def y_out(n, s, sent=None):
                act.wait_ge(d_done, n + 1)
                if sent is not None:
                    act.wait_ge(y_sent[(s - 2) % SRC], sent)
                nc.scalar.copy(yb[s % 2][:, :], psD[:, 0:D]).then_inc(y_ready, 1)

            def choice_weights():
                act.wait_ge(chosen, 2)
                nc.scalar.activation(cw[0][:, :], gap[:, :], ACT.Sigmoid)
                nc.scalar.activation(cw[1][:, :], gap[:, :], ACT.Sigmoid, scale=-1.0).then_inc(cw_done, 1)
                nc.scalar.preload_act_table(ACT.Silu)

            def step(n, n0, u, k, i=0):
                silu_step(n, (n0 + u) % 2)
                if n0 + u + 1 < NS:
                    source_out(n + 1, (n0 + u + 1) % 2)
                before = n0 + u - 1
                if NA <= before and (k == "routed" or before < LAST):
                    j = before - NA
                    y_out(n - 1, j % SRC, None if j < 2 else i * 16 + ((j - 2) // SRC + 1) * 16)

            source_out(0, 0)
            for n0, times, k in runs:
                if n0 == NA - 2:
                    choice_weights()
                if times:
                    with act.Fori(0, times) as i:
                        for u in range(UNROLL[k]):
                            step(i * UNROLL[k] + (n0 + u), n0, u, k, i)
                else:
                    step(n0, n0, 0, k)

        @block.vector
        def _(dve):
            nc.vector.memset(eps[:, :], EPS)
            for u in range(2):
                nc.vector.memset(hid[u][:, I:IP], 0.0)
            for t in range(NT):
                nc.vector.bn_aggr(mv[:, t, :], stats[:, t, :])
            dve.drain().then_inc(var_done, 1)
            dve.wait_ge(std_done, 1)
            nc.vector.reciprocal(rstd[:, :], rstd[:, :])
            dve.drain().then_inc(rstd_ready, 1)

            def normalise(u, t):
                return nc.vector.tensor_scalar(src[u][:, 0:D], X[:, t, :], mv[:, t, 0:1], rstd[:, bass.ds(t, 1)],
                                               ALU.subtract, ALU.mult)

            for t in range(AHEAD):
                normalise(t, t).then_inc(l_src, 1)
            with dve.Fori(1, NT // AHEAD) as tt:
                for u in range(AHEAD):
                    dve.wait_ge(l_T, tt * AHEAD + (u + 1 - AHEAD))
                    dve.wait_ge(xn_stored[u], tt * 16)
                    normalise(u, tt * AHEAD + u).then_inc(l_src, 1)
            dve.wait_ge(l_lg, 1)
            nc.vector.tensor_copy(lg[:, :, :].rearrange("p t e -> p (t e)"), psL[:, 0:NT * (E + 1)])
            dve.drain().then_inc(lg_ready, 1)

            def choose(k):
                over_e = lambda v: v[:, :, None].to_broadcast([P, NT, E])
                index = iota8[:, None, :].to_broadcast([P, NT, E])
                at = lg[:, :, 0:E] if k == 0 else lg2[:, :, :]
                nc.vector.tensor_reduce(mx[k][:, :], at, AX.X, ALU.max)
                dve.drain()
                nc.vector.tensor_tensor(eq[:, :, :], at, over_e(mx[k]), ALU.is_equal)
                dve.drain()
                nc.vector.tensor_tensor(eq[:, :, :], eq[:, :, :], index, ALU.mult)
                dve.drain()
                nc.vector.tensor_reduce(ix[:, :], eq[:, :, :], AX.X, ALU.min)
                dve.drain()
                nc.vector.tensor_tensor(pk[k][:, :, :], index, over_e(ix), ALU.is_equal)
                dve.drain()
                if k == 0:
                    nc.vector.scalar_tensor_tensor(lg2[:, :, :], pk[0][:, :, :], -3.0e38, lg[:, :, 0:E],
                                                   ALU.mult, ALU.add)
                    dve.drain().then_inc(chosen, 1)
                else:
                    nc.vector.tensor_tensor(both[:, :, :], pk[0][:, :, :], pk[1][:, :, :], ALU.add)
                    nc.vector.tensor_tensor(gap[:, :], mx[0][:, :], mx[1][:, :], ALU.subtract)
                    dve.drain().then_inc(chosen, 1)

            by_e = lambda ap: ap.rearrange("p (t e) -> p e t", e=E)

            def counts():
                dve.wait_ge(rank_done, 1)
                flat = lambda v: v[:, :, :].rearrange("p e t -> p (e t)")
                nc.vector.tensor_copy(tot[:, :, :], by_e(psR[1]))
                dve.drain()
                nc.vector.tensor_tensor_scan(flat(cum), one256[:, :], flat(tot), 0.0, ALU.mult, ALU.add)
                dve.drain()
                nc.vector.tensor_tensor(exc[:, :, :], cum[:, :, :], tot[:, :, :], ALU.subtract)
                dve.drain()
                nc.vector.tensor_tensor(cnt[:, :], cum[:, :, NT - 1], exc[:, :, 0], ALU.subtract)
                dve.drain()
                nc.vector.tensor_scalar(cnti[:, :], cnt[:, :], float(P - 1), None, ALU.add)
                dve.drain()
                nc.vector.tensor_scalar(cnti[:, :], cnti[:, :], P.bit_length() - 1, None, ALU.arith_shift_right)
                dve.drain()
                nc.vector.tensor_copy(nblk[:, :], cnti[:, :])
                dve.drain()
                nc.vector.tensor_tensor_scan(bend[:, :], one256[:, 0:E], nblk[:, :], 0.0, ALU.mult, ALU.add)
                dve.drain()
                nc.vector.tensor_tensor(base[:, :], bend[:, :], nblk[:, :], ALU.subtract)
                dve.drain()
                nc.vector.scalar_tensor_tensor(base[:, :], base[:, :], float(P), exc[:, :, 0], ALU.mult, ALU.subtract)
                dve.drain()

            def positions():
                nc.vector.tensor_tensor(slot[:, :, :], exc[:, :, :],
                                        base[:, :, None].to_broadcast([P, E, NT]), ALU.add)
                dve.drain()
                nc.vector.tensor_tensor(slot[:, :, :], slot[:, :, :], by_e(psR[0]), ALU.add)
                dve.drain()
                for k in range(TOPK):
                    nc.vector.tensor_tensor(eq[:, :, :], pk[k][:, :, :], slot[:, :, :].rearrange("p e t -> p t e"), ALU.mult)
                    dve.drain()
                    nc.vector.tensor_reduce(posf[:, k * NT:(k + 1) * NT], eq[:, :, :], AX.X, ALU.add)
                    dve.drain()
                nc.vector.tensor_copy(pos[:, :], posf[:, :])
                dve.drain()
                nc.vector.tensor_scalar(part_i[:, :], pos[:, :], P - 1, None, ALU.bitwise_and)
                nc.vector.tensor_scalar(pos[:, :], pos[:, :], P.bit_length() - 1, None, ALU.arith_shift_right)
                dve.drain()
                nc.vector.tensor_copy(pos_p[:, :], part_i[:, :])
                nc.vector.tensor_copy(pos_j[:, :], pos[:, :])
                dve.drain()

            def one_hots(i):
                c = slice(i * PIECE, (i + 1) * PIECE)
                over = lambda v, n: v[:, c, None].to_broadcast([P, PIECE, n])
                if i >= 2:
                    dve.wait_ge(inv_done, i - 1)
                nc.vector.tensor_tensor(hot_j[:, :, :], iota_j[:, None, :].to_broadcast([P, PIECE, NB]),
                                        over(pos_j, NB), ALU.is_equal)
                nc.vector.tensor_tensor(hot_p[i % 2][:, :, :], iota_p[:, None, :].to_broadcast([P, PIECE, P]),
                                        over(pos_p, P), ALU.is_equal)
                dve.drain()
                nc.vector.tensor_tensor(hot_id[i % 2][:, :, 0, :], hot_j[:, :, :], over(tile1, NB), ALU.mult)
                nc.vector.tensor_scalar(hot_id[i % 2][:, :, 1, :], hot_j[:, :, :], lane[:, :], None, ALU.mult)
                dve.drain().then_inc(inv_ready, 1)

            def slots():
                dve.wait_ge(inv_done, CH // PIECE)
                of_tile, of_lane = psI[:, 0:NB], psI[:, NB:2 * NB]
                nc.vector.tensor_scalar(empty[:, :], of_tile, 0.0, None, ALU.is_equal)
                nc.vector.tensor_scalar(place[:, :], of_tile, float(P), None, ALU.mult)
                dve.drain()
                nc.vector.tensor_tensor(empty[:, :], empty[:, :], dump[:, :], ALU.mult)
                nc.vector.tensor_tensor(place[:, :], place[:, :], of_lane, ALU.add)
                dve.drain()
                nc.vector.tensor_tensor(place[:, :], place[:, :], empty[:, :], ALU.add)
                dve.drain()
                nc.vector.tensor_scalar(slots_i[:, :, 1], place[:, :], -float(P), None, ALU.add)
                dve.drain()
                nc.vector.tensor_scalar(slots_i[:, :, 0], slots_i[:, :, 1], TOKENS - 1, None,
                                        ALU.bitwise_and).then_inc(slots_ready, 1)

            def block_experts():
                nc.vector.tensor_tensor(ble[:, :, :], bend[0:1, None, :].to_broadcast([1, NB, E]),
                                        iotab[:, :, None].to_broadcast([1, NB, E]), ALU.is_le)
                dve.drain()
                nc.vector.tensor_reduce(bex[:, :], ble[:, :, :], AX.X, ALU.add)
                dve.drain()
                nc.vector.tensor_scalar(bexi[:, :], bex[:, :], float(E - 1), None, ALU.min).then_inc(bex_done, 1)

            def hidden(n, u):
                dve.wait_ge(u_done, n + 1)
                dve.wait_ge(silu_done, n + 1)
                nc.vector.tensor_tensor(hid[u][:, 0:I], silu[u][:, :], psU[u][:, 0:I], ALU.mult).then_inc(hid_ready, 1)

            def hidden_out(n, u):
                dve.wait_ge(hT_done, n + 1)
                nc.vector.tensor_copy(hidT[u][:, :, :].rearrange("p k t -> p (k t)"), psH[:, 0:IP]).then_inc(hidT_ready, 1)

            def add_shared(n, u, t):
                dve.wait_ge(d_done, n + 1)
                nc.vector.scalar_tensor_tensor(X[:, t, :], psD[:, 0:D], sg[:, bass.ds(t, 1)], X[:, t, :],
                                               ALU.mult, ALU.add).then_inc(d_used, 1)

            def source(n, u, t, sent):
                if sent:
                    dve.wait_ge(y_sent[u], 16 * (NB // SRC))
                else:
                    dve.wait_ge(T_done, n - 1)
                normalise(u, t).then_inc(src_ready, 1)

            def combine(t, s, count):
                for k in range(TOPK):
                    for i in range(2):
                        if k == 0:
                            dve.wait_ge(got_loaded[s + i], count)
                        last = nc.vector.scalar_tensor_tensor(X[:, t + i, :], got[:, s + i, k, :],
                                                              cw[k][:, bass.ds(t + i, 1)], X[:, t + i, :],
                                                              ALU.mult, ALU.add)
                        if k == 1:
                            last.then_inc(got_used, 1)
                    dve.drain()
                if store is None:
                    for i in range(2):
                        nc.vector.bn_stats(stats[:, t + i, :], X[:, t + i, :])

            def step(n, n0, u, k, between=None):
                ahead, here = n0 + u + 2, n0 + u
                if ahead < NS and kind(ahead) != "routed":
                    source(n + 2, here % 2, tile(n + 2, kind(ahead)), LAST <= ahead < LAST + 2)
                hidden_out(n, here % 2)
                if here + 1 < NS:
                    hidden(n + 1, (here + 1) % 2)
                if between is not None:
                    between()
                if k != "routed":
                    add_shared(n, here % 2, tile(n, k))

            for u in range(AHEAD):
                dve.wait_ge(xn_stored[u], 16 * (NT // AHEAD))
            normalise(0, 0).then_inc(src_ready, 1)
            normalise(1, 1).then_inc(src_ready, 1)
            dve.wait_ge(consts_done, 2)
            hidden(0, 0)
            finding = {0: lambda: choose(0), 1: lambda: choose(1), 2: counts, 3: positions,
                       FOUND - 1: block_experts, FOUND: slots}
            for n in range(NA):
                step(n, n, 0, "shared", finding.get(n, (lambda: one_hots(n - 4)) if 0 <= n - 4 < CH // PIECE else None))
            with dve.Fori(0, (NB - 6) // 2) as i:
                for u in range(2):
                    step(i * 2 + (NA + u), NA, u, "routed")
            for n in range(LAST - 6, LAST):
                step(n, n, 0, "routed")
            dve.wait_ge(cw_done, 1)
            for n in range(LAST, NS):
                t = 2 * (n - LAST - 2)
                step(n, n, 0, "late", (lambda: combine(t, t % GS, 16 * (t // GS + 1))) if 0 <= t < EARLY else None)
            with dve.Fori(EARLY // GS, NT // GS) as tt:
                for s in range(0, GS, 2):
                    combine(tt * GS + s, s, tt * 16 + 16)

        @block.tensor
        def _(pe):
            def transpose_rows(bank, u):
                for k in range(KD):
                    last = nc.tensor.transpose(bank[:, k * P:(k + 1) * P], src[u][:, k * P:(k + 1) * P], ident[:, :])
                return last

            def logits_in(t, b, first=False):
                pe.wait_ge(l_src, t + 1)
                if not first:
                    pe.wait_ge(l_srcT, t - 1)
                transpose_rows(ps[b % 2], b).then_inc(l_T, 1)

            def logits(t, u):
                pe.wait_ge(l_srcT, t + 1)
                for k in range(KD):
                    nc.tensor.matmul(psL[:, bass.ds(t * (E + 1), E + 1)], srcT[u][:, k, :],
                                     W["router"][:, k, :], start=(k == 0), stop=(k == KD - 1))

            pe.wait_ge(weights_loaded[0], weights_loaded[1])
            logits_in(0, 0, True)
            logits_in(1, 1, True)
            with pe.Fori(0, NT // AHEAD - 1) as tt:
                for u in range(AHEAD):
                    logits(tt * AHEAD + u, u % 2)
                    logits_in(tt * AHEAD + (u + 2), (u + 2) % AHEAD)
            for t in range(NT - AHEAD, NT):
                logits(t, t % 2)
                if t + 2 < NT:
                    logits_in(t + 2, (t + 2) % AHEAD)
            pe.drain().then_inc(l_lg, 1)

            def ranks():
                pe.wait_ge(chosen, 2)
                flat = both[:, :, :].rearrange("p t e -> p (t e)")
                nc.tensor.matmul(psR[0], upper[:, :], flat, start=True, stop=True)
                nc.tensor.matmul(psR[1], ones[:, :], flat, start=True, stop=True).then_inc(rank_done, 1)

            def inverse(i):
                pe.wait_ge(inv_ready, i + 1)
                for c in range(PIECE):
                    last = nc.tensor.matmul(psI, hot_p[i % 2][:, c, :], hot_id[i % 2][:, c, :, :].rearrange("p a j -> p (a j)"),
                                            start=(i == 0 and c == 0), stop=(i == CH // PIECE - 1 and c == PIECE - 1))
                last.then_inc(inv_done, 1)

            def rows_in(n, b, k, loaded):
                if k == "routed":
                    pe.wait_ge(src_loaded[b], loaded)
                else:
                    pe.wait_ge(src_ready, tile(n, k) + 1)
                if not (isinstance(n, int) and n == 0):
                    pe.wait_ge(srcT_ready, n)
                transpose_rows(psT, b).then_inc(T_done, 1)

            def gate_up(n, u, e):
                pe.wait_ge(srcT_ready, n + 1)
                if isinstance(n, int) and n < 2:
                    pe.wait_ge(lg_ready, 1)
                else:
                    pe.wait_ge(hid_ready, n - 1)
                for half, (bank, done) in enumerate(((psG, g_done), (psU, u_done))):
                    for k in range(KD):
                        last = nc.tensor.matmul(bank[u][:, 0:I], srcT[u][:, k, :],
                                                W["gate_up"][:, k, e, half * I:(half + 1) * I],
                                                start=(k == 0), stop=(k == KD - 1))
                    last.then_inc(done, 1)

            def hidden_T(n, u):
                pe.wait_ge(hid_ready, n + 1)
                if not (isinstance(n, int) and n == 0):
                    pe.wait_ge(hidT_ready, n)
                for k in range(KI):
                    last = nc.tensor.transpose(psH[:, k * P:(k + 1) * P], hid[u][:, k * P:(k + 1) * P], ident[:, :])
                last.then_inc(hT_done, 1)

            def down(n, u, e, before):
                pe.wait_ge(hidT_ready, n + 1)
                if before == "shared":
                    pe.wait_ge(d_used, n)
                elif before == "routed":
                    pe.wait_ge(y_ready, n - NA)
                elif before == "late":
                    pe.wait_ge(d_used, n - NB)
                for k in range(KI):
                    last = nc.tensor.matmul(psD[:, 0:D], hidT[u][:, k, :], W["down"][:, k, e, :],
                                            start=(k == 0), stop=(k == KI - 1))
                last.then_inc(d_done, 1)

            def expert(n, k):
                if k != "routed":
                    return SHARED
                return pe.value_load(bexi[0:1, bass.ds(n - NA, 1)], min_val=0, max_val=E - 1)

            def step(n, n0, u, k, i=0):
                here = n0 + u
                if here:
                    hidden_T(n - 1, (here - 1) % 2)
                gate_up(n, here % 2, expert(n, k))
                if here + 1 < NS:
                    nk = kind(here + 1)
                    loaded = None
                    if nk == "routed":
                        j = here + 1 - NA
                        loaded = i * 16 + (j // SRC + 1) * 16
                    rows_in(n + 1, buffer(here + 1, 0, nk), nk, loaded)
                if 6 <= here < 6 + CH // PIECE:
                    inverse(here - 6)
                if here == 3:
                    ranks()
                if here:
                    down(n - 1, (here - 1) % 2, expert(n - 1, kind(here - 1)), kind(here - 2) if here >= 2 else None)

            rows_in(0, 0, "shared", None)
            for n0, times, k in runs:
                if n0 == NA:
                    pe.wait_ge(bex_done, 1)
                if times:
                    with pe.Fori(0, times) as i:
                        for u in range(UNROLL[k]):
                            step(i * UNROLL[k] + (n0 + u), n0, u, k, i)
                else:
                    step(n0, n0, 0, k)
            hidden_T(NS - 1, (NS - 1) % 2)
            down(NS - 1, (NS - 1) % 2, SHARED, "late")


CHUNK = 64
NC = S // CHUNK
HALVES = P // CHUNK
XC = CHUNK + 2
ROWS = NC * B
MAX_LR, MIN_DECAY, MAX_NORM, NORM_EPS = 0.2, 0.5, 30.0, 1e-5


def memory_phase(nc, tag, X, x_loaded, stats, ident, ones, m0T, w1T, w2T, weights_loaded, rates_w, rates_b, gate_w, gate_b):
    ctx = ExitStack()
    sems = []
    ctx.callback(release, nc, sems)
    with ctx:
        sb = lambda n, s, d=F32: ctx.enter_context(nc.sbuf_tensor(f"{tag}_{n}", s, d))
        sem = lambda n: new_semaphore(nc, sems, f"{tag}_{n}")
        xT = sb("xT", [P, KD, NC, B, XC])
        km = sb("km", [P, KD, ROWS + 2])
        G = sb("G", [P, NC, B, XC])
        xn = [sb(f"xn{u}", [P, D]) for u in range(2)]
        st = sb("st", [P, NT, 6]); mv = sb("mv", [P, NT, 2]); rstd = sb("rstd", [P, NT]); eps = sb("eps", [P, 1])
        ss = sb("ss", [P, NT]); nrm = sb("nrm", [P, NT])
        half = sb("half", [P, HALVES])
        mean_w = sb("mean_w", [P, NT, 2 * HALVES])
        seq = sb("seq", [ROWS, B])
        gwb = sb("gwb", [P, KD, P])
        esel = sb("esel", [2, 2, P])
        sig = [sb(f"sig{u}", [2, B, XC]) for u in range(2)]
        ea = sb("ea", [2, NC, B])
        kk2 = sb("kk2", [P, KD, ROWS]); kks = sb("kks", [P, ROWS])
        m0n = sb("m0n", [P, 1])
        gate = sb("gate", [P, NC, B]); dec = sb("dec", [P, NC, B]); cdec = sb("cdec", [P, NC, B])
        beta = sb("beta", [P, NC, B]); boc = sb("boc", [P, NC, B]); rc = sb("rc", [P, NC, B])
        c2 = sb("c2", [P, NC, B]); coef = sb("coef", [P, NC, 2, B]); kk = sb("kk", [P, NC, B])
        A = [sb(f"A{v}", [P, B]) for v in range(2)]; n2 = sb("n2", [P, B]); n2c = sb("n2c", [P, B]); cA = sb("cA", [P, B])
        f = sb("f", [P, B]); rA = sb("rA", [P, B]); t2 = sb("t2", [P, 2, B]); root = sb("root", [P, B]); scl = sb("scl", [P, B])
        halfpow = sb("halfpow", [P, B])
        w2s = sb("w2s", [P, KD, D])
        ET = sb("ET", [P, KD, NC, B]); Erow = sb("Erow", [P, D])
        y = [sb(f"y{q}", [P, KD, B, HALVES, CHUNK]) for q in range(2)]
        ye = [sb(f"ye{v}", [P, KD, B, 2]) for v in range(2)]
        h = [sb(f"h{q}", [P, KD, B, HALVES, CHUNK]) for q in range(2)]
        hs = sb("hs", [P, KD, B])
        e = sb("e", [P, KD, B]); prod = sb("prod", [P, KD, 2, B]); prods = sb("prods", [P, 2, B])

        ps = [ctx.enter_context(nc.psum_tensor(f"{tag}_ps{i}", [P, 512], F32)) for i in range(8)]
        psO = [ps[0:2], ps[2:4]]; psU = ps[4:6]; psE = ps[6]; psF = ps[7]
        psT, psM, psG, psK = ps[0:2], ps[2], ps[5:7], ps[7]
        keys = lambda k: km[:, k, 0:ROWS]

        consts = sem("consts"); var_done = sem("var_done"); std_done = sem("std_done")
        ss_done = sem("ss_done"); nrm_done = sem("nrm_done"); meanw_done = sem("meanw_done")
        n_ready = sem("n_ready"); T_done = sem("T_done"); xT_ready = sem("xT_ready"); mean_done = sem("mean_done")
        xc_ready = sem("xc_ready"); sig_ready = sem("sig_ready"); ea_ready = sem("ea_ready")
        G_done = sem("G_done"); G_ready = sem("G_ready"); kk_ready = sem("kk_ready"); sc_done = sem("sc_done")
        gate_ready = sem("gate_ready")
        o_done = sem("o_done"); y_copied = sem("y_copied"); ye_ready = sem("ye_ready")
        A_ready = sem("A_ready"); us_ready = sem("us_ready"); y_scaled = sem("y_scaled"); u_done = sem("u_done"); h_ready = sem("h_ready")
        hs_ready = sem("hs_ready"); e_done = sem("e_done"); ET_ready = sem("ET_ready"); ER_done = sem("ER_done")
        Erow_ready = sem("Erow_ready"); prods_ready = sem("prods_ready"); pq_done = sem("pq_done")
        n2_ready = sem("n2_ready"); root_ready = sem("root_ready"); f_done = sem("f_done"); f_used = sem("f_used")
        cz = sem("cz")

        block = ctx.enter_context(nc.Block())

        @block.gpsimd
        def _(pool):
            nc.gpsimd.memset(G[:, :, :, :], 0.0)
            nc.gpsimd.memset(ET[:, :, :, :], 0.0)
            nc.gpsimd.memset(Erow[:, :], 0.0)
            nc.gpsimd.memset(halfpow[:, :], 0.5)
            nc.gpsimd.memset(half[:, :], 0.0)
            nc.gpsimd.memset(esel[:, 0, :], MAX_LR / CHUNK)
            nc.gpsimd.memset(esel[:, 1, :], (1.0 - MIN_DECAY) / CHUNK).then_inc(cz, 1)
            pool.wait_ge(cz, 1)
            nc.gpsimd.memset(half[0:CHUNK, 0:1], 1.0 / CHUNK)
            nc.gpsimd.memset(half[CHUNK:P, 1:2], 1.0 / CHUNK)
            nc.gpsimd.affine_select(out=esel[:, 0, :], in_=esel[:, 0, :], compare_op=ALU.is_equal, fill=0.0,
                                    base=0, pattern=[[0, P]], channel_multiplier=1)
            nc.gpsimd.affine_select(out=esel[:, 1, :], in_=esel[:, 1, :], compare_op=ALU.is_equal, fill=0.0,
                                    base=-1, pattern=[[0, P]], channel_multiplier=1).then_inc(consts, 1)
            with pool.Fori(0, NC // 4) as tq:
                for v in range(4):
                    t = tq * 4 + v
                    pool.wait_ge(A_ready, t + 1)
                    pool.wait_ge(u_done, t * KD + KD)
                    chunk = y[v // 2][:, :, :, v % 2, :]
                    nc.gpsimd.tensor_tensor(chunk, chunk, A[v % 2][:, None, :, None].to_broadcast([P, KD, B, CHUNK]),
                                            ALU.mult).then_inc(y_scaled, 1)
                    pool.wait_ge(n2_ready, t + 1)
                    nc.gpsimd.tensor_tensor(root[:, :], n2[:, :], halfpow[:, :], ALU.pow).then_inc(root_ready, 1)

        @block.scalar
        def _(act):
            nc.scalar.preload_act_table(ACT.Sqrt)
            act.wait_ge(var_done, 1)
            nc.scalar.activation(rstd[:, :], mv[:, :, 1], ACT.Sqrt, bias=eps[:, :]).then_inc(std_done, 1)
            act.wait_ge(ss_done, 1)
            nc.scalar.sqrt(nrm[:, :], ss[:, :]).then_inc(nrm_done, 1)
            nc.scalar.preload_act_table(ACT.Sigmoid)
            with act.Fori(0, B) as b:
                with act.Fori(0, NT // B // 2) as cc:
                    for u in range(2):
                        act.wait_ge(T_done, b * (NT // B) + cc * 2 + (u + 1))
                        for k in range(KD):
                            last = nc.scalar.copy(xT[:, k, bass.ds(cc * 4 + 2 * u, HALVES), b, 0:CHUNK],
                                                  psT[u][:, k * P:(k + 1) * P].rearrange("p (c s) -> p c s", c=HALVES))
                        last.then_inc(xT_ready, 1)
            act.wait_ge(sc_done, 1)
            nc.scalar.activation(gate[:, :, :].rearrange("p t b -> p (t b)"), psK[:, 0:ROWS], ACT.Sigmoid,
                                 bias=gate_b[:, :]).then_inc(gate_ready, 1)

            def rates(t, u):
                act.wait_ge(G_done, t + 1)
                nc.scalar.activation(sig[u][:, :, :].rearrange("p b c -> p (b c)"), psG[u][ROWS:ROWS + 2, 0:B * XC],
                                     ACT.Sigmoid, bias=rates_b[ROWS:ROWS + 2, :]).then_inc(sig_ready, 1)

            for u in range(2):
                rates(u, u)
            with act.Fori(1, NC // 2) as tt:
                for u in range(2):
                    act.wait_ge(ea_ready, tt * 2 + (u - 1))
                    rates(tt * 2 + u, u)
            nc.scalar.preload_act_table(ACT.Silu)

            def step(tq, v, first=False):
                t = tq * 4 + v
                q, c = v // 2, v % 2
                if not first:
                    act.wait_ge(f_done, tq * 8 + (-4 if q == 0 else 0))
                for o in range(KD):
                    act.wait_ge(o_done, t * KD + (o + 1))
                    nc.scalar.copy(y[q][:, o, :, c, :], psO[c][o][:, 0:B * XC].rearrange("p (b x) -> p b x", b=B)[:, :, 0:CHUNK]
                                   ).then_inc(y_copied, 1)
                for j in range(KD):
                    act.wait_ge(us_ready, t * KD + (j + 1))
                    nc.scalar.activation(h[q][:, j, :, c, :], h[q][:, j, :, c, :], ACT.Silu).then_inc(h_ready, 1)
                act.wait_ge(ER_done, t + 1)
                nc.scalar.copy(Erow[0:ROWS, :], psE[0:ROWS, D:2 * D]).then_inc(Erow_ready, 1)

            for v in range(4):
                step(0, v, True)
            with act.Fori(1, NC // 4) as tq:
                for v in range(4):
                    step(tq, v)

        @block.vector
        def _(dve):
            nc.vector.memset(eps[:, :], EPS)
            for q, loaded in enumerate(x_loaded):
                dve.wait_ge(loaded, 16)
                part = NT // len(x_loaded)
                with dve.Fori(q * part // 4, (q + 1) * part // 4) as tt:
                    for u in range(4):
                        nc.vector.bn_stats(st[:, tt * 4 + u, :], X[:, tt * 4 + u, :])
            dve.drain()
            for t in range(NT):
                nc.vector.bn_aggr(mv[:, t, :], st[:, t, :])
            dve.drain().then_inc(var_done, 1)
            dve.wait_ge(std_done, 1)
            nc.vector.reciprocal(rstd[:, :], rstd[:, :])
            dve.drain()
            nc.vector.tensor_tensor(ss[:, :], mv[:, :, 1], rstd[:, :], ALU.mult)
            dve.drain()
            nc.vector.tensor_tensor(ss[:, :], ss[:, :], rstd[:, :], ALU.mult)
            dve.drain()
            nc.vector.tensor_scalar(ss[:, :], ss[:, :], float(D), NORM_EPS ** 2, ALU.mult, ALU.max).then_inc(ss_done, 1)

            def normalise(b, i, u):
                t = b * (NT // B) + i
                nc.vector.tensor_scalar(xn[u][:, :], X[:, t, :], mv[:, t, 0:1], rstd[:, bass.ds(t, 1)],
                                        ALU.subtract, ALU.mult).then_inc(n_ready, 1)

            for u in range(2):
                normalise(0, u, u)
            dve.wait_ge(nrm_done, 1)
            nc.vector.reciprocal(nrm[:, :], nrm[:, :])
            dve.wait_ge(consts, 1)
            dve.drain()
            nc.vector.tensor_tensor(mean_w[:, :, 0:HALVES], nrm[:, :, None].to_broadcast([P, NT, HALVES]),
                                    half[:, None, :].to_broadcast([P, NT, HALVES]), ALU.mult)
            nc.vector.tensor_copy(mean_w[:, :, HALVES:], half[:, None, :].to_broadcast([P, NT, HALVES])).then_inc(meanw_done, 1)
            TB = NT // B
            for i in range(2, TB):
                dve.wait_ge(mean_done, i - 1)
                normalise(0, i, i % 2)
            with dve.Fori(1, B) as b:
                with dve.Fori(0, TB // 2) as cc:
                    for u in range(2):
                        dve.wait_ge(mean_done, b * TB + cc * 2 + (u - 1))
                        normalise(b, cc * 2 + u, u)
            dve.wait_ge(*weights_loaded)
            for k in range(KD):
                nc.vector.tensor_copy(gwb[:, k, :], gate_w[:, k:k + 1].to_broadcast([P, P]))
            nc.vector.tensor_scalar(w2s[:, :, :], w2T[:, :, :], 1.0 / CHUNK, None, ALU.mult)
            nc.vector.tensor_reduce(seq[:, :], ident[0:ROWS, 0:ROWS].rearrange("p (t b) -> p b t", b=B), AX.X, ALU.add)
            flat0 = m0T[:, :, :].rearrange("p k o -> p (k o)")
            squares = h[0][:, :, :, :, :].rearrange("p k b c s -> p (k b c s)")[:, 0:KD * D]
            nc.vector.scalar_tensor_tensor(squares, flat0, 1.0, flat0, ALU.mult, ALU.mult, accum_out=m0n[:, :])
            dve.wait_ge(mean_done, NT)
            dve.wait_ge(xT_ready, NT)
            for k in range(KD):
                means = psM[:, k * NT * 4:(k + 1) * NT * 4].rearrange("p (b i c) -> p b i c", b=B, c=2 * HALVES)
                tb = lambda v: v.rearrange("p (i c) b -> p b i c", c=HALVES)
                for b in range(B):
                    nc.vector.tensor_copy(tb(keys(k).rearrange("p (t b) -> p t b", b=B))[:, b], means[:, b, :, 0:HALVES])
                    nc.vector.tensor_copy(tb(xT[:, k, :, :, CHUNK])[:, b], means[:, b, :, 0:HALVES])
            dve.drain()
            for k in range(KD):
                means = psM[:, k * NT * 4:(k + 1) * NT * 4].rearrange("p (b i c) -> p b i c", b=B, c=2 * HALVES)
                for b in range(B):
                    nc.vector.tensor_tensor(tb(xT[:, k, :, :, CHUNK + 1])[:, b], means[:, b, :, HALVES:],
                                            tb(keys(k).rearrange("p (t b) -> p t b", b=B))[:, b], ALU.subtract)
            nc.vector.tensor_copy(km[:, :, ROWS:], rates_w[:, :, :])
            nc.vector.tensor_tensor(kk2[:, :, :], km[:, :, 0:ROWS], km[:, :, 0:ROWS], ALU.mult)
            dve.drain().then_inc(xc_ready, 1)
            nc.vector.tensor_tensor(kks[:, :], kk2[:, 0, :], kk2[:, 1, :], ALU.add).then_inc(kk_ready, 1)
            with dve.Fori(0, NC // 2) as tt:
                for u in range(2):
                    t = tt * 2 + u
                    dve.wait_ge(sig_ready, t + 1)
                    nc.vector.tensor_tensor(G[0:ROWS, t, :, :], psG[u][0:ROWS, 0:B * XC].rearrange("p (b c) -> p b c", b=B),
                                            seq[:, :, None].to_broadcast([ROWS, B, XC]), ALU.mult).then_inc(G_ready, 1)
                    nc.vector.tensor_reduce(ea[:, t, :], sig[u][:, :, 0:CHUNK], AX.X, ALU.add).then_inc(ea_ready, 1)
            dve.wait_ge(gate_ready, 1)
            dve.wait_ge(sc_done, 2)
            fl = lambda v: v[:, :, :].rearrange("p t b -> p (t b)")
            nc.vector.tensor_copy(fl(kk), psK[:, ROWS:2 * ROWS])
            nc.vector.tensor_copy(n2[:, :], psK[:, 2 * ROWS:2 * ROWS + 1].to_broadcast([P, B]))
            nc.vector.tensor_tensor(fl(beta), psK[:, 256:256 + ROWS], fl(gate), ALU.mult)
            nc.vector.tensor_scalar(fl(dec), psK[:, 256 + ROWS:256 + 2 * ROWS], MIN_DECAY - 1.0, None, ALU.add)
            dve.drain()
            nc.vector.tensor_tensor(fl(cdec), fl(dec), fl(gate), ALU.mult)
            dve.drain()
            nc.vector.tensor_scalar(fl(dec), fl(cdec), 1.0, None, ALU.add)
            dve.drain()
            nc.vector.reciprocal(fl(rc), fl(dec))
            nc.vector.tensor_tensor(fl(c2), fl(dec), fl(dec), ALU.mult)
            nc.vector.scalar_tensor_tensor(coef[:, :, 0, :], dec[:, :, :], 2.0, beta[:, :, :], ALU.mult, ALU.mult)
            nc.vector.tensor_tensor(fl(gate), fl(beta), fl(beta), ALU.mult)
            dve.drain()
            nc.vector.tensor_tensor(fl(boc), fl(beta), fl(rc), ALU.mult)
            nc.vector.tensor_tensor(coef[:, :, 1, :], gate[:, :, :], kk[:, :, :], ALU.mult)
            nc.vector.memset(A[0][:, :], 1.0)
            nc.vector.memset(rA[:, :], 1.0)
            dve.drain().then_inc(A_ready, 1)

            def step(tq, v, no_result, first=False):
                t = tq * 4 + v
                q, c = v // 2, v % 2
                scale = A[v % 2]
                dve.wait_ge(y_copied, t * KD + KD)
                for o in range(KD):
                    out = psO[v % 2][o][:, 0:B * XC].rearrange("p (b c) -> p b c", b=B)
                    last = nc.vector.tensor_tensor(ye[v % 2][:, o, :, :], out[:, :, CHUNK:],
                                                   scale[:, :, None].to_broadcast([P, B, 2]), ALU.mult)
                last.then_inc(ye_ready, 1)
                nc.vector.tensor_tensor(f[:, :], boc[:, t, :], rA[:, :], ALU.mult)
                nc.vector.tensor_tensor(n2c[:, :], c2[:, t, :], n2[:, :], ALU.mult)
                nc.vector.tensor_tensor(cA[:, :], dec[:, t, :], scale[:, :], ALU.mult)
                for j in range(KD):
                    dve.wait_ge(u_done, t * KD + (j + 1))
                    nc.vector.tensor_tensor(h[q][:, j, :, c, :], psU[j][:, 0:B * CHUNK].rearrange("p (b s) -> p b s", b=B),
                                            scale[:, :, None].to_broadcast([P, B, CHUNK]), ALU.mult).then_inc(us_ready, 1)
                for j in range(KD):
                    dve.wait_ge(h_ready, t * KD + (j + 1))
                    nc.vector.tensor_reduce(hs[:, j, :], h[q][:, j, :, c, :], AX.X, ALU.add).then_inc(hs_ready, 1)
                if not no_result:
                    result(tq, v, 0)
                dve.wait_ge(e_done, t + 1)
                nc.vector.tensor_tensor(e[:, :, :], psE[:, 0:KD * B].rearrange("p (k b) -> p k b", k=KD),
                                        ye[v % 2][:, :, :, 1], ALU.add)
                dve.drain()
                nc.vector.tensor_tensor(ET[:, :, t, :], e[:, :, :], f[:, None, :].to_broadcast([P, KD, B]),
                                        ALU.mult).then_inc(ET_ready, 1)
                nc.vector.tensor_tensor(prod[:, :, 0, :], e[:, :, :], ye[v % 2][:, :, :, 0], ALU.mult)
                nc.vector.tensor_tensor(prod[:, :, 1, :], e[:, :, :], e[:, :, :], ALU.mult)
                dve.drain()
                nc.vector.tensor_tensor(prods[:, :, :], prod[:, 0, :, :], prod[:, 1, :, :], ALU.add).then_inc(prods_ready, 1)
                dve.wait_ge(pq_done, t + 1)
                nc.vector.tensor_tensor(t2[:, :, :], coef[:, t, :, :], psU[1][:, 256:256 + 2 * B].rearrange("p (q b) -> p q b", q=2),
                                        ALU.mult)
                dve.drain()
                nc.vector.tensor_tensor(n2c[:, :], n2c[:, :], t2[:, 0, :], ALU.add)
                dve.drain()
                nc.vector.tensor_tensor(n2c[:, :], n2c[:, :], t2[:, 1, :], ALU.add)
                dve.drain()
                nc.vector.tensor_scalar(n2[:, :], n2c[:, :], 0.0, None, ALU.max).then_inc(n2_ready, 1)
                dve.wait_ge(root_ready, t + 1)
                nc.vector.tensor_scalar(scl[:, :], root[:, :], 1e-6, None, ALU.add)
                dve.drain()
                nc.vector.reciprocal(scl[:, :], scl[:, :])
                dve.drain()
                nc.vector.tensor_scalar(scl[:, :], scl[:, :], MAX_NORM, 1.0, ALU.mult, ALU.min)
                dve.drain()
                if not first:
                    dve.wait_ge(y_scaled, t)
                nc.vector.tensor_tensor(A[1 - v % 2][:, :], cA[:, :], scl[:, :], ALU.mult)
                nc.vector.tensor_tensor(n2[:, :], n2[:, :], scl[:, :], ALU.mult)
                dve.drain().then_inc(A_ready, 1)
                nc.vector.reciprocal(rA[:, :], A[1 - v % 2][:, :])
                nc.vector.tensor_tensor(n2[:, :], n2[:, :], scl[:, :], ALU.mult)
                dve.drain()
                if not no_result:
                    result(tq, v, 1)
                    statistics(tq, v)

            def pair_tile(tq, v, i):
                return tq * 2 + (0 if v >= 2 else -1) + (v % 2 * 2 + i) * (NT // B)

            def statistics(tq, v):
                dve.drain()
                for i in range(2):
                    nc.vector.bn_stats(stats[:, pair_tile(tq, v, i), :], X[:, pair_tile(tq, v, i), :])

            def result(tq, v, i):
                t = pair_tile(tq, v, i)
                dve.wait_ge(f_done, tq * 8 + (v - 2) * 2 + (i + 1))
                nc.vector.tensor_tensor(X[:, t, :], X[:, t, :], psF[:, 0:D], ALU.add).then_inc(f_used, 1)

            for v in range(4):
                step(0, v, v < 2, v == 0)
            with dve.Fori(1, NC // 4) as tq:
                for v in range(4):
                    step(tq, v, False)
            for v in range(2):
                for i in range(2):
                    result(NC // 4, v, i)
                statistics(NC // 4, v)

        @block.tensor
        def _(pe):
            TB = NT // B
            pe.wait_ge(meanw_done, 1)

            def rows_in(b, i, u, first=False):
                t = b * TB + i
                pe.wait_ge(n_ready, t + 1)
                if not first:
                    pe.wait_ge(xT_ready, t - 1)
                for k in range(KD):
                    last = nc.tensor.transpose(psT[u][:, k * P:(k + 1) * P], xn[u][:, k * P:(k + 1) * P], ident[:, :])
                last.then_inc(T_done, 1)
                for k in range(KD):
                    last = nc.tensor.matmul(psM[:, bass.ds((t + k * NT) * 4, 4)], xn[u][:, k * P:(k + 1) * P],
                                            mean_w[:, t, :], start=True, stop=True)
                last.then_inc(mean_done, 1)

            for i in range(TB):
                rows_in(0, i, i % 2, i < 2)
            with pe.Fori(1, B) as b:
                with pe.Fori(0, TB // 2) as cc:
                    for u in range(2):
                        rows_in(b, cc * 2 + u, u)
            pe.wait_ge(xc_ready, 1)
            for k in range(KD):
                last = nc.tensor.matmul(psK[:, 0:ROWS], gwb[:, k, :], keys(k), start=(k == 0), stop=(k == KD - 1))
            pe.wait_ge(kk_ready, 1)
            nc.tensor.matmul(psK[:, ROWS:2 * ROWS], ones[:, :], kks[:, :], start=True, stop=True)
            nc.tensor.matmul(psK[:, 2 * ROWS:2 * ROWS + 1], ones[:, :], m0n[:, :], start=True, stop=True).then_inc(sc_done, 1)

            def rates_and_products(t, u, first):
                if not first:
                    pe.wait_ge(G_ready, t - 1)
                for k in range(KD):
                    xk = xT[:, k, t, :, :].rearrange("p b c -> p (b c)")
                    last = nc.tensor.matmul(psG[u][0:ROWS + 2, 0:B * XC], km[:, k, :], xk, start=(k == 0), stop=(k == KD - 1))
                last.then_inc(G_done, 1)

            for u in range(2):
                rates_and_products(u, u, True)
            with pe.Fori(1, NC // 2) as tt:
                for u in range(2):
                    rates_and_products(tt * 2 + u, u, False)
            pe.wait_ge(ea_ready, NC)
            pe.wait_ge(gate_ready, 1)
            for i in range(2):
                last = nc.tensor.matmul(psK[:, 256 + i * ROWS:256 + (i + 1) * ROWS], esel[:, i, :],
                                        ea[:, :, :].rearrange("p t b -> p (t b)"), start=True, stop=True)
            last.then_inc(sc_done, 1)
            pe.wait_ge(A_ready, 1)
            pe.wait_ge(G_ready, NC)

            def first_memory(t, v, o):
                for k in range(KD):
                    nc.tensor.matmul(psO[v % 2][o][:, 0:B * XC], m0T[:, k, o * P:(o + 1) * P],
                                     xT[:, k, t, :, :].rearrange("p b c -> p (b c)"), start=(k == 0), stop=False)

            def result_hidden(tq, v, i):
                q = 0 if v >= 2 else 1
                b = v % 2 * 2 + i
                count = tq * 8 + (v - 2) * 2 + i
                if not (isinstance(tq, int) and tq == 0 and v == 2 and i == 0):
                    pe.wait_ge(f_used, count)
                for k in range(KD):
                    nc.tensor.matmul(psF[:, 0:D], h[q][:, k, b, :, :].rearrange("p c s -> p (c s)"), w2T[:, k, :],
                                     start=(k == 0), stop=False, skip_group_check=True)

            def result_outputs(tq, v, i):
                q = 0 if v >= 2 else 1
                b = v % 2 * 2 + i
                pe.wait_ge(y_scaled, tq * 4 + (2 if v >= 2 else 0))
                for o in range(KD):
                    last = nc.tensor.matmul(psF[:, o * P:(o + 1) * P], y[q][:, o, b, :, :].rearrange("p c s -> p (c s)"),
                                            ident[:, :], start=False, stop=(o == KD - 1), skip_group_check=True)
                last.then_inc(f_done, 1)

            def step(tq, v, no_result, first=False, last_step=False):
                t = tq * 4 + v
                q, c = v // 2, v % 2
                if not first:
                    pe.wait_ge(Erow_ready, t)
                for o in range(KD):
                    nc.tensor.matmul(psO[v % 2][o][:, 0:B * XC], Erow[:, o * P:(o + 1) * P],
                                     G[:, t, :, :].rearrange("p b c -> p (b c)"), start=False, stop=True).then_inc(o_done, 1)
                if not last_step:
                    if not first:
                        pe.wait_ge(ye_ready, t)
                    first_memory(t + 1, v + 1, 0)
                pe.wait_ge(y_copied, t * KD + KD)
                if not first:
                    pe.wait_ge(n2_ready, t)
                for j in range(KD):
                    for o in range(KD):
                        last = nc.tensor.matmul(psU[j][:, 0:B * CHUNK], w1T[:, o, j * P:(j + 1) * P],
                                                y[q][:, o, :, c, :], start=(o == 0), stop=(o == KD - 1))
                    last.then_inc(u_done, 1)
                if not last_step:
                    first_memory(t + 1, v + 1, 1)
                if not no_result:
                    result_hidden(tq, v, 0)
                    result_outputs(tq, v, 0)
                pe.wait_ge(hs_ready, t * KD + KD)
                for o in range(KD):
                    for j in range(KD):
                        last = nc.tensor.matmul(psE[:, o * B:(o + 1) * B], w2s[:, j, o * P:(o + 1) * P], hs[:, j, :],
                                                start=(j == 0), stop=(j == KD - 1))
                last.then_inc(e_done, 1)
                if not no_result:
                    result_hidden(tq, v, 1)
                pe.wait_ge(ET_ready, t + 1)
                for o in range(KD):
                    last = nc.tensor.matmul(psE[0:ROWS, D + o * P:D + (o + 1) * P], ET[:, o, :, :].rearrange("p t b -> p (t b)"),
                                            ident[:, :], start=True, stop=True)
                last.then_inc(ER_done, 1)
                pe.wait_ge(prods_ready, t + 1)
                nc.tensor.matmul(psU[1][:, 256:256 + 2 * B], ones[:, :], prods[:, :, :].rearrange("p q b -> p (q b)"),
                                 start=True, stop=True).then_inc(pq_done, 1)
                if not no_result:
                    result_outputs(tq, v, 1)

            for o in range(KD):
                first_memory(0, 0, o)
            for v in range(4):
                step(0, v, v < 2, v == 0)
            with pe.Fori(1, NC // 4 - 1) as tq:
                for v in range(4):
                    step(tq, v, False)
            for v in range(4):
                step(NC // 4 - 1, v, False, False, v == 3)
            for v in range(2):
                for i in range(2):
                    result_hidden(NC // 4, v, i)
                    result_outputs(NC // 4, v, i)


HEADS, HD = 16, 16
GROUP = 4
NG = HEADS // GROUP
CT = 4
CW = CT * P
NCH = TOKENS // CW
QT = S // P
HALF = 512
Q_PARTS = [0, 0, 0, 1, 1, 2]
K_PARTS = [0, 1, 2, 0, 1, 0]
KROWS = len(Q_PARTS) * HD
MROWS = KROWS + 3
VC = HD + 1


def qkv_phase(nc, tag, X, stats, ident, wqk, wv, bqk, bv, bo, weights_loaded, qk_d, v_d):
    ctx = ExitStack()
    sems = []
    ctx.callback(release, nc, sems)
    with ctx:
        sb = lambda n, s, d=F32: ctx.enter_context(nc.sbuf_tensor(f"{tag}_{n}", s, d))
        sem = lambda n: new_semaphore(nc, sems, f"{tag}_{n}")
        xn = [sb(f"xn{j}", [P, D]) for j in range(CT)]
        xT = [sb(f"xT{u}", [P, KD, CW]) for u in range(2)]
        mv = sb("mv", [P, NT, 2]); rstd = sb("rstd", [P, NT]); eps = sb("eps", [P, 1])
        NM = 2 * KD
        parts = [[sb(f"parts{u}{m}", [P, 3, CW], BF16) for m in range(NM)] for u in range(2)]
        rest = [[sb(f"rest{u}{m}", [P, CW]) for m in range(NM)] for u in range(2)]
        vt = [[sb(f"vt{u}{j}", [P, HEADS, VC]) for j in range(CT)] for u in range(2)]
        ps = [ctx.enter_context(nc.psum_tensor(f"{tag}_ps{i}", [P, 512], F32)) for i in range(8)]
        psT, psQ, psV = ps[0:2], ps[2:6], ps[6:8]

        var_done = sem("var_done"); std_done = sem("std_done")
        n_ready = sem("n_ready"); T_done = sem("T_done"); xT_ready = sem("xT_ready")
        qk_done = sem("qk_done"); hi_ready = sem("hi_ready"); rest_ready = sem("rest_ready")
        mid_ready = sem("mid_ready"); lo_ready = sem("lo_ready")
        v_done = sem("v_done"); v_ready = sem("v_ready")
        parts_stored = [sem(f"parts_stored{u}") for u in range(2)]
        v_stored = [sem(f"v_stored{u}") for u in range(2)]

        block = ctx.enter_context(nc.Block())

        @block.sync
        def _(sp):
            with sp.Fori(0, NCH // 2) as cc:
                for u in range(2):
                    for m in range(NM):
                        sp.wait_ge(lo_ready, cc * (2 * NM) + (u * NM + m + 1))
                        sp.dma_start(qk_d[m // KD, :, cc, (m % KD) * P:(m % KD + 1) * P, u * CW:(u + 1) * CW]
                                     .rearrange("s p t -> p s t"), parts[u][m][:, :, :]).then_inc(parts_stored[u], 16)
                    for j in range(CT):
                        sp.wait_ge(v_ready, cc * (2 * CT) + (u * CT + j + 1))
                        sp.dma_start(v_d[cc, :, :, u * CT + j, :].rearrange("g p c -> p g c"),
                                     vt[u][j][:, :, :].rearrange("p (g h) c -> p g (h c)", g=NG)).then_inc(v_stored[u], 16)
            for u in range(2):
                sp.wait_ge(parts_stored[u], 16 * NM * (NCH // 2))
                sp.wait_ge(v_stored[u], 16 * CT * (NCH // 2))

        @block.gpsimd
        def _(pool):
            pool.wait_ge(*weights_loaded)
            with pool.Fori(0, NCH // 2) as cc:
                for u in range(2):
                    for m in range(NM):
                        pool.wait_ge(mid_ready, cc * (2 * NM) + (u * NM + m + 1))
                        nc.gpsimd.tensor_tensor(parts[u][m][:, 2, :], rest[u][m][:, :], parts[u][m][:, 1, :],
                                                ALU.subtract).then_inc(lo_ready, 1)
                    for j in range(CT):
                        pool.wait_ge(n_ready, cc * (2 * CT) + (u * CT + j + 1))
                        t = cc * (2 * CT) + (u * CT + j)
                        nc.gpsimd.tensor_tensor(X[:, t, :], X[:, t, :], bo[:, :], ALU.add)

        @block.scalar
        def _(act):
            nc.scalar.preload_act_table(ACT.Sqrt)
            act.wait_ge(var_done, 1)
            nc.scalar.activation(rstd[:, :], mv[:, :, 1], ACT.Sqrt, bias=eps[:, :]).then_inc(std_done, 1)

            def rows_out(c, u):
                act.wait_ge(T_done, c + 1)
                for k in range(KD):
                    last = nc.scalar.copy(xT[u][:, k, :], psT[k][:, :])
                last.then_inc(xT_ready, 1)

            def high(c, u, m):
                act.wait_ge(qk_done, c * NM + (m + 1))
                nc.scalar.activation(parts[u][m][:, 0, :], psQ[m][:, :], ACT.Identity,
                                     bias=bqk[:, m:m + 1]).then_inc(hi_ready, 1)

            rows_out(0, 0)
            act.wait_ge(*weights_loaded)
            for u in range(2):
                for m in range(NM):
                    high(u, u, m)
                rows_out(u + 1, 1 - u)
            with act.Fori(1, NCH // 2 - 1) as cc:
                for u in range(2):
                    act.wait_ge(parts_stored[u], cc * (16 * NM))
                    for m in range(NM):
                        high(cc * 2 + u, u, m)
                    rows_out(cc * 2 + (u + 1), 1 - u)
            for u in range(2):
                act.wait_ge(parts_stored[u], (NCH // 2 - 1) * 16 * NM)
                for m in range(NM):
                    high(NCH - 2 + u, u, m)
                if u == 0:
                    rows_out(NCH - 1, 1)

        @block.vector
        def _(dve):
            nc.vector.memset(eps[:, :], EPS)
            for u in range(2):
                for j in range(CT):
                    nc.vector.memset(vt[u][j][:, :, HD:VC], 1.0)
            for t in range(NT):
                nc.vector.bn_aggr(mv[:, t, :], stats[:, t, :])
            dve.drain().then_inc(var_done, 1)
            dve.wait_ge(std_done, 1)
            nc.vector.reciprocal(rstd[:, :], rstd[:, :])
            dve.drain()

            def rows(c):
                for j in range(CT):
                    t = c * CT + j
                    nc.vector.tensor_scalar(xn[j][:, :], X[:, t, :], mv[:, t, 0:1], rstd[:, bass.ds(t, 1)],
                                            ALU.subtract, ALU.mult).then_inc(n_ready, 1)

            def chunk(c, u, stored=None, more=True):
                if more:
                    dve.wait_ge(T_done, c + 1)
                    rows(c + 1)
                if stored is not None:
                    dve.wait_ge(parts_stored[u], stored * 16 * NM)
                    dve.wait_ge(v_stored[u], stored * 16 * CT)
                for m in range(NM):
                    dve.wait_ge(hi_ready, c * NM + (m + 1))
                    nc.vector.scalar_tensor_tensor(rest[u][m][:, :], psQ[m][:, :], bqk[:, m:m + 1],
                                                   parts[u][m][:, 0, :], ALU.add, ALU.subtract).then_inc(rest_ready, 1)
                    dve.wait_ge(rest_ready, c * NM + (m + 1))
                    nc.vector.tensor_copy(parts[u][m][:, 1, :], rest[u][m][:, :]).then_inc(mid_ready, 1)
                for j in range(CT):
                    dve.wait_ge(v_done, c * CT + (j + 1))
                    nc.vector.tensor_tensor(vt[u][j][:, :, 0:HD],
                                            psV[j % 2][:, 0:D].rearrange("p (h d) -> p h d", d=HD),
                                            bv[:, :].rearrange("p (h d) -> p h d", d=HD), ALU.add).then_inc(v_ready, 1)

            rows(0)
            dve.wait_ge(*weights_loaded)
            chunk(0, 0)
            chunk(1, 1)
            with dve.Fori(1, NCH // 2 - 1) as cc:
                for u in range(2):
                    chunk(cc * 2 + u, u, cc)
            chunk(NCH - 2, 0, NCH // 2 - 1)
            chunk(NCH - 1, 1, NCH // 2 - 1, False)

        @block.tensor
        def _(pe):
            def rows_in(c, first=False):
                pe.wait_ge(n_ready, c * CT + CT)
                if not first:
                    pe.wait_ge(xT_ready, c)
                for k in range(KD):
                    for j in range(CT):
                        last = nc.tensor.transpose(psT[k][:, j * P:(j + 1) * P], xn[j][:, k * P:(k + 1) * P], ident[:, :])
                last.then_inc(T_done, 1)

            def chunk(c, u, first=False, more=True):
                pe.wait_ge(xT_ready, c + 1)
                for m in range(NM):
                    if not first:
                        pe.wait_ge(rest_ready, c * NM + (m + 1 - NM))
                    for k in range(KD):
                        last = nc.tensor.matmul(psQ[m][:, :], wqk[:, k, m * P:(m + 1) * P], xT[u][:, k, :],
                                                start=(k == 0), stop=(k == KD - 1))
                    last.then_inc(qk_done, 1)
                if more:
                    rows_in(c + 1)
                for j in range(CT):
                    if not (first and j < 2):
                        pe.wait_ge(v_ready, c * CT + (j - 1))
                    for k in range(KD):
                        last = nc.tensor.matmul(psV[j % 2][:, 0:D], xT[u][:, k, j * P:(j + 1) * P], wv[:, k, :],
                                                start=(k == 0), stop=(k == KD - 1))
                    last.then_inc(v_done, 1)

            rows_in(0, True)
            pe.wait_ge(*weights_loaded)
            chunk(0, 0, True)
            chunk(1, 1)
            with pe.Fori(1, NCH // 2 - 1) as cc:
                for u in range(2):
                    chunk(cc * 2 + u, u)
            chunk(NCH - 2, 0)
            chunk(NCH - 1, 1, False, False)


def scores_phase(nc, tag, ident, identb, qk_d, v_d, o_d):
    ctx = ExitStack()
    sems = []
    ctx.callback(release, nc, sems)
    with ctx:
        sb = lambda n, s, d=F32: ctx.enter_context(nc.sbuf_tensor(f"{tag}_{n}", s, d))
        sem = lambda n: new_semaphore(nc, sems, f"{tag}_{n}")
        qs = [sb(f"qs{g}", [MROWS, GROUP, S], BF16) for g in range(NG)]
        ks = [sb(f"ks{g}", [MROWS, GROUP, S], BF16) for g in range(NG)]
        va = [sb(f"va{g}", [P, QT, GROUP * VC]) for g in range(NG)]
        pt = [[sb(f"pt{v}{h}", [P, 2, HALF]) for h in range(2)] for v in range(2)]
        SUB = 2 * QT * GROUP
        mxh = sb("mxh", [P, QT, GROUP, 2])
        mx = sb("mx", [P, QT * GROUP])
        zeros = sb("zeros", [P, QT * GROUP])
        mxr = sb("mxr", [P, QT * GROUP])
        mx3 = sb("mx3", [P, QT, GROUP, 3], BF16)
        mxT = [sb(f"mxT{v}", [GROUP * 3, S], BF16) for v in range(2)]
        osb = [sb(f"osb{h}", [P, HALF]) for h in range(2)]
        rden = [sb(f"rden{h}", [P, QT // 2, GROUP]) for h in range(2)]
        ot = [sb(f"ot{h}", [P, QT // 2, GROUP, HD]) for h in range(2)]
        psS = [ctx.enter_context(nc.psum_tensor(f"{tag}_psS{h}", [P, HALF], F32)) for h in range(2)]
        psE = [ctx.enter_context(nc.psum_tensor(f"{tag}_psE{h}", [P, 2, HALF], F32)) for h in range(2)]
        psO = ctx.enter_context(nc.psum_tensor(f"{tag}_psO", [P, HALF], F32))
        psX = ctx.enter_context(nc.psum_tensor(f"{tag}_psX", [P, HALF], F32))

        rows_ready = sem("rows_ready"); psO_cleared = sem("psO_cleared")
        loaded = [sem(f"loaded{g}") for g in range(NG)]
        v_loaded = [sem(f"v_loaded{g}") for g in range(NG)]
        sub_done = sem("sub_done"); sub_used = sem("sub_used")
        mx_found = sem("mx_found"); mx_ready = sem("mx_ready"); mxT_done = sem("mxT_done"); mxT_ready = sem("mxT_ready")
        mx_rows = [sem(f"mx_rows{g}") for g in range(NG)]
        e_done = sem("e_done"); p_ready = sem("p_ready"); pv_done = sem("pv_done")
        o_ready = sem("o_ready"); oT_done = sem("oT_done"); ot_ready = sem("ot_ready")
        o_stored = [sem(f"o_stored{h}") for h in range(2)]

        SLOTS = 2 * QT
        SHARE = SUB // SLOTS
        LEAD = 4
        EARLY = 4
        following = lambda b, g: (b, g + 1) if g + 1 < NG else (b + 1, 0)

        def taken_along(b, g, s):
            nb, ng = following(b, g)
            first = (s + LEAD) % SLOTS * SHARE
            if s >= SLOTS - LEAD:
                nb, ng = following(nb, ng)
            return nb, ng, range(first, first + SHARE)

        MAX_T = (SLOTS - LEAD, SLOTS - LEAD + 1)
        in_range = lambda b, g: not (isinstance(b, int) and b >= B)
        before = lambda b, g, n: b * (NG * n) + g * n

        block = ctx.enter_context(nc.Block())

        @block.sync
        def _(sp):
            def load(b, g):
                for dst, w, parts in ((qs, 0, Q_PARTS), (ks, 1, K_PARTS)):
                    for i, part in enumerate(parts):
                        sp.dma_start(dst[g][i * HD:(i + 1) * HD, :, :],
                                     qk_d[w, part, b, g * GROUP * HD:(g + 1) * GROUP * HD, :]
                                     .rearrange("(r d) t -> d r t", d=HD)).then_inc(loaded[g], 16)
                sp.dma_start(va[g][:, :, :], v_d[b, g, :, :, :]).then_inc(v_loaded[g], 16)

            def max_rows(b, g):
                sp.wait_ge(mxT_ready, before(b, g, 2) + 2)
                for r in range(GROUP):
                    sp.dma_start(qs[g][KROWS:MROWS, r, :], mxT[g % 2][r * 3:(r + 1) * 3, :]).then_inc(mx_rows[g], 16)

            def results(b, g, h):
                sp.wait_ge(ot_ready, before(b, g, 2) + (h + 2))
                sp.dma_start(o_d[b, h * QT // 2:(h + 1) * QT // 2, :, g * GROUP * HD:(g + 1) * GROUP * HD]
                             .rearrange("t p c -> p t c"),
                             ot[h][:, :, :, :].rearrange("p t r c -> p t (r c)")).then_inc(o_stored[h], 16)

            def group(b, g, last):
                results(b, g, 0)
                if not (last and g == NG - 1):
                    max_rows(*following(b, g))
                if not last:
                    sp.wait_ge(pv_done, before(b, g, SLOTS) + SLOTS)
                    load(b + 1, g)
                results(b, g, 1)

            for h in range(2):
                sp.sem_inc(o_stored[h], 16)
            for g in range(NG):
                load(0, g)
            max_rows(0, 0)
            with sp.Fori(0, B - 1) as b:
                for g in range(NG):
                    group(b, g, False)
            for g in range(NG):
                group(B - 1, g, True)
            for h in range(2):
                sp.wait_ge(o_stored[h], 16 * (B * NG + 1))

        @block.gpsimd
        def _(pool):
            nc.gpsimd.memset(zeros[:, :], 0.0).then_inc(rows_ready, 1)
            pool.wait_ge(rows_ready, 1)
            for g in range(NG):
                nc.gpsimd.memset(ks[g][KROWS:MROWS, :, :], -1.0).then_inc(rows_ready, 1)
                pool.wait_ge(rows_ready, g + 2)

            def maximum_parts(b, g):
                pool.wait_ge(mx_found, before(b, g, 1) + 1)
                part = lambda i: mx3[:, :, :, i].rearrange("p q r -> p (q r)")
                nc.gpsimd.tensor_tensor(part(0), mx[:, :], zeros[:, :], ALU.add)
                pool.drain()
                nc.gpsimd.tensor_tensor(mxr[:, :], mx[:, :], part(0), ALU.subtract)
                pool.drain()
                nc.gpsimd.tensor_copy(part(1), mxr[:, :])
                pool.drain()
                nc.gpsimd.tensor_tensor(part(2), mxr[:, :], part(1), ALU.subtract).then_inc(mx_ready, 1)

            maximum_parts(0, 0)
            with pool.Fori(0, B - 1) as b:
                for g in range(NG):
                    maximum_parts(*following(b, g))
            for g in range(NG - 1):
                maximum_parts(B - 1, g + 1)

        @block.scalar
        def _(act):
            nc.scalar.preload_act_table(ACT.Exp)

            def exps(b, g, s, h, first=False):
                act.wait_ge(e_done, before(b, g, 2 * SLOTS) + (2 * s + h + 1))
                if not first:
                    act.wait_ge(pv_done, before(b, g, SLOTS) + (s - 1))
                nc.scalar.activation(pt[s % 2][h][:, :, :], psE[h][:, :, :], ACT.Exp,
                                     scale=HD ** -0.5).then_inc(p_ready, 1)

            def sums_out(b, g, h):
                act.wait_ge(pv_done, before(b, g, SLOTS) + (h + 1) * QT)
                nc.scalar.copy(osb[h][:, :], psO[:, :]).then_inc(o_ready, 1)

            def maxima_out(b, g, v):
                act.wait_ge(mxT_done, before(b, g, 2) + (v + 1))
                nc.scalar.copy(mxT[g % 2][:, v * HALF:(v + 1) * HALF], psX[0:GROUP * 3, :]).then_inc(mxT_ready, 1)

            def slots(b, g, which, first=False, last=False):
                for s in which:
                    if s == 1 and not first:
                        sums_out(*(b, g - 1) if g else (b - 1, NG - 1), 1)
                    if s == QT + 1:
                        sums_out(b, g, 0)
                    exps(b, g, s, 0, first and s < 2)
                    exps(b, g, s, 1, first and s < 2)
                    if s in MAX_T and not last:
                        maxima_out(*following(b, g), MAX_T.index(s))

            for v in range(2):
                maxima_out(0, 0, v)
            slots(0, 0, range(EARLY), first=True)
            with act.Fori(0, B - 1) as b:
                for g in range(NG):
                    slots(b, g, range(EARLY, SLOTS))
                    slots(*following(b, g), range(EARLY))
            for g in range(NG):
                slots(B - 1, g, range(EARLY, SLOTS), last=g == NG - 1)
                if g + 1 < NG:
                    slots(B - 1, g + 1, range(EARLY))
            sums_out(B - 1, NG - 1, 1)

        @block.vector
        def _(dve):
            nc.vector.memset(psO[:, :], 0.0).then_inc(psO_cleared, 1)
            dve.sem_inc(ot_ready, 1)

            def maxima(b, g, which):
                for v in which:
                    dve.wait_ge(sub_done, before(b, g, SUB) + (v + 1))
                    nc.vector.tensor_reduce(mxh[:, v // 8, v // 2 % GROUP, v % 2:v % 2 + 1], psS[v % 2][:, :], AX.X,
                                            ALU.max).then_inc(sub_used, 1)

            def group_maxima(b, g, first=False):
                dve.drain()
                if not first:
                    dve.wait_ge(mx_ready, before(b, g, 1))
                halves = mxh[:, :, :, :].rearrange("p q r h -> p (q r) h")
                nc.vector.tensor_tensor(mx[:, :], halves[:, :, 0], halves[:, :, 1], ALU.max).then_inc(mx_found, 1)

            def divide(b, g, h):
                dve.wait_ge(oT_done, before(b, g, 2) + (h + 1))
                view = psX[:, :].rearrange("p (t r c) -> p t r c", r=GROUP, c=32)
                nc.vector.reciprocal(rden[h][:, :, :], view[:, :, :, HD])
                dve.drain()
                dve.wait_ge(o_stored[h], before(b, g, 16) + 16)
                nc.vector.tensor_tensor(ot[h][:, :, :, :].rearrange("p t r c -> p (t r) c"),
                                        psX[:, :].rearrange("p (t c) -> p t c", c=32)[:, :, 0:HD],
                                        rden[h][:, :, :].rearrange("p t r -> p (t r)")[:, :, None]
                                        .to_broadcast([P, QT // 2 * GROUP, HD]), ALU.mult).then_inc(ot_ready, 1)

            def slots(b, g, which, first=False, last=False):
                for s in which:
                    nb, ng, which_max = taken_along(b, g, s)
                    if in_range(nb, ng):
                        maxima(nb, ng, which_max)
                        if s == SLOTS - LEAD - 1:
                            group_maxima(nb, ng)
                    if s == 3 and not first:
                        divide(*(b, g - 1) if g else (b - 1, NG - 1), 1)
                    if s == QT + 3:
                        divide(b, g, 0)

            maxima(0, 0, range(SUB))
            group_maxima(0, 0, True)
            maxima(0, 1, range(LEAD * SHARE))
            slots(0, 0, range(EARLY), first=True)
            with dve.Fori(0, B - 1) as b:
                for g in range(NG):
                    slots(b, g, range(EARLY, SLOTS))
                    slots(*following(b, g), range(EARLY))
            for g in range(NG):
                slots(B - 1, g, range(EARLY, SLOTS), last=g == NG - 1)
                if g + 1 < NG:
                    slots(B - 1, g + 1, range(EARLY), last=g + 1 == NG - 1)
            divide(B - 1, NG - 1, 1)

        @block.tensor
        def _(pe):
            def maxima(b, g, which, first=False):
                for v in which:
                    if not (first and v < 2):
                        pe.wait_ge(sub_used, before(b, g, SUB) + (v - 1))
                    nc.tensor.matmul(psS[v % 2][:, :], qs[g][0:KROWS, v // 2 % GROUP, v // 8 * P:(v // 8 + 1) * P],
                                     ks[g][0:KROWS, v // 2 % GROUP, v % 2 * HALF:(v % 2 + 1) * HALF],
                                     start=True, stop=True).then_inc(sub_done, 1)

            def scores(b, g, s, r, first=False):
                half, kt = divmod(s, QT)
                if r % 2 == 0 and not first:
                    pe.wait_ge(p_ready, before(b, g, 2 * SLOTS) + (2 * s + r // 2 - 1))
                product = nc.tensor.matmul(psE[r // 2][:, r % 2, :], ks[g][0:MROWS, r, kt * P:(kt + 1) * P],
                                           qs[g][0:MROWS, r, half * HALF:(half + 1) * HALF], start=True, stop=True)
                if r % 2 == 1:
                    product.then_inc(e_done, 1)

            def sums(b, g, s, c, first=False):
                half, kt = divmod(s, QT)
                if c == 0:
                    pe.wait_ge(p_ready, before(b, g, 2 * SLOTS) + (2 * s + 2))
                    if s == 0:
                        pe.wait_ge(v_loaded[g], b * 16 + 16)
                    if kt == 0 and not first:
                        pe.wait_ge(o_ready, before(b, g, 2) + half)
                cols = slice(c * HALF // 2, (c + 1) * HALF // 2)
                for r in range(GROUP):
                    last = nc.tensor.matmul(psO[32 * r:32 * r + VC, cols], va[g][:, kt, r * VC:(r + 1) * VC],
                                            pt[s % 2][r // 2][:, r % 2, cols], start=(kt == 0 and c == 0),
                                            stop=(kt == QT - 1 and c == 1), tile_position=(0, 32 * r),
                                            skip_group_check=True)
                if c == 1:
                    last.then_inc(pv_done, 1)

            def maxima_T(b, g, v, psX_free):
                pe.wait_ge(mx_ready, before(b, g, 1) + 1)
                if psX_free is not None:
                    pe.wait_ge(*psX_free)
                for q in range(QT // 2):
                    last = nc.tensor.matmul(psX[0:GROUP * 3, q * P:(q + 1) * P],
                                            mx3[:, v * (QT // 2) + q, :, :].rearrange("p r c -> p (r c)"),
                                            identb[:, :], start=True, stop=True)
                last.then_inc(mxT_done, 1)

            def sums_T(b, g, h, psX_free):
                pe.wait_ge(o_ready, before(b, g, 2) + (h + 1))
                pe.wait_ge(*psX_free)
                for q in range(QT // 2):
                    last = nc.tensor.transpose(psX[:, q * P:(q + 1) * P], osb[h][:, q * P:(q + 1) * P], ident[:, :])
                last.then_inc(oT_done, 1)

            def slots(b, g, which, first=False, last=False):
                nb, ng = following(b, g)
                pb, pg = (b, g - 1) if g else (b - 1, NG - 1)
                for s in which:
                    mb, mg, which_max = taken_along(b, g, s)
                    some = which_max if in_range(mb, mg) else ()
                    if s == 0:
                        pe.wait_ge(mx_rows[g], b * (16 * GROUP) + 16 * GROUP)
                    if s == SLOTS - LEAD and some:
                        pe.wait_ge(loaded[mg], mb * (16 * 12) + 16 * 12)
                    scores(b, g, s, 0, first and s == 0)
                    maxima(mb, mg, some[0:1])
                    if s >= 2:
                        sums(b, g, s - 2, 1)
                    elif not first:
                        sums(pb, pg, SLOTS - 2 + s, 1)
                    maxima(mb, mg, some[1:2])
                    for r in (1, 2):
                        scores(b, g, s, r, first and s == 0)
                    maxima(mb, mg, some[2:3])
                    if s >= 1:
                        sums(b, g, s - 1, 0, first and s == 1)
                    elif not first:
                        sums(pb, pg, SLOTS - 1, 0)
                    maxima(mb, mg, some[3:4])
                    scores(b, g, s, 3)
                    if s == 2 and not first:
                        sums_T(pb, pg, 1, (mxT_ready, before(b, g, 2) + 2))
                    if s == QT + 2:
                        sums_T(b, g, 0, (ot_ready, before(b, g, 2) + 1))
                    if s in MAX_T and not last:
                        v = MAX_T.index(s)
                        maxima_T(nb, ng, v, (mxT_ready, before(nb, ng, 2) + 1) if v else
                                 (ot_ready, before(b, g, 2) + 2))

            pe.wait_ge(loaded[0], 16 * 12)
            maxima(0, 0, range(SUB), first=True)
            maxima_T(0, 0, 0, None)
            maxima_T(0, 0, 1, (mxT_ready, 1))
            pe.wait_ge(loaded[1], 16 * 12)
            maxima(0, 1, range(LEAD * SHARE))
            pe.wait_ge(rows_ready, NG + 1)
            pe.wait_ge(psO_cleared, 1)
            slots(0, 0, range(EARLY), first=True)
            with pe.Fori(0, B - 1) as b:
                for g in range(NG):
                    slots(b, g, range(EARLY, SLOTS))
                    slots(*following(b, g), range(EARLY))
            for g in range(NG):
                slots(B - 1, g, range(EARLY, SLOTS), last=g == NG - 1)
                if g + 1 < NG:
                    slots(B - 1, g + 1, range(EARLY), last=g + 1 == NG - 1)
            sums(B - 1, NG - 1, SLOTS - 2, 1)
            for c in range(2):
                sums(B - 1, NG - 1, SLOTS - 1, c)
            sums_T(B - 1, NG - 1, 1, (ot_ready, before(B - 1, NG - 1, 2) + 2))


def out_projection_phase(nc, tag, X, stats, ident, wo, weights_loaded, o_d):
    ctx = ExitStack()
    sems = []
    ctx.callback(release, nc, sems)
    with ctx:
        sb = lambda n, s, d=F32: ctx.enter_context(nc.sbuf_tensor(f"{tag}_{n}", s, d))
        sem = lambda n: new_semaphore(nc, sems, f"{tag}_{n}")
        o = [sb(f"o{u}", [P, D]) for u in range(4)]
        oT = [sb(f"oT{u}", [P, KD, P]) for u in range(2)]
        psT = [ctx.enter_context(nc.psum_tensor(f"{tag}_psT{u}", [P, 512], F32)) for u in range(2)]
        psY = [ctx.enter_context(nc.psum_tensor(f"{tag}_psY{u}", [P, 512], F32)) for u in range(2)]
        o_loaded = [sem(f"o_loaded{u}") for u in range(4)]
        T_done = sem("T_done"); oT_ready = sem("oT_ready"); y_done = sem("y_done"); y_used = sem("y_used")
        block = ctx.enter_context(nc.Block())

        @block.sync
        def _(sp):
            rows = o_d.rearrange("b t p c -> (b t) p c")
            for u in range(4):
                sp.dma_start(o[u][:, :], rows[u]).then_inc(o_loaded[u], 16)
            with sp.Fori(1, NT // 4) as tt:
                for u in range(4):
                    sp.wait_ge(T_done, tt * 4 + (u - 3))
                    sp.dma_start(o[u][:, :], rows[tt * 4 + u]).then_inc(o_loaded[u], 16)

        @block.scalar
        def _(act):
            with act.Fori(0, NT // 2) as tt:
                for u in range(2):
                    act.wait_ge(T_done, tt * 2 + (u + 1))
                    nc.scalar.copy(oT[u][:, :, :].rearrange("p k t -> p (k t)"), psT[u][:, 0:D]).then_inc(oT_ready, 1)

        @block.vector
        def _(dve):
            with dve.Fori(0, NT // 4) as tt:
                for u in range(4):
                    t = tt * 4 + u
                    dve.wait_ge(y_done, t + 1)
                    nc.vector.tensor_tensor(X[:, t, :], X[:, t, :], psY[u % 2][:, 0:D], ALU.add).then_inc(y_used, 1)
                    dve.wait_ge(y_used, t + 1)
                    nc.vector.bn_stats(stats[:, t, :], X[:, t, :])

        @block.tensor
        def _(pe):
            def transposes(t, u, first=False):
                pe.wait_ge(o_loaded[u], (t - u) * 4 + 16)
                if not first:
                    pe.wait_ge(oT_ready, t - 1)
                for k in range(KD):
                    last = nc.tensor.transpose(psT[u % 2][:, k * P:(k + 1) * P], o[u][:, k * P:(k + 1) * P], ident[:, :])
                last.then_inc(T_done, 1)

            def product(t, u, first=False):
                pe.wait_ge(oT_ready, t + 1)
                if not first:
                    pe.wait_ge(y_used, t - 1)
                for k in range(KD):
                    last = nc.tensor.matmul(psY[u % 2][:, 0:D], oT[u % 2][:, k, :], wo[:, k, :],
                                            start=(k == 0), stop=(k == KD - 1))
                last.then_inc(y_done, 1)

            transposes(0, 0, True)
            pe.wait_ge(*weights_loaded)
            for t in range(3):
                transposes(t + 1, t + 1, t == 0)
                product(t, t, t < 2)
            with pe.Fori(0, NT // 4 - 1) as tt:
                for u in range(4):
                    t = tt * 4 + (3 + u)
                    transposes(t + 1, u)
                    product(t, (3 + u) % 4)
            product(NT - 1, 3)


def memory_moe_attention_moe_kernel(nc, x, m0T, w1T, w2T, rates_w, rates_b, gate_w, gate_b,
                                    gate_up, down_a, down_b, router, wqk, wv, wo, bqk, bv, bo, out):
    ctx = ExitStack()
    with ctx:
        def alloc(where, name, shape, dtype=F32):
            return where.enter_context(nc.sbuf_tensor(name, shape, dtype))

        X = alloc(ctx, "X", [P, NT, D])
        stats = alloc(ctx, "stats", [P, NT, 6])
        ident = alloc(ctx, "ident", [P, P]); identb = alloc(ctx, "identb", [P, P], BF16)
        ones = alloc(ctx, "ones", [P, P])
        W = {"gate_up": alloc(ctx, "W_gate_up", [P, KD, E + 1, 2 * I]), "router": alloc(ctx, "W_router", [P, KD, E + 1])}
        Wqk = alloc(ctx, "Wqk", [P, KD, 2 * D]); Wv = alloc(ctx, "Wv", [P, KD, D])
        Bqk = alloc(ctx, "Bqk", [P, 2 * KD]); Bv = alloc(ctx, "Bv", [P, D]); Bo = alloc(ctx, "Bo", [P, D])
        xn_d = nc.dram_tensor("normalised_rows", [TOKENS, D], F32).ap()
        ys = nc.dram_tensor("expert_rows", [ROWS_ALL + SLOTS_ALL, D], F32).ap()
        qk_d = nc.dram_tensor("query_key_parts", [2, 3, B, D, S], BF16).ap()
        v_d = nc.dram_tensor("values", [B, NG, P, QT, GROUP * VC], F32).ap()
        o_d = nc.dram_tensor("head_results", [B, QT, P, D], F32).ap()

        sem = lambda n: ctx.enter_context(nc.semaphore(n))
        x_loaded = [sem(f"x_loaded{q}") for q in range(4)]; memory_loaded = sem("memory_loaded"); moe_loaded = sem("moe_loaded"); down_loaded = sem("down_loaded")
        attention_loaded = sem("attention_loaded"); zero_ready = sem("zero_ready")
        ident_ready = sem("ident_ready"); stored = sem("stored"); wo_loaded = sem("wo_loaded")

        def load_down(sp, down, loaded):
            sp.dma_start(down[:, 0:I // P, :, :], down_a).then_inc(loaded, 16)
            sp.dma_start(down[0:I % P, I // P, :, :], down_b).then_inc(loaded, 16)

        first_half = ExitStack()
        with first_half:
            M0 = alloc(first_half, "M0", [P, KD, D])
            W1 = alloc(first_half, "W1", [P, KD, D]); W2 = alloc(first_half, "W2", [P, KD, D])
            Rw = alloc(first_half, "Rw", [P, KD, 2]); Rb = alloc(first_half, "Rb", [ROWS + 2, 1])
            Gw = alloc(first_half, "Gw", [P, KD]); Gb = alloc(first_half, "Gb", [P, 1])
            W["down"] = alloc(first_half, "W_down1", [P, KI, E + 1, D])

            with nc.Block() as block:
                @block.sync
                def _(sp):
                    for q, loaded in enumerate(x_loaded):
                        tiles = slice(q * NT // len(x_loaded), (q + 1) * NT // len(x_loaded))
                        sp.dma_start(X[:, tiles, :], x[:, tiles, :]).then_inc(loaded, 16)
                    for dst, src in ((M0, m0T), (W1, w1T), (W2, w2T), (Rw, rates_w)):
                        sp.dma_start(dst[:, :, :], src).then_inc(memory_loaded, 16)
                    sp.dma_start(Rb[ROWS:, :], rates_b).then_inc(memory_loaded, 16)
                    sp.dma_start(Gw[:, :], gate_w).then_inc(memory_loaded, 16)
                    sp.dma_start(Gb[:, :], gate_b.to_broadcast([P, 1])).then_inc(memory_loaded, 16)
                    sp.dma_start(W["router"][:, :, :], router).then_inc(moe_loaded, 16)
                    sp.dma_start(W["gate_up"][:, :, :, :], gate_up).then_inc(moe_loaded, 16)
                    sp.wait_ge(zero_ready, 1)
                    load_down(sp, W["down"], moe_loaded)
                    for dst, src in ((Wqk, wqk), (Wv, wv)):
                        sp.dma_start(dst[:, :, :], src).then_inc(attention_loaded, 16)
                    sp.dma_start(Bqk[:, :], bqk).then_inc(attention_loaded, 16)
                    sp.dma_start(Bv[:, :], bv.to_broadcast([P, D])).then_inc(attention_loaded, 16)
                    sp.dma_start(Bo[:, :], bo.to_broadcast([P, D])).then_inc(attention_loaded, 16)

                @block.vector
                def _(dve):
                    nc.vector.memset(W["down"][I % P:P, I // P, :, :], 0.0)
                    nc.vector.memset(ones[:, :], 1.0)
                    dve.drain().then_inc(zero_ready, 1)

                @block.gpsimd
                def _(pool):
                    nc.gpsimd.memset(ident[:, :], 0.0).then_inc(ident_ready, 1)
                    pool.wait_ge(ident_ready, 1)
                    nc.gpsimd.affine_select(out=ident[:, :], in_=ident[:, :], compare_op=ALU.not_equal, fill=1.0,
                                            base=0, pattern=[[-1, P]], channel_multiplier=1).then_inc(ident_ready, 1)
                    pool.wait_ge(ident_ready, 2)
                    nc.gpsimd.tensor_copy(identb[:, :], ident[:, :])

            memory_phase(nc, "mem", X, x_loaded, stats, ident, ones, M0, W1, W2, (memory_loaded, 16 * 7), Rw, Rb, Gw, Gb)
            ffn_phase(nc, "moe1", X, stats, ident, ones, W, (moe_loaded, 16 * 4), xn_d, ys)

        qkv_phase(nc, "qkv", X, stats, ident, Wqk, Wv, Bqk, Bv, Bo, (attention_loaded, 16 * 5), qk_d, v_d)
        scores_phase(nc, "scores", ident, identb, qk_d, v_d, o_d)

        second_half = ExitStack()
        with second_half:
            W["down"] = alloc(second_half, "W_down2", [P, KI, E + 1, D]); Wo = alloc(second_half, "Wo", [P, KD, D])
            with nc.Block() as block:
                @block.vector
                def _(dve):
                    nc.vector.memset(W["down"][I % P:P, I // P, :, :], 0.0)
                    dve.drain().then_inc(zero_ready, 1)

                @block.sync
                def _(sp):
                    sp.dma_start(Wo[:, :, :], wo).then_inc(wo_loaded, 16)
                    sp.wait_ge(zero_ready, 2)
                    load_down(sp, W["down"], down_loaded)
            out_projection_phase(nc, "out", X, stats, ident, Wo, (wo_loaded, 16), o_d)
            ffn_phase(nc, "moe2", X, stats, ident, ones, W, (down_loaded, 16 * 2), xn_d, ys, (out, stored))


def kernel(**inputs):
    import numpy as np
    import concourse.bacc as bacc
    from concourse.bass_utils import run_bass_kernel_spmd

    a = {name: np.asarray(v) for name, v in inputs.items()}
    mem = lambda n: a["L0_attn_a_" + n]
    att = lambda n: a["L0_attn_b_" + n]
    moe = lambda n: a["L0_ffn_" + n]
    tiles = lambda w: w.reshape(-1, P, w.shape[-1]).transpose(1, 0, 2)
    wqkv = att("Wqkv").reshape(HEADS, 3, HD, D)
    bqkv = att("bqkv").reshape(HEADS, 3, HD)
    experts = lambda n: np.concatenate([moe("w_" + n), moe("sw_" + n)[None]])
    gate_up = np.concatenate([experts("gate"), experts("up")], axis=2)
    down = experts("down")
    arrays = {
        "x": mem("x").reshape(NT, P, D).transpose(1, 0, 2),
        "m0T": tiles(mem("M_init").T), "w1T": tiles(mem("vg_w1").T), "w2T": tiles(mem("vg_w2").T),
        "rates_w": tiles(np.stack([mem("eta_w"), mem("alpha_w")], 1)),
        "rates_b": np.concatenate([mem("eta_b"), mem("alpha_b")]).reshape(2, 1),
        "gate_w": mem("gate_w").reshape(KD, P).T, "gate_b": mem("gate_b").reshape(1, 1),
        "gate_up": gate_up.reshape(E + 1, KD, P, 2 * I).transpose(2, 1, 0, 3),
        "down_a": down[:, :I // P * P].reshape(E + 1, I // P, P, D).transpose(2, 1, 0, 3),
        "down_b": down[:, I // P * P:].transpose(1, 0, 2),
        "router": tiles(np.concatenate([moe("gate_w"), moe("shared_gate_w")]).T),
        "wqk": tiles(wqkv[:, 0:2].transpose(3, 1, 0, 2).reshape(D, 2 * D)),
        "wv": tiles(wqkv[:, 2].transpose(2, 0, 1).reshape(D, D)), "wo": tiles(att("Wo").T),
        "bqk": bqkv[:, 0:2].transpose(1, 0, 2).reshape(2 * KD, P).T,
        "bv": bqkv[:, 2].reshape(1, D), "bo": att("bo").reshape(1, D),
    }
    nc = bacc.Bacc("TRN2", target_bir_lowering=False, num_devices=1)
    feeds, args = {}, []
    for name, v in arrays.items():
        v = np.ascontiguousarray(v)
        feeds[f"in_{name}_dram"] = v
        args.append(nc.dram_tensor(f"in_{name}_dram", v.shape, mybir.dt.from_np(v.dtype), kind="ExternalInput").ap())
    args.append(nc.dram_tensor("out_0_dram", (P, NT, D), F32, kind="ExternalOutput").ap())
    memory_moe_attention_moe_kernel(nc, *args)
    r = run_bass_kernel_spmd(nc, [feeds], core_ids=[0])
    return r.results[0]["out_0_dram"].transpose(1, 0, 2).reshape(B, S, D)
```

```python
import concourse.bass as bass
from concourse import mybir
from contextlib import ExitStack

F32 = mybir.dt.float32
I32 = mybir.dt.int32
U32 = mybir.dt.uint32
BF16 = mybir.dt.bfloat16
ALU = mybir.AluOpType
ACT = mybir.ActivationFunctionType
AX = mybir.AxisListType

P = 128
B, S, D = 4, 1024, 256
TOKENS = B * S
NT = TOKENS // P
KD = D // P
E, TOPK, I = 8, 2, 352
SHARED = E
IP = -(-I // P) * P
KI = IP // P
NB = (TOKENS * TOPK) // P + E
SLOTS_ALL = NB * P
ROWS_ALL = TOPK * TOKENS
SRC = 6
AHEAD = 4
NA = 16
PIECE = 8
NS = NT + NB
EPS = 1e-5


def new_semaphore(nc, sems, name):
    sems.append(nc.alloc_semaphore(name))
    return sems[-1]


def release(nc, sems):
    nc.clear_and_free_semaphores(sems)
    nc.all_engine_barrier()


def ffn_phase(nc, tag, X, stats, ident, ones, work, W, weights_loaded, xn_d, ys, store=None):
    ctx = ExitStack()
    sems = []
    ctx.callback(release, nc, sems)
    with ctx:
        sb = lambda n, s, d=F32: ctx.enter_context(nc.sbuf_tensor(f"{tag}_{n}", s, d))
        sem = lambda n: new_semaphore(nc, sems, f"{tag}_{n}")
        GS = 4
        got = work[:, 0:GS * TOPK, :].rearrange("p (s k) d -> p s k d", k=TOPK)
        rows = iter(range(GS * TOPK, NT))
        row = lambda: work[:, next(rows), :]
        src = [row() for u in range(SRC)]
        srcT = [row().rearrange("p (k t) -> p k t", k=KD) for u in range(2)]
        silu = [sb(f"silu{u}", [P, I]) for u in range(2)]
        hid = [sb(f"hid{u}", [P, IP]) for u in range(2)]
        hidT = [sb(f"hidT{u}", [P, KI, P]) for u in range(2)]
        yb = [row() for u in range(2)]
        mv = sb("mv", [P, NT, 2])
        rstd = sb("rstd", [P, NT])
        eps = sb("eps", [P, 1])
        lg = sb("lg", [P, NT, E + 1])
        iota8 = sb("iota8", [P, E])
        upper = sb("upper", [P, P])
        iotab = sb("iotab", [1, NB])
        one256 = sb("one256", [P, NT * E])
        choices = lambda: row().rearrange("p (t e) -> p t e", e=E)
        eq = choices()
        pk = [choices() for k in range(TOPK)]
        mx = [sb(f"mx{k}", [P, NT]) for k in range(TOPK)]
        ix = sb("ix", [P, NT])
        lg2 = choices()
        gap = sb("gap", [P, NT])
        cw = [sb(f"cw{k}", [P, NT]) for k in range(TOPK)]
        sg = sb("sg", [P, NT])
        both = choices()
        tot = sb("tot", [P, E, NT])
        cum = sb("cum", [P, E, NT])
        exc = sb("exc", [P, E, NT])
        slot = sb("slot", [P, E, NT])
        cnt = sb("cnt", [P, E])
        cnti = sb("cnti", [P, E], I32)
        nblk = sb("nblk", [P, E])
        bend = sb("bend", [P, E])
        base = sb("base", [P, E])
        CH = TOPK * NT
        pos = sb("pos", [P, CH], I32); part_i = sb("part_i", [P, CH], I32)
        pos_p = sb("pos_p", [P, CH], BF16); pos_j = sb("pos_j", [P, CH], BF16)
        posf = sb("posf", [P, CH])
        iota_p = sb("iota_p", [P, P], BF16); iota_j = sb("iota_j", [P, NB], BF16)
        tile1 = sb("tile1", [P, CH], BF16)
        lane = sb("lane", [P, 1])
        dump = sb("dump", [P, NB])
        hot_p = [sb(f"hot_p{u}", [P, PIECE, P], BF16) for u in range(2)]
        hot_j = sb("hot_j", [P, PIECE, NB], BF16)
        hot_id = [sb(f"hot_id{u}", [P, PIECE, 2, NB], BF16) for u in range(2)]
        place = sb("place", [P, NB]); empty = sb("empty", [P, NB])
        slots_i = sb("slots_i", [P, NB, 2], I32)
        now_i = [sb(f"now_i{u}", [P, 2], I32) for u in range(SRC)]
        ble = sb("ble", [1, NB, E])
        bex = sb("bex", [1, NB])
        bexi = sb("bexi", [1, NB], I32)

        ps = [ctx.enter_context(nc.psum_tensor(f"{tag}_ps{i}", [P, 512], F32)) for i in range(8)]
        psT, psH, psG, psU, psD = ps[0], ps[1], ps[2:4], ps[4:6], ps[6]
        psL = ps[2]
        psR = (ps[7][:, 0:NT * E], ps[7][:, NT * E:2 * NT * E])
        psI = ps[7][:, 0:2 * NB]

        consts_done = sem("consts_done"); ones_set = sem("ones_set")
        var_done = sem("var_done"); std_done = sem("std_done"); rstd_ready = sem("rstd_ready")
        l_src = sem("l_src"); l_T = sem("l_T"); l_srcT = sem("l_srcT"); l_lg = sem("l_lg"); lg_ready = sem("lg_ready")
        sg_done = sem("sg_done"); chosen = sem("chosen"); rank_done = sem("rank_done"); cw_done = sem("cw_done")
        bex_done = sem("bex_done"); slots_ready = sem("slots_ready"); inv_ready = sem("inv_ready"); inv_done = sem("inv_done")
        xn_stored = [sem(f"xn_stored{u}") for u in range(AHEAD)]
        due = sem("due")
        src_ready = sem("src_ready")
        src_loaded = [sem(f"src_loaded{u}") for u in range(SRC)]
        T_done = sem("T_done"); srcT_ready = sem("srcT_ready")
        g_done = sem("g_done"); u_done = sem("u_done"); silu_done = sem("silu_done")
        hid_ready = sem("hid_ready"); hT_done = sem("hT_done"); hidT_ready = sem("hidT_ready")
        d_done = sem("d_done"); d_used = sem("d_used")
        y_ready = sem("y_ready")
        y_sent = [sem(f"y_sent{u}") for u in range(SRC)]
        got_loaded = [sem(f"got_loaded{s}") for s in range(GS)]
        got_used = sem("got_used")

        LAST = NA + NB
        kind = lambda n: "shared" if n < NA else "routed" if n < LAST else "late"
        UNROLL = {"shared": 2, "routed": SRC, "late": 2}
        runs = []
        n = 0
        while n < NS:
            k, width = kind(n), UNROLL[kind(n)]
            like = n
            while NA <= n and like + 2 < NS and kind(n - 3) == kind(like + 2) == k:
                like += 1
            times = (like - n) // width
            runs.append((n, times, k))
            n += max(times * width, 1)
        tile = lambda n, k: n if k == "shared" else n - NB
        buffer = lambda n0, u, k: (n0 - NA + u) % SRC if k == "routed" else (n0 + u) % 2

        FOUND = 4 + CH // PIECE + 1
        EARLY = min(NT, 2 * (NT - NA - 2)) // GS * GS

        block = ctx.enter_context(nc.Block())

        @block.sync
        def _(sp):
            results = ys[0:ROWS_ALL, :].rearrange("(k t p) d -> t p k d", k=TOPK, p=P)
            with sp.Fori(0, NT // AHEAD) as tt:
                for u in range(AHEAD):
                    sp.wait_ge(l_src, tt * AHEAD + (u + 1))
                    sp.dma_start(xn_d.rearrange("(t p) d -> t p d", p=P)[tt * AHEAD + u], src[u][:, :]
                                 ).then_inc(xn_stored[u], 16)
            for u in range(SRC):
                sp.wait_ge(y_sent[u], 16 * (NB // SRC))
            for t in range(GS):
                sp.dma_start(got[:, t, :, :], results[t]).then_inc(got_loaded[t], 16)
            with sp.Fori(1, NT // GS) as tt:
                for s in range(GS):
                    sp.wait_ge(got_used, tt * GS + (s - GS + 1))
                    sp.dma_start(got[:, s, :, :], results[tt * GS + s]).then_inc(got_loaded[s], 16)
            if store is not None:
                sp.wait_ge(store[1], 16 * NT // GS)

        @block.gpsimd
        def _(pool):
            nc.gpsimd.iota(iota8[:, :], [[1, E]], base=-E, channel_multiplier=0,
                           allow_small_or_imprecise_dtypes=True)
            nc.gpsimd.iota(iotab[:, :], [[1, NB]], base=0, channel_multiplier=0,
                           allow_small_or_imprecise_dtypes=True)
            nc.gpsimd.memset(one256[:, :], 1.0)
            nc.gpsimd.memset(upper[:, :], 1.0).then_inc(ones_set, 1)
            pool.wait_ge(ones_set, 1)
            nc.gpsimd.affine_select(out=upper[:, :], in_=upper[:, :], compare_op=ALU.is_gt, fill=0.0,
                                    base=0, pattern=[[1, P]], channel_multiplier=-1).then_inc(consts_done, 1)
            nc.gpsimd.iota(iota_p[:, :], [[1, P]], base=0, channel_multiplier=0, allow_small_or_imprecise_dtypes=True)
            nc.gpsimd.iota(iota_j[:, :], [[1, NB]], base=0, channel_multiplier=0, allow_small_or_imprecise_dtypes=True)
            nc.gpsimd.iota(tile1[:, :], [[1, CH]], base=1, channel_multiplier=0, allow_small_or_imprecise_dtypes=True)
            nc.gpsimd.iota(lane[:, :], [[1, 1]], base=0, channel_multiplier=1, allow_small_or_imprecise_dtypes=True)
            nc.gpsimd.iota(dump[:, :], [[P, NB]], base=ROWS_ALL + P, channel_multiplier=1,
                           allow_small_or_imprecise_dtypes=True).then_inc(consts_done, 1)

            def fetch(j, u, free=None):
                if free is not None:
                    pool.wait_ge(y_sent[u], free)
                    pool.sem_inc(due, 1)
                nc.gpsimd.tensor_copy(now_i[u][:, :], slots_i[:, j, :])
                pool.drain()
                nc.gpsimd.indirect_dma_start(
                    out=src[u][:, :], out_offset=None, in_=xn_d,
                    in_offset=bass.IndirectOffsetOnAxis(ap=now_i[u][:, 0:1].bitcast(U32), axis=0)
                ).then_inc(src_loaded[u], 16)

            def send(j, u):
                pool.wait_ge(y_ready, j + 1)
                pool.sem_inc(due, 1)
                nc.gpsimd.indirect_dma_start(
                    out=ys, out_offset=bass.IndirectOffsetOnAxis(ap=now_i[u][:, 1:2].bitcast(U32), axis=0),
                    in_=yb[u % 2][:, :], in_offset=None).then_inc(y_sent[u], 16)

            pool.wait_ge(slots_ready, 1)
            for u in range(AHEAD):
                pool.wait_ge(xn_stored[u], 16 * (NT // AHEAD))
            for j in range(AHEAD):
                if j < 2:
                    pool.wait_ge(T_done, NA - 1 + j)
                fetch(j, j)
            for j in range(SRC):
                fetch(j + AHEAD, (j + AHEAD) % SRC, 16 if j + AHEAD >= SRC else None)
                send(j, j)
            with pool.Fori(1, NB // SRC - 1) as jj:
                for u in range(SRC):
                    fetch(jj * SRC + (u + AHEAD), (u + AHEAD) % SRC, jj * 16 + (16 if u + AHEAD >= SRC else 0))
                    send(jj * SRC + u, u)
            for j in range(NB - SRC, NB):
                if j + AHEAD < NB:
                    fetch(j + AHEAD, (j + AHEAD) % SRC, (j + AHEAD) // SRC * 16)
                send(j, j % SRC)
            if store is not None:
                out_pt, stored = store
                for t in range(0, NT, GS):
                    pool.wait_ge(got_used, t + GS)
                    pool.dma_start(out_pt[:, t:t + GS, :], X[:, t:t + GS, :]).then_inc(stored, 16)

        @block.scalar
        def _(act):
            nc.scalar.preload_act_table(ACT.Sqrt)
            act.wait_ge(var_done, 1)
            nc.scalar.activation(rstd[:, :], mv[:, :, 1], ACT.Sqrt, bias=eps[:, :]).then_inc(std_done, 1)
            nc.scalar.preload_act_table(ACT.Sigmoid)
            with act.Fori(0, NT // 2) as tt:
                for u in range(2):
                    act.wait_ge(l_T, tt * 2 + (u + 1))
                    nc.scalar.copy(srcT[u][:, :, :].rearrange("p k t -> p (k t)"), ps[u][:, 0:D]).then_inc(l_srcT, 1)
            act.wait_ge(lg_ready, 1)
            nc.scalar.activation(sg[:, :], lg[:, :, E], ACT.Sigmoid).then_inc(sg_done, 1)
            nc.scalar.preload_act_table(ACT.Silu)

            def source_out(n, u):
                act.wait_ge(T_done, n + 1)
                nc.scalar.copy(srcT[u][:, :, :].rearrange("p k t -> p (k t)"), psT[:, 0:D]).then_inc(srcT_ready, 1)

            def silu_step(n, u):
                act.wait_ge(g_done, n + 1)
                nc.scalar.activation(silu[u][:, :], psG[u][:, 0:I], ACT.Silu).then_inc(silu_done, 1)

            def y_out(n, s, sent=None):
                act.wait_ge(d_done, n + 1)
                if sent is not None:
                    act.wait_ge(y_sent[(s - 2) % SRC], sent)
                nc.scalar.copy(yb[s % 2][:, :], psD[:, 0:D]).then_inc(y_ready, 1)

            def choice_weights():
                act.wait_ge(chosen, 2)
                nc.scalar.activation(cw[0][:, :], gap[:, :], ACT.Sigmoid)
                nc.scalar.activation(cw[1][:, :], gap[:, :], ACT.Sigmoid, scale=-1.0).then_inc(cw_done, 1)
                nc.scalar.preload_act_table(ACT.Silu)

            def step(n, n0, u, k, i=0):
                silu_step(n, (n0 + u) % 2)
                if n0 + u + 1 < NS:
                    source_out(n + 1, (n0 + u + 1) % 2)
                before = n0 + u - 1
                if NA <= before and (k == "routed" or before < LAST):
                    j = before - NA
                    y_out(n - 1, j % SRC, None if j < 2 else i * 16 + ((j - 2) // SRC + 1) * 16)

            source_out(0, 0)
            for n0, times, k in runs:
                if n0 == NA - 2:
                    choice_weights()
                if times:
                    with act.Fori(0, times) as i:
                        for u in range(UNROLL[k]):
                            step(i * UNROLL[k] + (n0 + u), n0, u, k, i)
                else:
                    step(n0, n0, 0, k)

        @block.vector
        def _(dve):
            nc.vector.memset(eps[:, :], EPS)
            for u in range(2):
                nc.vector.memset(hid[u][:, I:IP], 0.0)
            for t in range(NT):
                nc.vector.bn_aggr(mv[:, t, :], stats[:, t, :])
            dve.drain().then_inc(var_done, 1)
            dve.wait_ge(std_done, 1)
            nc.vector.reciprocal(rstd[:, :], rstd[:, :])
            dve.drain().then_inc(rstd_ready, 1)

            def normalise(u, t):
                return nc.vector.tensor_scalar(src[u][:, 0:D], X[:, t, :], mv[:, t, 0:1], rstd[:, bass.ds(t, 1)],
                                               ALU.subtract, ALU.mult)

            for t in range(AHEAD):
                normalise(t, t).then_inc(l_src, 1)
            with dve.Fori(1, NT // AHEAD) as tt:
                for u in range(AHEAD):
                    dve.wait_ge(l_T, tt * AHEAD + (u + 1 - AHEAD))
                    dve.wait_ge(xn_stored[u], tt * 16)
                    normalise(u, tt * AHEAD + u).then_inc(l_src, 1)
            dve.wait_ge(l_lg, 1)
            nc.vector.tensor_copy(lg[:, :, :].rearrange("p t e -> p (t e)"), psL[:, 0:NT * (E + 1)])
            dve.drain().then_inc(lg_ready, 1)

            def choose(k):
                over_e = lambda v: v[:, :, None].to_broadcast([P, NT, E])
                index = iota8[:, None, :].to_broadcast([P, NT, E])
                at = lg[:, :, 0:E] if k == 0 else lg2[:, :, :]
                nc.vector.tensor_reduce(mx[k][:, :], at, AX.X, ALU.max)
                dve.drain()
                nc.vector.tensor_tensor(eq[:, :, :], at, over_e(mx[k]), ALU.is_equal)
                dve.drain()
                nc.vector.tensor_tensor(eq[:, :, :], eq[:, :, :], index, ALU.mult)
                dve.drain()
                nc.vector.tensor_reduce(ix[:, :], eq[:, :, :], AX.X, ALU.min)
                dve.drain()
                nc.vector.tensor_tensor(pk[k][:, :, :], index, over_e(ix), ALU.is_equal)
                dve.drain()
                if k == 0:
                    nc.vector.scalar_tensor_tensor(lg2[:, :, :], pk[0][:, :, :], -3.0e38, lg[:, :, 0:E],
                                                   ALU.mult, ALU.add)
                    dve.drain().then_inc(chosen, 1)
                else:
                    nc.vector.tensor_tensor(both[:, :, :], pk[0][:, :, :], pk[1][:, :, :], ALU.add)
                    nc.vector.tensor_tensor(gap[:, :], mx[0][:, :], mx[1][:, :], ALU.subtract)
                    dve.drain().then_inc(chosen, 1)

            by_e = lambda ap: ap.rearrange("p (t e) -> p e t", e=E)

            def counts():
                dve.wait_ge(rank_done, 1)
                flat = lambda v: v[:, :, :].rearrange("p e t -> p (e t)")
                nc.vector.tensor_copy(tot[:, :, :], by_e(psR[1]))
                dve.drain()
                nc.vector.tensor_tensor_scan(flat(cum), one256[:, :], flat(tot), 0.0, ALU.mult, ALU.add)
                dve.drain()
                nc.vector.tensor_tensor(exc[:, :, :], cum[:, :, :], tot[:, :, :], ALU.subtract)
                dve.drain()
                nc.vector.tensor_tensor(cnt[:, :], cum[:, :, NT - 1], exc[:, :, 0], ALU.subtract)
                dve.drain()
                nc.vector.tensor_scalar(cnti[:, :], cnt[:, :], float(P - 1), None, ALU.add)
                dve.drain()
                nc.vector.tensor_scalar(cnti[:, :], cnti[:, :], P.bit_length() - 1, None, ALU.arith_shift_right)
                dve.drain()
                nc.vector.tensor_copy(nblk[:, :], cnti[:, :])
                dve.drain()
                nc.vector.tensor_tensor_scan(bend[:, :], one256[:, 0:E], nblk[:, :], 0.0, ALU.mult, ALU.add)
                dve.drain()
                nc.vector.tensor_tensor(base[:, :], bend[:, :], nblk[:, :], ALU.subtract)
                dve.drain()
                nc.vector.scalar_tensor_tensor(base[:, :], base[:, :], float(P), exc[:, :, 0], ALU.mult, ALU.subtract)
                dve.drain()

            def positions():
                nc.vector.tensor_tensor(slot[:, :, :], exc[:, :, :],
                                        base[:, :, None].to_broadcast([P, E, NT]), ALU.add)
                dve.drain()
                nc.vector.tensor_tensor(slot[:, :, :], slot[:, :, :], by_e(psR[0]), ALU.add)
                dve.drain()
                for k in range(TOPK):
                    nc.vector.tensor_tensor(eq[:, :, :], pk[k][:, :, :], slot[:, :, :].rearrange("p e t -> p t e"), ALU.mult)
                    dve.drain()
                    nc.vector.tensor_reduce(posf[:, k * NT:(k + 1) * NT], eq[:, :, :], AX.X, ALU.add)
                    dve.drain()
                nc.vector.tensor_copy(pos[:, :], posf[:, :])
                dve.drain()
                nc.vector.tensor_scalar(part_i[:, :], pos[:, :], P - 1, None, ALU.bitwise_and)
                nc.vector.tensor_scalar(pos[:, :], pos[:, :], P.bit_length() - 1, None, ALU.arith_shift_right)
                dve.drain()
                nc.vector.tensor_copy(pos_p[:, :], part_i[:, :])
                nc.vector.tensor_copy(pos_j[:, :], pos[:, :])
                dve.drain()

            def one_hots(i):
                c = slice(i * PIECE, (i + 1) * PIECE)
                over = lambda v, n: v[:, c, None].to_broadcast([P, PIECE, n])
                if i >= 2:
                    dve.wait_ge(inv_done, i - 1)
                nc.vector.tensor_tensor(hot_j[:, :, :], iota_j[:, None, :].to_broadcast([P, PIECE, NB]),
                                        over(pos_j, NB), ALU.is_equal)
                nc.vector.tensor_tensor(hot_p[i % 2][:, :, :], iota_p[:, None, :].to_broadcast([P, PIECE, P]),
                                        over(pos_p, P), ALU.is_equal)
                dve.drain()
                nc.vector.tensor_tensor(hot_id[i % 2][:, :, 0, :], hot_j[:, :, :], over(tile1, NB), ALU.mult)
                nc.vector.tensor_scalar(hot_id[i % 2][:, :, 1, :], hot_j[:, :, :], lane[:, :], None, ALU.mult)
                dve.drain().then_inc(inv_ready, 1)

            def slots():
                dve.wait_ge(inv_done, CH // PIECE)
                of_tile, of_lane = psI[:, 0:NB], psI[:, NB:2 * NB]
                nc.vector.tensor_scalar(empty[:, :], of_tile, 0.0, None, ALU.is_equal)
                nc.vector.tensor_scalar(place[:, :], of_tile, float(P), None, ALU.mult)
                dve.drain()
                nc.vector.tensor_tensor(empty[:, :], empty[:, :], dump[:, :], ALU.mult)
                nc.vector.tensor_tensor(place[:, :], place[:, :], of_lane, ALU.add)
                dve.drain()
                nc.vector.tensor_tensor(place[:, :], place[:, :], empty[:, :], ALU.add)
                dve.drain()
                nc.vector.tensor_scalar(slots_i[:, :, 1], place[:, :], -float(P), None, ALU.add)
                dve.drain()
                nc.vector.tensor_scalar(slots_i[:, :, 0], slots_i[:, :, 1], TOKENS - 1, None,
                                        ALU.bitwise_and).then_inc(slots_ready, 1)

            def block_experts():
                nc.vector.tensor_tensor(ble[:, :, :], bend[0:1, None, :].to_broadcast([1, NB, E]),
                                        iotab[:, :, None].to_broadcast([1, NB, E]), ALU.is_le)
                dve.drain()
                nc.vector.tensor_reduce(bex[:, :], ble[:, :, :], AX.X, ALU.add)
                dve.drain()
                nc.vector.tensor_scalar(bexi[:, :], bex[:, :], float(E - 1), None, ALU.min).then_inc(bex_done, 1)

            def hidden(n, u):
                dve.wait_ge(u_done, n + 1)
                dve.wait_ge(silu_done, n + 1)
                nc.vector.tensor_tensor(hid[u][:, 0:I], silu[u][:, :], psU[u][:, 0:I], ALU.mult).then_inc(hid_ready, 1)

            def hidden_out(n, u):
                dve.wait_ge(hT_done, n + 1)
                nc.vector.tensor_copy(hidT[u][:, :, :].rearrange("p k t -> p (k t)"), psH[:, 0:IP]).then_inc(hidT_ready, 1)

            def add_shared(n, u, t):
                dve.wait_ge(d_done, n + 1)
                nc.vector.scalar_tensor_tensor(X[:, t, :], psD[:, 0:D], sg[:, bass.ds(t, 1)], X[:, t, :],
                                               ALU.mult, ALU.add).then_inc(d_used, 1)

            def source(n, u, t, sent):
                if sent:
                    dve.wait_ge(y_sent[u], 16 * (NB // SRC))
                else:
                    dve.wait_ge(T_done, n - 1)
                normalise(u, t).then_inc(src_ready, 1)

            def combine(t, s, count):
                for k in range(TOPK):
                    for i in range(2):
                        if k == 0:
                            dve.wait_ge(got_loaded[s + i], count)
                        last = nc.vector.scalar_tensor_tensor(X[:, t + i, :], got[:, s + i, k, :],
                                                              cw[k][:, bass.ds(t + i, 1)], X[:, t + i, :],
                                                              ALU.mult, ALU.add)
                        if k == 1:
                            last.then_inc(got_used, 1)
                    dve.drain()
                if store is None:
                    for i in range(2):
                        nc.vector.bn_stats(stats[:, t + i, :], X[:, t + i, :])

            def step(n, n0, u, k, between=None):
                ahead, here = n0 + u + 2, n0 + u
                if ahead < NS and kind(ahead) != "routed":
                    source(n + 2, here % 2, tile(n + 2, kind(ahead)), LAST <= ahead < LAST + 2)
                hidden_out(n, here % 2)
                if here + 1 < NS:
                    hidden(n + 1, (here + 1) % 2)
                if between is not None:
                    between()
                if k != "routed":
                    add_shared(n, here % 2, tile(n, k))

            for u in range(AHEAD):
                dve.wait_ge(xn_stored[u], 16 * (NT // AHEAD))
            normalise(0, 0).then_inc(src_ready, 1)
            normalise(1, 1).then_inc(src_ready, 1)
            dve.wait_ge(consts_done, 2)
            hidden(0, 0)
            finding = {0: lambda: choose(0), 1: lambda: choose(1), 2: counts, 3: positions,
                       FOUND - 1: block_experts, FOUND: slots}
            for n in range(NA):
                step(n, n, 0, "shared", finding.get(n, (lambda: one_hots(n - 4)) if 0 <= n - 4 < CH // PIECE else None))
            with dve.Fori(0, (NB - 6) // 2) as i:
                for u in range(2):
                    step(i * 2 + (NA + u), NA, u, "routed")
            for n in range(LAST - 6, LAST):
                step(n, n, 0, "routed")
            dve.wait_ge(cw_done, 1)
            for n in range(LAST, NS):
                t = 2 * (n - LAST - 2)
                step(n, n, 0, "late", (lambda: combine(t, t % GS, 16 * (t // GS + 1))) if 0 <= t < EARLY else None)
            with dve.Fori(EARLY // GS, NT // GS) as tt:
                for s in range(0, GS, 2):
                    combine(tt * GS + s, s, tt * 16 + 16)

        @block.tensor
        def _(pe):
            def transpose_rows(bank, u):
                for k in range(KD):
                    last = nc.tensor.transpose(bank[:, k * P:(k + 1) * P], src[u][:, k * P:(k + 1) * P], ident[:, :])
                return last

            def logits_in(t, b, first=False):
                pe.wait_ge(l_src, t + 1)
                if not first:
                    pe.wait_ge(l_srcT, t - 1)
                transpose_rows(ps[b % 2], b).then_inc(l_T, 1)

            def logits(t, u):
                pe.wait_ge(l_srcT, t + 1)
                for k in range(KD):
                    nc.tensor.matmul(psL[:, bass.ds(t * (E + 1), E + 1)], srcT[u][:, k, :],
                                     W["router"][:, k, :], start=(k == 0), stop=(k == KD - 1))

            pe.wait_ge(weights_loaded[0], weights_loaded[1])
            logits_in(0, 0, True)
            logits_in(1, 1, True)
            with pe.Fori(0, NT // AHEAD - 1) as tt:
                for u in range(AHEAD):
                    logits(tt * AHEAD + u, u % 2)
                    logits_in(tt * AHEAD + (u + 2), (u + 2) % AHEAD)
            for t in range(NT - AHEAD, NT):
                logits(t, t % 2)
                if t + 2 < NT:
                    logits_in(t + 2, (t + 2) % AHEAD)
            pe.drain().then_inc(l_lg, 1)

            def ranks():
                pe.wait_ge(chosen, 2)
                flat = both[:, :, :].rearrange("p t e -> p (t e)")
                nc.tensor.matmul(psR[0], upper[:, :], flat, start=True, stop=True)
                nc.tensor.matmul(psR[1], ones[:, :], flat, start=True, stop=True).then_inc(rank_done, 1)

            def inverse(i):
                pe.wait_ge(inv_ready, i + 1)
                for c in range(PIECE):
                    last = nc.tensor.matmul(psI, hot_p[i % 2][:, c, :], hot_id[i % 2][:, c, :, :].rearrange("p a j -> p (a j)"),
                                            start=(i == 0 and c == 0), stop=(i == CH // PIECE - 1 and c == PIECE - 1))
                last.then_inc(inv_done, 1)

            def rows_in(n, b, k, loaded):
                if k == "routed":
                    pe.wait_ge(src_loaded[b], loaded)
                else:
                    pe.wait_ge(src_ready, tile(n, k) + 1)
                if not (isinstance(n, int) and n == 0):
                    pe.wait_ge(srcT_ready, n)
                transpose_rows(psT, b).then_inc(T_done, 1)

            def gate_up(n, u, e):
                pe.wait_ge(srcT_ready, n + 1)
                if isinstance(n, int) and n < 2:
                    pe.wait_ge(lg_ready, 1)
                else:
                    pe.wait_ge(hid_ready, n - 1)
                for half, (bank, done) in enumerate(((psG, g_done), (psU, u_done))):
                    for k in range(KD):
                        last = nc.tensor.matmul(bank[u][:, 0:I], srcT[u][:, k, :],
                                                W["gate_up"][:, k, e, half * I:(half + 1) * I],
                                                start=(k == 0), stop=(k == KD - 1))
                    last.then_inc(done, 1)

            def hidden_T(n, u):
                pe.wait_ge(hid_ready, n + 1)
                if not (isinstance(n, int) and n == 0):
                    pe.wait_ge(hidT_ready, n)
                for k in range(KI):
                    last = nc.tensor.transpose(psH[:, k * P:(k + 1) * P], hid[u][:, k * P:(k + 1) * P], ident[:, :])
                last.then_inc(hT_done, 1)

            def down(n, u, e, before):
                pe.wait_ge(hidT_ready, n + 1)
                if before == "shared":
                    pe.wait_ge(d_used, n)
                elif before == "routed":
                    pe.wait_ge(y_ready, n - NA)
                elif before == "late":
                    pe.wait_ge(d_used, n - NB)
                for k in range(KI):
                    last = nc.tensor.matmul(psD[:, 0:D], hidT[u][:, k, :], W["down"][:, k, e, :],
                                            start=(k == 0), stop=(k == KI - 1))
                last.then_inc(d_done, 1)

            def expert(n, k):
                if k != "routed":
                    return SHARED
                return pe.value_load(bexi[0:1, bass.ds(n - NA, 1)], min_val=0, max_val=E - 1)

            def step(n, n0, u, k, i=0):
                here = n0 + u
                if here:
                    hidden_T(n - 1, (here - 1) % 2)
                gate_up(n, here % 2, expert(n, k))
                if here + 1 < NS:
                    nk = kind(here + 1)
                    loaded = None
                    if nk == "routed":
                        j = here + 1 - NA
                        loaded = i * 16 + (j // SRC + 1) * 16
                    rows_in(n + 1, buffer(here + 1, 0, nk), nk, loaded)
                if 6 <= here < 6 + CH // PIECE:
                    inverse(here - 6)
                if here == 3:
                    ranks()
                if here:
                    down(n - 1, (here - 1) % 2, expert(n - 1, kind(here - 1)), kind(here - 2) if here >= 2 else None)

            rows_in(0, 0, "shared", None)
            for n0, times, k in runs:
                if n0 == NA:
                    pe.wait_ge(bex_done, 1)
                if times:
                    with pe.Fori(0, times) as i:
                        for u in range(UNROLL[k]):
                            step(i * UNROLL[k] + (n0 + u), n0, u, k, i)
                else:
                    step(n0, n0, 0, k)
            hidden_T(NS - 1, (NS - 1) % 2)
            down(NS - 1, (NS - 1) % 2, SHARED, "late")


CHUNK = 64
NC = S // CHUNK
HALVES = P // CHUNK
XC = CHUNK + 2
ROWS = NC * B
MAX_LR, MIN_DECAY, MAX_NORM, NORM_EPS = 0.2, 0.5, 30.0, 1e-5


def memory_phase(nc, tag, X, x_loaded, stats, ident, ones, work, m0T, w1T, w2T, weights_loaded, rates_w, rates_b, gate_w, gate_b):
    ctx = ExitStack()
    sems = []
    ctx.callback(release, nc, sems)
    with ctx:
        sb = lambda n, s, d=F32: ctx.enter_context(nc.sbuf_tensor(f"{tag}_{n}", s, d))
        sem = lambda n: new_semaphore(nc, sems, f"{tag}_{n}")
        xT = sb("xT", [P, KD, NC, B, XC])
        km = sb("km", [P, KD, ROWS + 2])
        flat = work[:, :, :].rearrange("p t d -> p (t d)")
        taken = 0

        def take(size):
            nonlocal taken
            taken += size
            return flat[:, taken - size:taken]

        per_chunk = lambda: take(KD * B * P).rearrange("p (k b v x) -> p k b v x", k=KD, b=B, v=HALVES)
        G = take(NC * B * XC).rearrange("p (c b x) -> p c b x", b=B, x=XC)
        y = [per_chunk() for q in range(2)]
        h = [per_chunk(), sb("h1", [P, KD, B, HALVES, CHUNK])]
        w2s = take(KD * D).rearrange("p (k d) -> p k d", k=KD)
        xn = [sb(f"xn{u}", [P, D]) for u in range(2)]
        st = sb("st", [P, NT, 6]); mv = sb("mv", [P, NT, 2]); rstd = sb("rstd", [P, NT]); eps = sb("eps", [P, 1])
        ss = sb("ss", [P, NT]); nrm = sb("nrm", [P, NT])
        half = sb("half", [P, HALVES])
        mean_w = sb("mean_w", [P, NT, 2 * HALVES])
        seq = sb("seq", [ROWS, B])
        gwb = sb("gwb", [P, KD, P])
        esel = sb("esel", [2, 2, P])
        sig = [sb(f"sig{u}", [2, B, XC]) for u in range(2)]
        ea = sb("ea", [2, NC, B])
        kk2 = sb("kk2", [P, KD, ROWS]); kks = sb("kks", [P, ROWS])
        m0n = sb("m0n", [P, 1])
        gate = sb("gate", [P, NC, B]); dec = sb("dec", [P, NC, B]); cdec = sb("cdec", [P, NC, B])
        beta = sb("beta", [P, NC, B]); boc = sb("boc", [P, NC, B]); rc = sb("rc", [P, NC, B])
        c2 = sb("c2", [P, NC, B]); coef = sb("coef", [P, NC, 2, B]); kk = sb("kk", [P, NC, B])
        A = [sb(f"A{v}", [P, B]) for v in range(2)]; n2 = sb("n2", [P, B]); n2c = sb("n2c", [P, B]); cA = sb("cA", [P, B])
        f = sb("f", [P, B]); rA = sb("rA", [P, B]); t2 = sb("t2", [P, 2, B]); root = sb("root", [P, B]); scl = sb("scl", [P, B])
        halfpow = sb("halfpow", [P, B])
        ET = sb("ET", [P, KD, NC, B]); Erow = take(D)
        ye = [sb(f"ye{v}", [P, KD, B, 2]) for v in range(2)]
        hs = sb("hs", [P, KD, B])
        e = sb("e", [P, KD, B]); prod = sb("prod", [P, KD, 2, B]); prods = sb("prods", [P, 2, B])

        ps = [ctx.enter_context(nc.psum_tensor(f"{tag}_ps{i}", [P, 512], F32)) for i in range(8)]
        psO = [ps[0:2], ps[2:4]]; psU = ps[4:6]; psE = ps[6]; psF = ps[7]
        psT, psM, psG, psK = ps[0:2], ps[2], ps[5:7], ps[7]
        keys = lambda k: km[:, k, 0:ROWS]

        consts = sem("consts"); var_done = sem("var_done"); std_done = sem("std_done")
        ss_done = sem("ss_done"); nrm_done = sem("nrm_done"); meanw_done = sem("meanw_done")
        n_ready = sem("n_ready"); T_done = sem("T_done"); xT_ready = sem("xT_ready"); mean_done = sem("mean_done")
        xc_ready = sem("xc_ready"); sig_ready = sem("sig_ready"); ea_ready = sem("ea_ready")
        G_done = sem("G_done"); G_ready = sem("G_ready"); kk_ready = sem("kk_ready"); sc_done = sem("sc_done")
        gate_ready = sem("gate_ready")
        o_done = sem("o_done"); y_copied = sem("y_copied"); ye_ready = sem("ye_ready")
        A_ready = sem("A_ready"); us_ready = sem("us_ready"); y_scaled = sem("y_scaled"); u_done = sem("u_done"); h_ready = sem("h_ready")
        hs_ready = sem("hs_ready"); e_done = sem("e_done"); ET_ready = sem("ET_ready"); ER_done = sem("ER_done")
        Erow_ready = sem("Erow_ready"); prods_ready = sem("prods_ready"); pq_done = sem("pq_done")
        n2_ready = sem("n2_ready"); root_ready = sem("root_ready"); f_done = sem("f_done"); f_used = sem("f_used")
        cz = sem("cz")

        block = ctx.enter_context(nc.Block())

        @block.gpsimd
        def _(pool):
            nc.gpsimd.memset(G[:, :, :, :], 0.0)
            nc.gpsimd.memset(ET[:, :, :, :], 0.0)
            nc.gpsimd.memset(Erow[:, :], 0.0)
            nc.gpsimd.memset(halfpow[:, :], 0.5)
            nc.gpsimd.memset(half[:, :], 0.0)
            nc.gpsimd.memset(esel[:, 0, :], MAX_LR / CHUNK)
            nc.gpsimd.memset(esel[:, 1, :], (1.0 - MIN_DECAY) / CHUNK).then_inc(cz, 1)
            pool.wait_ge(cz, 1)
            nc.gpsimd.memset(half[0:CHUNK, 0:1], 1.0 / CHUNK)
            nc.gpsimd.memset(half[CHUNK:P, 1:2], 1.0 / CHUNK)
            nc.gpsimd.affine_select(out=esel[:, 0, :], in_=esel[:, 0, :], compare_op=ALU.is_equal, fill=0.0,
                                    base=0, pattern=[[0, P]], channel_multiplier=1)
            nc.gpsimd.affine_select(out=esel[:, 1, :], in_=esel[:, 1, :], compare_op=ALU.is_equal, fill=0.0,
                                    base=-1, pattern=[[0, P]], channel_multiplier=1).then_inc(consts, 1)
            with pool.Fori(0, NC // 4) as tq:
                for v in range(4):
                    t = tq * 4 + v
                    pool.wait_ge(A_ready, t + 1)
                    pool.wait_ge(u_done, t * KD + KD)
                    chunk = y[v // 2][:, :, :, v % 2, :]
                    nc.gpsimd.tensor_tensor(chunk, chunk, A[v % 2][:, None, :, None].to_broadcast([P, KD, B, CHUNK]),
                                            ALU.mult).then_inc(y_scaled, 1)
                    pool.wait_ge(n2_ready, t + 1)
                    nc.gpsimd.tensor_tensor(root[:, :], n2[:, :], halfpow[:, :], ALU.pow).then_inc(root_ready, 1)

        @block.scalar
        def _(act):
            nc.scalar.preload_act_table(ACT.Sqrt)
            act.wait_ge(var_done, 1)
            nc.scalar.activation(rstd[:, :], mv[:, :, 1], ACT.Sqrt, bias=eps[:, :]).then_inc(std_done, 1)
            act.wait_ge(ss_done, 1)
            nc.scalar.sqrt(nrm[:, :], ss[:, :]).then_inc(nrm_done, 1)
            nc.scalar.preload_act_table(ACT.Sigmoid)
            with act.Fori(0, B) as b:
                with act.Fori(0, NT // B // 2) as cc:
                    for u in range(2):
                        act.wait_ge(T_done, b * (NT // B) + cc * 2 + (u + 1))
                        for k in range(KD):
                            last = nc.scalar.copy(xT[:, k, bass.ds(cc * 4 + 2 * u, HALVES), b, 0:CHUNK],
                                                  psT[u][:, k * P:(k + 1) * P].rearrange("p (c s) -> p c s", c=HALVES))
                        last.then_inc(xT_ready, 1)
            act.wait_ge(sc_done, 1)
            nc.scalar.activation(gate[:, :, :].rearrange("p t b -> p (t b)"), psK[:, 0:ROWS], ACT.Sigmoid,
                                 bias=gate_b[:, :]).then_inc(gate_ready, 1)

            def rates(t, u):
                act.wait_ge(G_done, t + 1)
                nc.scalar.activation(sig[u][:, :, :].rearrange("p b c -> p (b c)"), psG[u][ROWS:ROWS + 2, 0:B * XC],
                                     ACT.Sigmoid, bias=rates_b[ROWS:ROWS + 2, :]).then_inc(sig_ready, 1)

            for u in range(2):
                rates(u, u)
            with act.Fori(1, NC // 2) as tt:
                for u in range(2):
                    act.wait_ge(ea_ready, tt * 2 + (u - 1))
                    rates(tt * 2 + u, u)
            nc.scalar.preload_act_table(ACT.Silu)

            def step(tq, v, first=False):
                t = tq * 4 + v
                q, c = v // 2, v % 2
                if not first:
                    act.wait_ge(f_done, tq * 8 + (-4 if q == 0 else 0))
                for o in range(KD):
                    act.wait_ge(o_done, t * KD + (o + 1))
                    nc.scalar.copy(y[q][:, o, :, c, :], psO[c][o][:, 0:B * XC].rearrange("p (b x) -> p b x", b=B)[:, :, 0:CHUNK]
                                   ).then_inc(y_copied, 1)
                for j in range(KD):
                    act.wait_ge(us_ready, t * KD + (j + 1))
                    nc.scalar.activation(h[q][:, j, :, c, :], h[q][:, j, :, c, :], ACT.Silu).then_inc(h_ready, 1)
                act.wait_ge(ER_done, t + 1)
                nc.scalar.copy(Erow[0:ROWS, :], psE[0:ROWS, D:2 * D]).then_inc(Erow_ready, 1)

            for v in range(4):
                step(0, v, True)
            with act.Fori(1, NC // 4) as tq:
                for v in range(4):
                    step(tq, v)

        @block.vector
        def _(dve):
            nc.vector.memset(eps[:, :], EPS)
            for q, loaded in enumerate(x_loaded):
                dve.wait_ge(loaded, 16)
                part = NT // len(x_loaded)
                with dve.Fori(q * part // 4, (q + 1) * part // 4) as tt:
                    for u in range(4):
                        nc.vector.bn_stats(st[:, tt * 4 + u, :], X[:, tt * 4 + u, :])
            dve.drain()
            for t in range(NT):
                nc.vector.bn_aggr(mv[:, t, :], st[:, t, :])
            dve.drain().then_inc(var_done, 1)
            dve.wait_ge(std_done, 1)
            nc.vector.reciprocal(rstd[:, :], rstd[:, :])
            dve.drain()
            nc.vector.tensor_tensor(ss[:, :], mv[:, :, 1], rstd[:, :], ALU.mult)
            dve.drain()
            nc.vector.tensor_tensor(ss[:, :], ss[:, :], rstd[:, :], ALU.mult)
            dve.drain()
            nc.vector.tensor_scalar(ss[:, :], ss[:, :], float(D), NORM_EPS ** 2, ALU.mult, ALU.max).then_inc(ss_done, 1)

            def normalise(b, i, u):
                t = b * (NT // B) + i
                nc.vector.tensor_scalar(xn[u][:, :], X[:, t, :], mv[:, t, 0:1], rstd[:, bass.ds(t, 1)],
                                        ALU.subtract, ALU.mult).then_inc(n_ready, 1)

            for u in range(2):
                normalise(0, u, u)
            dve.wait_ge(nrm_done, 1)
            nc.vector.reciprocal(nrm[:, :], nrm[:, :])
            dve.wait_ge(consts, 1)
            dve.drain()
            nc.vector.tensor_tensor(mean_w[:, :, 0:HALVES], nrm[:, :, None].to_broadcast([P, NT, HALVES]),
                                    half[:, None, :].to_broadcast([P, NT, HALVES]), ALU.mult)
            nc.vector.tensor_copy(mean_w[:, :, HALVES:], half[:, None, :].to_broadcast([P, NT, HALVES])).then_inc(meanw_done, 1)
            TB = NT // B
            for i in range(2, TB):
                dve.wait_ge(mean_done, i - 1)
                normalise(0, i, i % 2)
            with dve.Fori(1, B) as b:
                with dve.Fori(0, TB // 2) as cc:
                    for u in range(2):
                        dve.wait_ge(mean_done, b * TB + cc * 2 + (u - 1))
                        normalise(b, cc * 2 + u, u)
            dve.wait_ge(*weights_loaded)
            for k in range(KD):
                nc.vector.tensor_copy(gwb[:, k, :], gate_w[:, k:k + 1].to_broadcast([P, P]))
            nc.vector.tensor_scalar(w2s[:, :, :], w2T[:, :, :], 1.0 / CHUNK, None, ALU.mult)
            nc.vector.tensor_reduce(seq[:, :], ident[0:ROWS, 0:ROWS].rearrange("p (t b) -> p b t", b=B), AX.X, ALU.add)
            flat0 = m0T[:, :, :].rearrange("p k o -> p (k o)")
            squares = h[0][:, :, :, :, :].rearrange("p k b c s -> p (k b c s)")[:, 0:KD * D]
            nc.vector.scalar_tensor_tensor(squares, flat0, 1.0, flat0, ALU.mult, ALU.mult, accum_out=m0n[:, :])
            dve.wait_ge(mean_done, NT)
            dve.wait_ge(xT_ready, NT)
            for k in range(KD):
                means = psM[:, k * NT * 4:(k + 1) * NT * 4].rearrange("p (b i c) -> p b i c", b=B, c=2 * HALVES)
                tb = lambda v: v.rearrange("p (i c) b -> p b i c", c=HALVES)
                for b in range(B):
                    nc.vector.tensor_copy(tb(keys(k).rearrange("p (t b) -> p t b", b=B))[:, b], means[:, b, :, 0:HALVES])
                    nc.vector.tensor_copy(tb(xT[:, k, :, :, CHUNK])[:, b], means[:, b, :, 0:HALVES])
            dve.drain()
            for k in range(KD):
                means = psM[:, k * NT * 4:(k + 1) * NT * 4].rearrange("p (b i c) -> p b i c", b=B, c=2 * HALVES)
                for b in range(B):
                    nc.vector.tensor_tensor(tb(xT[:, k, :, :, CHUNK + 1])[:, b], means[:, b, :, HALVES:],
                                            tb(keys(k).rearrange("p (t b) -> p t b", b=B))[:, b], ALU.subtract)
            nc.vector.tensor_copy(km[:, :, ROWS:], rates_w[:, :, :])
            nc.vector.tensor_tensor(kk2[:, :, :], km[:, :, 0:ROWS], km[:, :, 0:ROWS], ALU.mult)
            dve.drain().then_inc(xc_ready, 1)
            nc.vector.tensor_tensor(kks[:, :], kk2[:, 0, :], kk2[:, 1, :], ALU.add).then_inc(kk_ready, 1)
            with dve.Fori(0, NC // 2) as tt:
                for u in range(2):
                    t = tt * 2 + u
                    dve.wait_ge(sig_ready, t + 1)
                    nc.vector.tensor_tensor(G[0:ROWS, t, :, :], psG[u][0:ROWS, 0:B * XC].rearrange("p (b c) -> p b c", b=B),
                                            seq[:, :, None].to_broadcast([ROWS, B, XC]), ALU.mult).then_inc(G_ready, 1)
                    nc.vector.tensor_reduce(ea[:, t, :], sig[u][:, :, 0:CHUNK], AX.X, ALU.add).then_inc(ea_ready, 1)
            dve.wait_ge(gate_ready, 1)
            dve.wait_ge(sc_done, 2)
            fl = lambda v: v[:, :, :].rearrange("p t b -> p (t b)")
            nc.vector.tensor_copy(fl(kk), psK[:, ROWS:2 * ROWS])
            nc.vector.tensor_copy(n2[:, :], psK[:, 2 * ROWS:2 * ROWS + 1].to_broadcast([P, B]))
            nc.vector.tensor_tensor(fl(beta), psK[:, 256:256 + ROWS], fl(gate), ALU.mult)
            nc.vector.tensor_scalar(fl(dec), psK[:, 256 + ROWS:256 + 2 * ROWS], MIN_DECAY - 1.0, None, ALU.add)
            dve.drain()
            nc.vector.tensor_tensor(fl(cdec), fl(dec), fl(gate), ALU.mult)
            dve.drain()
            nc.vector.tensor_scalar(fl(dec), fl(cdec), 1.0, None, ALU.add)
            dve.drain()
            nc.vector.reciprocal(fl(rc), fl(dec))
            nc.vector.tensor_tensor(fl(c2), fl(dec), fl(dec), ALU.mult)
            nc.vector.scalar_tensor_tensor(coef[:, :, 0, :], dec[:, :, :], 2.0, beta[:, :, :], ALU.mult, ALU.mult)
            nc.vector.tensor_tensor(fl(gate), fl(beta), fl(beta), ALU.mult)
            dve.drain()
            nc.vector.tensor_tensor(fl(boc), fl(beta), fl(rc), ALU.mult)
            nc.vector.tensor_tensor(coef[:, :, 1, :], gate[:, :, :], kk[:, :, :], ALU.mult)
            nc.vector.memset(A[0][:, :], 1.0)
            nc.vector.memset(rA[:, :], 1.0)
            dve.drain().then_inc(A_ready, 1)

            def step(tq, v, no_result, first=False):
                t = tq * 4 + v
                q, c = v // 2, v % 2
                scale = A[v % 2]
                dve.wait_ge(y_copied, t * KD + KD)
                for o in range(KD):
                    out = psO[v % 2][o][:, 0:B * XC].rearrange("p (b c) -> p b c", b=B)
                    last = nc.vector.tensor_tensor(ye[v % 2][:, o, :, :], out[:, :, CHUNK:],
                                                   scale[:, :, None].to_broadcast([P, B, 2]), ALU.mult)
                last.then_inc(ye_ready, 1)
                nc.vector.tensor_tensor(f[:, :], boc[:, t, :], rA[:, :], ALU.mult)
                nc.vector.tensor_tensor(n2c[:, :], c2[:, t, :], n2[:, :], ALU.mult)
                nc.vector.tensor_tensor(cA[:, :], dec[:, t, :], scale[:, :], ALU.mult)
                for j in range(KD):
                    dve.wait_ge(u_done, t * KD + (j + 1))
                    nc.vector.tensor_tensor(h[q][:, j, :, c, :], psU[j][:, 0:B * CHUNK].rearrange("p (b s) -> p b s", b=B),
                                            scale[:, :, None].to_broadcast([P, B, CHUNK]), ALU.mult).then_inc(us_ready, 1)
                for j in range(KD):
                    dve.wait_ge(h_ready, t * KD + (j + 1))
                    nc.vector.tensor_reduce(hs[:, j, :], h[q][:, j, :, c, :], AX.X, ALU.add).then_inc(hs_ready, 1)
                if not no_result:
                    result(tq, v, 0)
                dve.wait_ge(e_done, t + 1)
                nc.vector.tensor_tensor(e[:, :, :], psE[:, 0:KD * B].rearrange("p (k b) -> p k b", k=KD),
                                        ye[v % 2][:, :, :, 1], ALU.add)
                dve.drain()
                nc.vector.tensor_tensor(ET[:, :, t, :], e[:, :, :], f[:, None, :].to_broadcast([P, KD, B]),
                                        ALU.mult).then_inc(ET_ready, 1)
                nc.vector.tensor_tensor(prod[:, :, 0, :], e[:, :, :], ye[v % 2][:, :, :, 0], ALU.mult)
                nc.vector.tensor_tensor(prod[:, :, 1, :], e[:, :, :], e[:, :, :], ALU.mult)
                dve.drain()
                nc.vector.tensor_tensor(prods[:, :, :], prod[:, 0, :, :], prod[:, 1, :, :], ALU.add).then_inc(prods_ready, 1)
                dve.wait_ge(pq_done, t + 1)
                nc.vector.tensor_tensor(t2[:, :, :], coef[:, t, :, :], psU[1][:, 256:256 + 2 * B].rearrange("p (q b) -> p q b", q=2),
                                        ALU.mult)
                dve.drain()
                nc.vector.tensor_tensor(n2c[:, :], n2c[:, :], t2[:, 0, :], ALU.add)
                dve.drain()
                nc.vector.tensor_tensor(n2c[:, :], n2c[:, :], t2[:, 1, :], ALU.add)
                dve.drain()
                nc.vector.tensor_scalar(n2[:, :], n2c[:, :], 0.0, None, ALU.max).then_inc(n2_ready, 1)
                dve.wait_ge(root_ready, t + 1)
                nc.vector.tensor_scalar(scl[:, :], root[:, :], 1e-6, None, ALU.add)
                dve.drain()
                nc.vector.reciprocal(scl[:, :], scl[:, :])
                dve.drain()
                nc.vector.tensor_scalar(scl[:, :], scl[:, :], MAX_NORM, 1.0, ALU.mult, ALU.min)
                dve.drain()
                if not first:
                    dve.wait_ge(y_scaled, t)
                nc.vector.tensor_tensor(A[1 - v % 2][:, :], cA[:, :], scl[:, :], ALU.mult)
                nc.vector.tensor_tensor(n2[:, :], n2[:, :], scl[:, :], ALU.mult)
                dve.drain().then_inc(A_ready, 1)
                nc.vector.reciprocal(rA[:, :], A[1 - v % 2][:, :])
                nc.vector.tensor_tensor(n2[:, :], n2[:, :], scl[:, :], ALU.mult)
                dve.drain()
                if not no_result:
                    result(tq, v, 1)
                    statistics(tq, v)

            def pair_tile(tq, v, i):
                return tq * 2 + (0 if v >= 2 else -1) + (v % 2 * 2 + i) * (NT // B)

            def statistics(tq, v):
                dve.drain()
                for i in range(2):
                    nc.vector.bn_stats(stats[:, pair_tile(tq, v, i), :], X[:, pair_tile(tq, v, i), :])

            def result(tq, v, i):
                t = pair_tile(tq, v, i)
                dve.wait_ge(f_done, tq * 8 + (v - 2) * 2 + (i + 1))
                nc.vector.tensor_tensor(X[:, t, :], X[:, t, :], psF[:, 0:D], ALU.add).then_inc(f_used, 1)

            for v in range(4):
                step(0, v, v < 2, v == 0)
            with dve.Fori(1, NC // 4) as tq:
                for v in range(4):
                    step(tq, v, False)
            for v in range(2):
                for i in range(2):
                    result(NC // 4, v, i)
                statistics(NC // 4, v)

        @block.tensor
        def _(pe):
            TB = NT // B
            pe.wait_ge(meanw_done, 1)

            def rows_in(b, i, u, first=False):
                t = b * TB + i
                pe.wait_ge(n_ready, t + 1)
                if not first:
                    pe.wait_ge(xT_ready, t - 1)
                for k in range(KD):
                    last = nc.tensor.transpose(psT[u][:, k * P:(k + 1) * P], xn[u][:, k * P:(k + 1) * P], ident[:, :])
                last.then_inc(T_done, 1)
                for k in range(KD):
                    last = nc.tensor.matmul(psM[:, bass.ds((t + k * NT) * 4, 4)], xn[u][:, k * P:(k + 1) * P],
                                            mean_w[:, t, :], start=True, stop=True)
                last.then_inc(mean_done, 1)

            for i in range(TB):
                rows_in(0, i, i % 2, i < 2)
            with pe.Fori(1, B) as b:
                with pe.Fori(0, TB // 2) as cc:
                    for u in range(2):
                        rows_in(b, cc * 2 + u, u)
            pe.wait_ge(xc_ready, 1)
            for k in range(KD):
                last = nc.tensor.matmul(psK[:, 0:ROWS], gwb[:, k, :], keys(k), start=(k == 0), stop=(k == KD - 1))
            pe.wait_ge(kk_ready, 1)
            nc.tensor.matmul(psK[:, ROWS:2 * ROWS], ones[:, :], kks[:, :], start=True, stop=True)
            nc.tensor.matmul(psK[:, 2 * ROWS:2 * ROWS + 1], ones[:, :], m0n[:, :], start=True, stop=True).then_inc(sc_done, 1)

            def rates_and_products(t, u, first):
                if not first:
                    pe.wait_ge(G_ready, t - 1)
                for k in range(KD):
                    xk = xT[:, k, t, :, :].rearrange("p b c -> p (b c)")
                    last = nc.tensor.matmul(psG[u][0:ROWS + 2, 0:B * XC], km[:, k, :], xk, start=(k == 0), stop=(k == KD - 1))
                last.then_inc(G_done, 1)

            for u in range(2):
                rates_and_products(u, u, True)
            with pe.Fori(1, NC // 2) as tt:
                for u in range(2):
                    rates_and_products(tt * 2 + u, u, False)
            pe.wait_ge(ea_ready, NC)
            pe.wait_ge(gate_ready, 1)
            for i in range(2):
                last = nc.tensor.matmul(psK[:, 256 + i * ROWS:256 + (i + 1) * ROWS], esel[:, i, :],
                                        ea[:, :, :].rearrange("p t b -> p (t b)"), start=True, stop=True)
            last.then_inc(sc_done, 1)
            pe.wait_ge(A_ready, 1)
            pe.wait_ge(G_ready, NC)

            def first_memory(t, v, o):
                for k in range(KD):
                    nc.tensor.matmul(psO[v % 2][o][:, 0:B * XC], m0T[:, k, o * P:(o + 1) * P],
                                     xT[:, k, t, :, :].rearrange("p b c -> p (b c)"), start=(k == 0), stop=False)

            def result_hidden(tq, v, i):
                q = 0 if v >= 2 else 1
                b = v % 2 * 2 + i
                count = tq * 8 + (v - 2) * 2 + i
                if not (isinstance(tq, int) and tq == 0 and v == 2 and i == 0):
                    pe.wait_ge(f_used, count)
                for k in range(KD):
                    nc.tensor.matmul(psF[:, 0:D], h[q][:, k, b, :, :].rearrange("p c s -> p (c s)"), w2T[:, k, :],
                                     start=(k == 0), stop=False, skip_group_check=True)

            def result_outputs(tq, v, i):
                q = 0 if v >= 2 else 1
                b = v % 2 * 2 + i
                pe.wait_ge(y_scaled, tq * 4 + (2 if v >= 2 else 0))
                for o in range(KD):
                    last = nc.tensor.matmul(psF[:, o * P:(o + 1) * P], y[q][:, o, b, :, :].rearrange("p c s -> p (c s)"),
                                            ident[:, :], start=False, stop=(o == KD - 1), skip_group_check=True)
                last.then_inc(f_done, 1)

            def step(tq, v, no_result, first=False, last_step=False):
                t = tq * 4 + v
                q, c = v // 2, v % 2
                if not first:
                    pe.wait_ge(Erow_ready, t)
                for o in range(KD):
                    nc.tensor.matmul(psO[v % 2][o][:, 0:B * XC], Erow[:, o * P:(o + 1) * P],
                                     G[:, t, :, :].rearrange("p b c -> p (b c)"), start=False, stop=True).then_inc(o_done, 1)
                if not last_step:
                    if not first:
                        pe.wait_ge(ye_ready, t)
                    first_memory(t + 1, v + 1, 0)
                pe.wait_ge(y_copied, t * KD + KD)
                if not first:
                    pe.wait_ge(n2_ready, t)
                for j in range(KD):
                    for o in range(KD):
                        last = nc.tensor.matmul(psU[j][:, 0:B * CHUNK], w1T[:, o, j * P:(j + 1) * P],
                                                y[q][:, o, :, c, :], start=(o == 0), stop=(o == KD - 1))
                    last.then_inc(u_done, 1)
                if not last_step:
                    first_memory(t + 1, v + 1, 1)
                if not no_result:
                    result_hidden(tq, v, 0)
                    result_outputs(tq, v, 0)
                pe.wait_ge(hs_ready, t * KD + KD)
                for o in range(KD):
                    for j in range(KD):
                        last = nc.tensor.matmul(psE[:, o * B:(o + 1) * B], w2s[:, j, o * P:(o + 1) * P], hs[:, j, :],
                                                start=(j == 0), stop=(j == KD - 1))
                last.then_inc(e_done, 1)
                if not no_result:
                    result_hidden(tq, v, 1)
                pe.wait_ge(ET_ready, t + 1)
                for o in range(KD):
                    last = nc.tensor.matmul(psE[0:ROWS, D + o * P:D + (o + 1) * P], ET[:, o, :, :].rearrange("p t b -> p (t b)"),
                                            ident[:, :], start=True, stop=True)
                last.then_inc(ER_done, 1)
                pe.wait_ge(prods_ready, t + 1)
                nc.tensor.matmul(psU[1][:, 256:256 + 2 * B], ones[:, :], prods[:, :, :].rearrange("p q b -> p (q b)"),
                                 start=True, stop=True).then_inc(pq_done, 1)
                if not no_result:
                    result_outputs(tq, v, 1)

            for o in range(KD):
                first_memory(0, 0, o)
            for v in range(4):
                step(0, v, v < 2, v == 0)
            with pe.Fori(1, NC // 4 - 1) as tq:
                for v in range(4):
                    step(tq, v, False)
            for v in range(4):
                step(NC // 4 - 1, v, False, False, v == 3)
            for v in range(2):
                for i in range(2):
                    result_hidden(NC // 4, v, i)
                    result_outputs(NC // 4, v, i)


HEADS, HD = 16, 16
GROUP = 4
NG = HEADS // GROUP
CT = 4
CW = CT * P
NCH = TOKENS // CW
QT = S // P
HALF = 512
Q_PARTS = [0, 0, 0, 1, 1, 2]
K_PARTS = [0, 1, 2, 0, 1, 0]
KROWS = len(Q_PARTS) * HD
MROWS = KROWS + 3
VC = HD + 1


SUB = 2 * QT * GROUP
SLOTS = 2 * QT
SHARE = SUB // SLOTS
LEAD = 4


class HandedOn:

    def __init__(self, sb, sem):
        self.qs = [sb(f"qs{g}", [MROWS, GROUP, S], BF16) for g in range(NG)]
        self.ks = [sb(f"ks{g}", [MROWS, GROUP, S], BF16) for g in range(NG)]
        self.va = [sb(f"va{g}", [P, QT, GROUP * VC]) for g in range(NG)]
        self.mxh = sb("mxh", [P, QT, GROUP, 2])
        self.mx = sb("mx", [P, QT * GROUP])
        self.mxr = sb("mxr", [P, QT * GROUP])
        self.zeros = sb("zeros", [P, QT * GROUP])
        self.mx3 = sb("mx3", [P, QT, GROUP, 3], BF16)
        self.mxT = [sb(f"mxT{v}", [GROUP * 3, S], BF16) for v in range(2)]
        self.loaded = [sem(f"loaded{g}") for g in range(NG)]
        self.v_loaded = [sem(f"v_loaded{g}") for g in range(NG)]
        self.sub_done = sem("sub_done")
        self.sub_used = sem("sub_used")
        self.mx_found = sem("mx_found")
        self.mx_ready = sem("mx_ready")
        self.mxT_done = sem("mxT_done")
        self.mxT_ready = sem("mxT_ready")
        self.mx_rows = [sem(f"mx_rows{g}") for g in range(NG)]
        self.rows_ready = sem("rows_ready")


def following(b, g):
    return (b, g + 1) if g + 1 < NG else (b + 1, 0)


def before(b, g, n):
    return b * (NG * n) + g * n


def load_group(sp, a, b, g, qk_d, v_d):
    for dst, w, parts in ((a.qs, 0, Q_PARTS), (a.ks, 1, K_PARTS)):
        for i, part in enumerate(parts):
            sp.dma_start(dst[g][i * HD:(i + 1) * HD, :, :],
                         qk_d[w, part, b, g * GROUP * HD:(g + 1) * GROUP * HD, :]
                         .rearrange("(r d) t -> d r t", d=HD)).then_inc(a.loaded[g], 16)
    sp.dma_start(a.va[g][:, :, :], v_d[b, g, :, :, :]).then_inc(a.v_loaded[g], 16)


def maximum_products(nc, pe, a, psS, b, g, which, first=False):
    for v in which:
        if not (first and v < 2):
            pe.wait_ge(a.sub_used, before(b, g, SUB) + (v - 1))
        nc.tensor.matmul(psS[v % 2][:, :], a.qs[g][0:KROWS, v // 2 % GROUP, v // 8 * P:(v // 8 + 1) * P],
                         a.ks[g][0:KROWS, v // 2 % GROUP, v % 2 * HALF:(v % 2 + 1) * HALF],
                         start=True, stop=True).then_inc(a.sub_done, 1)


def maximum_reductions(nc, dve, a, psS, b, g, which):
    for v in which:
        dve.wait_ge(a.sub_done, before(b, g, SUB) + (v + 1))
        nc.vector.tensor_reduce(a.mxh[:, v // 8, v // 2 % GROUP, v % 2:v % 2 + 1], psS[v % 2][:, :], AX.X,
                                ALU.max).then_inc(a.sub_used, 1)


def group_maxima(nc, dve, a, b, g, first=False):
    dve.drain()
    if not first:
        dve.wait_ge(a.mx_ready, before(b, g, 1))
    halves = a.mxh[:, :, :, :].rearrange("p q r h -> p (q r) h")
    nc.vector.tensor_tensor(a.mx[:, :], halves[:, :, 0], halves[:, :, 1], ALU.max).then_inc(a.mx_found, 1)


def maximum_parts(nc, pool, a, b, g):
    pool.wait_ge(a.mx_found, before(b, g, 1) + 1)
    part = lambda i: a.mx3[:, :, :, i].rearrange("p q r -> p (q r)")
    nc.gpsimd.tensor_tensor(part(0), a.mx[:, :], a.zeros[:, :], ALU.add)
    pool.drain()
    nc.gpsimd.tensor_tensor(a.mxr[:, :], a.mx[:, :], part(0), ALU.subtract)
    pool.drain()
    nc.gpsimd.tensor_copy(part(1), a.mxr[:, :])
    pool.drain()
    nc.gpsimd.tensor_tensor(part(2), a.mxr[:, :], part(1), ALU.subtract).then_inc(a.mx_ready, 1)


def maxima_rows(nc, pe, a, bank, identb, b, g, v, bank_free):
    pe.wait_ge(a.mx_ready, before(b, g, 1) + 1)
    if bank_free is not None:
        pe.wait_ge(*bank_free)
    for q in range(QT // 2):
        last = nc.tensor.matmul(bank[0:GROUP * 3, q * P:(q + 1) * P],
                                a.mx3[:, v * (QT // 2) + q, :, :].rearrange("p r c -> p (r c)"),
                                identb[:, :], start=True, stop=True)
    last.then_inc(a.mxT_done, 1)


def maxima_out(nc, act, a, bank, b, g, v):
    act.wait_ge(a.mxT_done, before(b, g, 2) + (v + 1))
    nc.scalar.copy(a.mxT[g % 2][:, v * HALF:(v + 1) * HALF], bank[0:GROUP * 3, :]).then_inc(a.mxT_ready, 1)


def place_rows(sp, a, b, g):
    sp.wait_ge(a.mxT_ready, before(b, g, 2) + 2)
    for r in range(GROUP):
        sp.dma_start(a.qs[g][KROWS:MROWS, r, :], a.mxT[g % 2][r * 3:(r + 1) * 3, :]).then_inc(a.mx_rows[g], 16)


def attention_phase(nc, tag, X, stats, ident, identb, wqk, wv, bqk, bv, bo, weights_loaded, qk_d, v_d, O):
    ctx = ExitStack()
    sems = []
    ctx.callback(release, nc, sems)
    with ctx:
        sb = lambda n, s, d=F32: ctx.enter_context(nc.sbuf_tensor(f"{tag}_{n}", s, d))
        sem = lambda n: new_semaphore(nc, sems, f"{tag}_{n}")
        a = HandedOn(sb, sem)
        qkv_phase(nc, f"{tag}_qkv", X, stats, ident, identb, wqk, wv, bqk, bv, bo, weights_loaded, a, qk_d, v_d)
        scores_phase(nc, f"{tag}_scores", ident, identb, a, qk_d, v_d, O)


def qkv_phase(nc, tag, X, stats, ident, identb, wqk, wv, bqk, bv, bo, weights_loaded, a, qk_d, v_d):
    ctx = ExitStack()
    sems = []
    ctx.callback(release, nc, sems)
    with ctx:
        sb = lambda n, s, d=F32: ctx.enter_context(nc.sbuf_tensor(f"{tag}_{n}", s, d))
        sem = lambda n: new_semaphore(nc, sems, f"{tag}_{n}")
        xn = [sb(f"xn{j}", [P, D]) for j in range(CT)]
        xT = [sb(f"xT{u}", [P, KD, CW]) for u in range(2)]
        mv = sb("mv", [P, NT, 2]); rstd = sb("rstd", [P, NT]); eps = sb("eps", [P, 1])
        NM = 2 * KD
        parts = [[sb(f"parts{u}{m}", [P, 3, CW], BF16) for m in range(NM)] for u in range(2)]
        rest = [sb(f"rest{m}", [P, CW]) for m in range(NM)]
        vt = [[sb(f"vt{u}{j}", [P, HEADS, VC]) for j in range(CT)] for u in range(2)]
        ps = [ctx.enter_context(nc.psum_tensor(f"{tag}_ps{i}", [P, 512], F32)) for i in range(8)]
        psT, psQ, psV, psS = ps[0:2], ps[2:4], ps[4:6], ps[6:8]

        var_done = sem("var_done"); std_done = sem("std_done")
        n_ready = sem("n_ready"); T_done = sem("T_done"); xT_ready = sem("xT_ready")
        qk_done = sem("qk_done"); hi_ready = sem("hi_ready"); rest_ready = sem("rest_ready")
        mid_ready = sem("mid_ready"); lo_ready = sem("lo_ready")
        v_done = sem("v_done"); v_ready = sem("v_ready")
        parts_stored = [sem(f"parts_stored{u}") for u in range(2)]
        v_stored = [sem(f"v_stored{u}") for u in range(2)]

        BESIDE, MAX_AT = 3, NM + CT
        early = [(0, v) for v in range(SUB)] + [(1, v) for v in range(LEAD * SHARE)]
        PER = -(-len(early) // ((NCH - BESIDE) * MAX_AT))

        def early_maxima(c, i):
            first = ((c - BESIDE) * MAX_AT + i) * PER
            return early[first:first + PER] if c >= BESIDE else []

        block = ctx.enter_context(nc.Block())

        @block.sync
        def _(sp):
            for c in range(NCH):
                u = c % 2
                b, half = divmod(c, NCH // B)
                for m in range(NM):
                    sp.wait_ge(lo_ready, c * NM + m + 1)
                    sp.dma_start(qk_d[m // KD, :, b, (m % KD) * P:(m % KD + 1) * P, half * CW:(half + 1) * CW]
                                 .rearrange("s p t -> p s t"), parts[u][m][:, :, :]).then_inc(parts_stored[u], 16)
                for j in range(CT):
                    sp.wait_ge(v_ready, c * CT + j + 1)
                    sp.dma_start(v_d[b, :, :, half * CT + j, :].rearrange("g p c -> p g c"),
                                 vt[u][j][:, :, :].rearrange("p (g h) c -> p g (h c)", g=NG)).then_inc(v_stored[u], 16)
                    if c == NCH - 1 and j == 0:
                        place_rows(sp, a, 0, 0)
                if c == 1:
                    for v in range(2):
                        sp.wait_ge(parts_stored[v], 16 * NM)
                        sp.wait_ge(v_stored[v], 16 * CT)
                if 1 <= c < 1 + NG:
                    load_group(sp, a, 0, c - 1, qk_d, v_d)
            for u in range(2):
                sp.wait_ge(parts_stored[u], 16 * NM * (NCH // 2))
                sp.wait_ge(v_stored[u], 16 * CT * (NCH // 2))

        @block.gpsimd
        def _(pool):
            nc.gpsimd.memset(a.zeros[:, :], 0.0).then_inc(a.rows_ready, 1)
            pool.wait_ge(a.rows_ready, 1)
            for g in range(NG):
                nc.gpsimd.memset(a.ks[g][KROWS:MROWS, :, :], -1.0).then_inc(a.rows_ready, 1)
                pool.wait_ge(a.rows_ready, g + 2)
            pool.wait_ge(*weights_loaded)
            for c in range(NCH):
                if c == NCH - 1:
                    maximum_parts(nc, pool, a, 0, 0)
                for m in range(NM):
                    pool.wait_ge(mid_ready, c * NM + m + 1)
                    nc.gpsimd.tensor_tensor(parts[c % 2][m][:, 2, :], rest[m][:, :], parts[c % 2][m][:, 1, :],
                                            ALU.subtract).then_inc(lo_ready, 1)
                for j in range(CT):
                    pool.wait_ge(n_ready, c * CT + j + 1)
                    nc.gpsimd.tensor_tensor(X[:, c * CT + j, :], X[:, c * CT + j, :], bo[:, :], ALU.add)

        @block.scalar
        def _(act):
            nc.scalar.preload_act_table(ACT.Sqrt)
            act.wait_ge(var_done, 1)
            nc.scalar.activation(rstd[:, :], mv[:, :, 1], ACT.Sqrt, bias=eps[:, :]).then_inc(std_done, 1)

            def rows_out(c):
                act.wait_ge(T_done, c + 1)
                for k in range(KD):
                    last = nc.scalar.copy(xT[c % 2][:, k, :], psT[k][:, :])
                last.then_inc(xT_ready, 1)

            def high(c, m):
                act.wait_ge(qk_done, c * NM + m + 1)
                nc.scalar.activation(parts[c % 2][m][:, 0, :], psQ[m % 2][:, :], ACT.Identity,
                                     bias=bqk[:, m:m + 1]).then_inc(hi_ready, 1)

            def middle(c, m):
                act.wait_ge(rest_ready, c * NM + m + 1)
                nc.scalar.copy(parts[c % 2][m][:, 1, :], rest[m][:, :]).then_inc(mid_ready, 1)

            rows_out(0)
            act.wait_ge(*weights_loaded)
            for c in range(NCH):
                if c >= 2:
                    act.wait_ge(parts_stored[c % 2], c // 2 * 16 * NM)
                for m in range(NM):
                    high(c, m)
                    if m:
                        middle(c, m - 1)
                middle(c, NM - 1)
                if c == NCH - 1:
                    for v in range(2):
                        maxima_out(nc, act, a, psT[v], 0, 0, v)
                if c + 1 < NCH:
                    rows_out(c + 1)

        @block.vector
        def _(dve):
            nc.vector.memset(eps[:, :], EPS)
            for u in range(2):
                for j in range(CT):
                    nc.vector.memset(vt[u][j][:, :, HD:VC], 1.0)
            for t in range(NT):
                nc.vector.bn_aggr(mv[:, t, :], stats[:, t, :])
            dve.drain().then_inc(var_done, 1)
            dve.wait_ge(std_done, 1)
            nc.vector.reciprocal(rstd[:, :], rstd[:, :])
            dve.drain()

            def rows(c):
                for j in range(CT):
                    t = c * CT + j
                    nc.vector.tensor_scalar(xn[j][:, :], X[:, t, :], mv[:, t, 0:1], rstd[:, t:t + 1],
                                            ALU.subtract, ALU.mult).then_inc(n_ready, 1)

            def maxima(c, i):
                for g, v in early_maxima(c, i):
                    maximum_reductions(nc, dve, a, psS, 0, g, [v])
                    if (g, v) == (0, SUB - 1):
                        group_maxima(nc, dve, a, 0, 0, True)
                        dve.wait_ge(a.mx_found, 1)

            rows(0)
            dve.wait_ge(*weights_loaded)
            for c in range(NCH):
                u = c % 2
                if c + 1 < NCH:
                    dve.wait_ge(T_done, c + 1)
                    rows(c + 1)
                if c >= 2:
                    dve.wait_ge(v_stored[u], c // 2 * 16 * CT)
                for m in range(NM):
                    dve.wait_ge(hi_ready, c * NM + m + 1)
                    if c:
                        dve.wait_ge(lo_ready, c * NM + m + 1 - NM)
                    nc.vector.scalar_tensor_tensor(rest[m][:, :], psQ[m % 2][:, :], bqk[:, m:m + 1],
                                                   parts[u][m][:, 0, :], ALU.add, ALU.subtract).then_inc(rest_ready, 1)
                    maxima(c, m)
                for j in range(CT):
                    dve.wait_ge(v_done, c * CT + j + 1)
                    nc.vector.tensor_tensor(vt[u][j][:, :, 0:HD],
                                            psV[j % 2][:, 0:D].rearrange("p (h d) -> p h d", d=HD),
                                            bv[:, :].rearrange("p (h d) -> p h d", d=HD), ALU.add).then_inc(v_ready, 1)
                    maxima(c, NM + j)

        @block.tensor
        def _(pe):
            def rows_in(c):
                pe.wait_ge(n_ready, c * CT + CT)
                if c:
                    pe.wait_ge(xT_ready, c)
                for k in range(KD):
                    for j in range(CT):
                        last = nc.tensor.transpose(psT[k][:, j * P:(j + 1) * P], xn[j][:, k * P:(k + 1) * P], ident[:, :])
                last.then_inc(T_done, 1)

            def maxima(c, i):
                for g, v in early_maxima(c, i):
                    if v == 0:
                        pe.wait_ge(a.loaded[g], 16 * 2 * len(Q_PARTS))
                    maximum_products(nc, pe, a, psS, 0, g, [v], first=g == 0)

            rows_in(0)
            pe.wait_ge(*weights_loaded)
            for c in range(NCH):
                u = c % 2
                pe.wait_ge(xT_ready, c + 1)
                for m in range(NM):
                    if c * NM + m >= 2:
                        pe.wait_ge(rest_ready, c * NM + m - 1)
                    for k in range(KD):
                        last = nc.tensor.matmul(psQ[m % 2][:, :], wqk[:, k, m * P:(m + 1) * P], xT[u][:, k, :],
                                                start=(k == 0), stop=(k == KD - 1))
                    last.then_inc(qk_done, 1)
                    maxima(c, m)
                if c == NCH - 1:
                    for v in range(2):
                        maxima_rows(nc, pe, a, psT[v], identb, 0, 0, v, None)
                if c + 1 < NCH:
                    rows_in(c + 1)
                for j in range(CT):
                    if c * CT + j >= 2:
                        pe.wait_ge(v_ready, c * CT + j - 1)
                    for k in range(KD):
                        last = nc.tensor.matmul(psV[j % 2][:, 0:D], xT[u][:, k, j * P:(j + 1) * P], wv[:, k, :],
                                                start=(k == 0), stop=(k == KD - 1))
                    last.then_inc(v_done, 1)
                    maxima(c, NM + j)


def scores_phase(nc, tag, ident, identb, a, qk_d, v_d, O):
    ctx = ExitStack()
    sems = []
    ctx.callback(release, nc, sems)
    with ctx:
        sb = lambda n, s, d=F32: ctx.enter_context(nc.sbuf_tensor(f"{tag}_{n}", s, d))
        sem = lambda n: new_semaphore(nc, sems, f"{tag}_{n}")
        qs, ks, va, loaded, v_loaded = a.qs, a.ks, a.va, a.loaded, a.v_loaded
        mxT_ready, mx_rows = a.mxT_ready, a.mx_rows
        pt = [[sb(f"pt{v}{h}", [P, 2, HALF]) for h in range(2)] for v in range(2)]
        osb = [sb(f"osb{h}", [P, HALF]) for h in range(2)]
        rden = [sb(f"rden{h}", [P, QT // 2, GROUP]) for h in range(2)]
        psS = [ctx.enter_context(nc.psum_tensor(f"{tag}_psS{h}", [P, HALF], F32)) for h in range(2)]
        psE = [ctx.enter_context(nc.psum_tensor(f"{tag}_psE{h}", [P, 2, HALF], F32)) for h in range(2)]
        psO = ctx.enter_context(nc.psum_tensor(f"{tag}_psO", [P, HALF], F32))
        psX = ctx.enter_context(nc.psum_tensor(f"{tag}_psX", [P, HALF], F32))

        psO_cleared = sem("psO_cleared")
        e_done = sem("e_done"); p_ready = sem("p_ready"); pv_done = sem("pv_done")
        o_ready = sem("o_ready"); oT_done = sem("oT_done"); ot_ready = sem("ot_ready")

        EARLY = 4

        def taken_along(b, g, s):
            nb, ng = following(b, g)
            first = (s + LEAD) % SLOTS * SHARE
            if s >= SLOTS - LEAD:
                nb, ng = following(nb, ng)
            return nb, ng, range(first, first + SHARE)

        MAX_T = (SLOTS - LEAD, SLOTS - LEAD + 1)
        in_range = lambda b, g: not (isinstance(b, int) and b >= B)

        block = ctx.enter_context(nc.Block())

        @block.sync
        def _(sp):
            def group(b, g, last):
                if not (last and g == NG - 1):
                    place_rows(sp, a, *following(b, g))
                if not last:
                    sp.wait_ge(pv_done, before(b, g, SLOTS) + SLOTS)
                    load_group(sp, a, b + 1, g, qk_d, v_d)

            with sp.Fori(0, B - 1) as b:
                for g in range(NG):
                    group(b, g, False)
            for g in range(NG):
                group(B - 1, g, True)

        @block.gpsimd
        def _(pool):
            with pool.Fori(0, B - 1) as b:
                for g in range(NG):
                    maximum_parts(nc, pool, a, *following(b, g))
            for g in range(NG - 1):
                maximum_parts(nc, pool, a, B - 1, g + 1)

        @block.scalar
        def _(act):
            nc.scalar.preload_act_table(ACT.Exp)

            def exps(b, g, s, h, first=False):
                act.wait_ge(e_done, before(b, g, 2 * SLOTS) + (2 * s + h + 1))
                if not first:
                    act.wait_ge(pv_done, before(b, g, SLOTS) + (s - 1))
                nc.scalar.activation(pt[s % 2][h][:, :, :], psE[h][:, :, :], ACT.Exp,
                                     scale=HD ** -0.5).then_inc(p_ready, 1)

            def sums_out(b, g, h):
                act.wait_ge(pv_done, before(b, g, SLOTS) + (h + 1) * QT)
                nc.scalar.copy(osb[h][:, :], psO[:, :]).then_inc(o_ready, 1)

            def slots(b, g, which, first=False, last=False):
                for s in which:
                    if s == 1 and not first:
                        sums_out(*(b, g - 1) if g else (b - 1, NG - 1), 1)
                    if s == QT + 1:
                        sums_out(b, g, 0)
                    exps(b, g, s, 0, first and s < 2)
                    exps(b, g, s, 1, first and s < 2)
                    if s in MAX_T and not last:
                        maxima_out(nc, act, a, psX, *following(b, g), MAX_T.index(s))

            slots(0, 0, range(EARLY), first=True)
            with act.Fori(0, B - 1) as b:
                for g in range(NG):
                    slots(b, g, range(EARLY, SLOTS))
                    slots(*following(b, g), range(EARLY))
            for g in range(NG):
                slots(B - 1, g, range(EARLY, SLOTS), last=g == NG - 1)
                if g + 1 < NG:
                    slots(B - 1, g + 1, range(EARLY))
            sums_out(B - 1, NG - 1, 1)

        @block.vector
        def _(dve):
            nc.vector.memset(psO[:, :], 0.0).then_inc(psO_cleared, 1)
            dve.sem_inc(ot_ready, 1)

            def divide(b, g, h):
                dve.wait_ge(oT_done, before(b, g, 2) + (h + 1))
                view = psX[:, :].rearrange("p (t r c) -> p t r c", r=GROUP, c=32)
                nc.vector.reciprocal(rden[h][:, :, :], view[:, :, :, HD])
                dve.drain()
                tiles = bass.ds(b * QT + h * (QT // 2), QT // 2)
                nc.vector.tensor_tensor(O[:, tiles, g * GROUP * HD:(g + 1) * GROUP * HD]
                                        .rearrange("p t (r c) -> p t r c", c=HD), view[:, :, :, 0:HD],
                                        rden[h][:, :, :, None].to_broadcast([P, QT // 2, GROUP, HD]),
                                        ALU.mult).then_inc(ot_ready, 1)

            def slots(b, g, which, first=False, last=False):
                for s in which:
                    nb, ng, which_max = taken_along(b, g, s)
                    if in_range(nb, ng):
                        maximum_reductions(nc, dve, a, psS, nb, ng, which_max)
                        if s == SLOTS - LEAD - 1:
                            group_maxima(nc, dve, a, nb, ng)
                    if s == 3 and not first:
                        divide(*(b, g - 1) if g else (b - 1, NG - 1), 1)
                    if s == QT + 3:
                        divide(b, g, 0)

            slots(0, 0, range(EARLY), first=True)
            with dve.Fori(0, B - 1) as b:
                for g in range(NG):
                    slots(b, g, range(EARLY, SLOTS))
                    slots(*following(b, g), range(EARLY))
            for g in range(NG):
                slots(B - 1, g, range(EARLY, SLOTS), last=g == NG - 1)
                if g + 1 < NG:
                    slots(B - 1, g + 1, range(EARLY), last=g + 1 == NG - 1)
            divide(B - 1, NG - 1, 1)

        @block.tensor
        def _(pe):
            def scores(b, g, s, r, first=False):
                half, kt = divmod(s, QT)
                if r % 2 == 0 and not first:
                    pe.wait_ge(p_ready, before(b, g, 2 * SLOTS) + (2 * s + r // 2 - 1))
                product = nc.tensor.matmul(psE[r // 2][:, r % 2, :], ks[g][0:MROWS, r, kt * P:(kt + 1) * P],
                                           qs[g][0:MROWS, r, half * HALF:(half + 1) * HALF], start=True, stop=True)
                if r % 2 == 1:
                    product.then_inc(e_done, 1)

            def sums(b, g, s, c, first=False):
                half, kt = divmod(s, QT)
                if c == 0:
                    pe.wait_ge(p_ready, before(b, g, 2 * SLOTS) + (2 * s + 2))
                    if s == 0:
                        pe.wait_ge(v_loaded[g], b * 16 + 16)
                    if kt == 0 and not first:
                        pe.wait_ge(o_ready, before(b, g, 2) + half)
                cols = slice(c * HALF // 2, (c + 1) * HALF // 2)
                for r in range(GROUP):
                    last = nc.tensor.matmul(psO[32 * r:32 * r + VC, cols], va[g][:, kt, r * VC:(r + 1) * VC],
                                            pt[s % 2][r // 2][:, r % 2, cols], start=(kt == 0 and c == 0),
                                            stop=(kt == QT - 1 and c == 1), tile_position=(0, 32 * r),
                                            skip_group_check=True)
                if c == 1:
                    last.then_inc(pv_done, 1)

            def sums_T(b, g, h, psX_free):
                pe.wait_ge(o_ready, before(b, g, 2) + (h + 1))
                pe.wait_ge(*psX_free)
                for q in range(QT // 2):
                    last = nc.tensor.transpose(psX[:, q * P:(q + 1) * P], osb[h][:, q * P:(q + 1) * P], ident[:, :])
                last.then_inc(oT_done, 1)

            def slots(b, g, which, first=False, last=False):
                nb, ng = following(b, g)
                pb, pg = (b, g - 1) if g else (b - 1, NG - 1)
                for s in which:
                    mb, mg, which_max = taken_along(b, g, s)
                    some = which_max if in_range(mb, mg) else ()
                    if s == 0:
                        pe.wait_ge(mx_rows[g], b * (16 * GROUP) + 16 * GROUP)
                    if s == SLOTS - LEAD and some:
                        pe.wait_ge(loaded[mg], mb * (16 * 12) + 16 * 12)
                    scores(b, g, s, 0, first and s == 0)
                    maximum_products(nc, pe, a, psS, mb, mg, some[0:1])
                    if s >= 2:
                        sums(b, g, s - 2, 1)
                    elif not first:
                        sums(pb, pg, SLOTS - 2 + s, 1)
                    maximum_products(nc, pe, a, psS, mb, mg, some[1:2])
                    for r in (1, 2):
                        scores(b, g, s, r, first and s == 0)
                    maximum_products(nc, pe, a, psS, mb, mg, some[2:3])
                    if s >= 1:
                        sums(b, g, s - 1, 0, first and s == 1)
                    elif not first:
                        sums(pb, pg, SLOTS - 1, 0)
                    maximum_products(nc, pe, a, psS, mb, mg, some[3:4])
                    scores(b, g, s, 3)
                    if s == 2 and not first:
                        sums_T(pb, pg, 1, (mxT_ready, before(b, g, 2) + 2))
                    if s == QT + 2:
                        sums_T(b, g, 0, (ot_ready, before(b, g, 2) + 1))
                    if s in MAX_T and not last:
                        v = MAX_T.index(s)
                        maxima_rows(nc, pe, a, psX, identb, nb, ng, v, (mxT_ready, before(nb, ng, 2) + 1) if v else
                                    (ot_ready, before(b, g, 2) + 2))

            pe.wait_ge(psO_cleared, 1)
            slots(0, 0, range(EARLY), first=True)
            with pe.Fori(0, B - 1) as b:
                for g in range(NG):
                    slots(b, g, range(EARLY, SLOTS))
                    slots(*following(b, g), range(EARLY))
            for g in range(NG):
                slots(B - 1, g, range(EARLY, SLOTS), last=g == NG - 1)
                if g + 1 < NG:
                    slots(B - 1, g + 1, range(EARLY), last=g + 1 == NG - 1)
            sums(B - 1, NG - 1, SLOTS - 2, 1)
            for c in range(2):
                sums(B - 1, NG - 1, SLOTS - 1, c)
            sums_T(B - 1, NG - 1, 1, (ot_ready, before(B - 1, NG - 1, 2) + 2))


def out_projection_phase(nc, tag, X, stats, ident, wo, weights_loaded, O):
    ctx = ExitStack()
    sems = []
    ctx.callback(release, nc, sems)
    with ctx:
        sb = lambda n, s, d=F32: ctx.enter_context(nc.sbuf_tensor(f"{tag}_{n}", s, d))
        sem = lambda n: new_semaphore(nc, sems, f"{tag}_{n}")
        o = [sb(f"o{u}", [P, D]) for u in range(4)]
        oT = [sb(f"oT{u}", [P, KD, P]) for u in range(2)]
        psT = [ctx.enter_context(nc.psum_tensor(f"{tag}_psT{u}", [P, 512], F32)) for u in range(2)]
        psY = [ctx.enter_context(nc.psum_tensor(f"{tag}_psY{u}", [P, 512], F32)) for u in range(2)]
        o_copied = sem("o_copied"); T_done = sem("T_done"); oT_ready = sem("oT_ready"); y_done = sem("y_done"); y_used = sem("y_used")
        block = ctx.enter_context(nc.Block())

        @block.scalar
        def _(act):
            def rows_out(t, u):
                act.wait_ge(T_done, t + 1)
                nc.scalar.copy(oT[u % 2][:, :, :].rearrange("p k t -> p (k t)"), psT[u % 2][:, 0:D]).then_inc(oT_ready, 1)

            for u in range(4):
                nc.scalar.copy(o[u][:, :], O[:, u, :]).then_inc(o_copied, 1)
            with act.Fori(0, NT // 4 - 1) as tt:
                for u in range(4):
                    rows_out(tt * 4 + u, u)
                    nc.scalar.copy(o[u][:, :], O[:, tt * 4 + (u + 4), :]).then_inc(o_copied, 1)
            for u in range(4):
                rows_out(NT - 4 + u, u)

        @block.vector
        def _(dve):
            with dve.Fori(0, NT // 4) as tt:
                for u in range(4):
                    t = tt * 4 + u
                    dve.wait_ge(y_done, t + 1)
                    nc.vector.tensor_tensor(X[:, t, :], X[:, t, :], psY[u % 2][:, 0:D], ALU.add).then_inc(y_used, 1)
                    dve.wait_ge(y_used, t + 1)
                    nc.vector.bn_stats(stats[:, t, :], X[:, t, :])

        @block.tensor
        def _(pe):
            def transposes(t, u, first=False):
                pe.wait_ge(o_copied, t + 1)
                if not first:
                    pe.wait_ge(oT_ready, t - 1)
                for k in range(KD):
                    last = nc.tensor.transpose(psT[u % 2][:, k * P:(k + 1) * P], o[u][:, k * P:(k + 1) * P], ident[:, :])
                last.then_inc(T_done, 1)

            def product(t, u, first=False):
                pe.wait_ge(oT_ready, t + 1)
                if not first:
                    pe.wait_ge(y_used, t - 1)
                for k in range(KD):
                    last = nc.tensor.matmul(psY[u % 2][:, 0:D], oT[u % 2][:, k, :], wo[:, k, :],
                                            start=(k == 0), stop=(k == KD - 1))
                last.then_inc(y_done, 1)

            transposes(0, 0, True)
            pe.wait_ge(*weights_loaded)
            for t in range(3):
                transposes(t + 1, t + 1, t == 0)
                product(t, t, t < 2)
            with pe.Fori(0, NT // 4 - 1) as tt:
                for u in range(4):
                    t = tt * 4 + (3 + u)
                    transposes(t + 1, u)
                    product(t, (3 + u) % 4)
            product(NT - 1, 3)


def memory_moe_attention_moe_kernel(nc, x, m0T, w1T, w2T, rates_w, rates_b, gate_w, gate_b,
                                    gate_up, down_a, down_b, router, wqk, wv, wo, bqk, bv, bo, out):
    ctx = ExitStack()
    with ctx:
        def alloc(where, name, shape, dtype=F32):
            return where.enter_context(nc.sbuf_tensor(name, shape, dtype))

        X = alloc(ctx, "X", [P, NT, D])
        stats = alloc(ctx, "stats", [P, NT, 6])
        ident = alloc(ctx, "ident", [P, P]); identb = alloc(ctx, "identb", [P, P], BF16)
        ones = alloc(ctx, "ones", [P, P])
        work = alloc(ctx, "work", [P, NT, D])
        W = {"router": alloc(ctx, "W_router", [P, KD, E + 1])}
        Wqk = alloc(ctx, "Wqk", [P, KD, 2 * D]); Wv = alloc(ctx, "Wv", [P, KD, D])
        Bqk = alloc(ctx, "Bqk", [P, 2 * KD]); Bv = alloc(ctx, "Bv", [P, D]); Bo = alloc(ctx, "Bo", [P, D])
        xn_d = nc.dram_tensor("normalised_rows", [TOKENS, D], F32).ap()
        ys = nc.dram_tensor("expert_rows", [ROWS_ALL + SLOTS_ALL, D], F32).ap()
        qk_d = nc.dram_tensor("query_key_parts", [2, 3, B, D, S], BF16).ap()
        v_d = nc.dram_tensor("values", [B, NG, P, QT, GROUP * VC], F32).ap()

        sem = lambda n: ctx.enter_context(nc.semaphore(n))
        x_loaded = [sem(f"x_loaded{q}") for q in range(4)]; memory_loaded = sem("memory_loaded"); moe_loaded = sem("moe_loaded"); experts_loaded = sem("experts_loaded")
        attention_loaded = sem("attention_loaded"); zero_ready = sem("zero_ready")
        ident_ready = sem("ident_ready"); stored = sem("stored"); wo_loaded = sem("wo_loaded")

        def load_down(sp, down, loaded):
            sp.dma_start(down[:, 0:I // P, :, :], down_a).then_inc(loaded, 16)
            sp.dma_start(down[0:I % P, I // P, :, :], down_b).then_inc(loaded, 16)

        first_half = ExitStack()
        with first_half:
            M0 = alloc(first_half, "M0", [P, KD, D])
            W1 = alloc(first_half, "W1", [P, KD, D]); W2 = alloc(first_half, "W2", [P, KD, D])
            Rw = alloc(first_half, "Rw", [P, KD, 2]); Rb = alloc(first_half, "Rb", [ROWS + 2, 1])
            Gw = alloc(first_half, "Gw", [P, KD]); Gb = alloc(first_half, "Gb", [P, 1])
            W["down"] = alloc(first_half, "W_down1", [P, KI, E + 1, D])
            W["gate_up"] = alloc(first_half, "W_gate_up1", [P, KD, E + 1, 2 * I])

            with nc.Block() as block:
                @block.sync
                def _(sp):
                    for q, loaded in enumerate(x_loaded):
                        tiles = slice(q * NT // len(x_loaded), (q + 1) * NT // len(x_loaded))
                        sp.dma_start(X[:, tiles, :], x[:, tiles, :]).then_inc(loaded, 16)
                    for dst, src in ((M0, m0T), (W1, w1T), (W2, w2T), (Rw, rates_w)):
                        sp.dma_start(dst[:, :, :], src).then_inc(memory_loaded, 16)
                    sp.dma_start(Rb[ROWS:, :], rates_b).then_inc(memory_loaded, 16)
                    sp.dma_start(Gw[:, :], gate_w).then_inc(memory_loaded, 16)
                    sp.dma_start(Gb[:, :], gate_b.to_broadcast([P, 1])).then_inc(memory_loaded, 16)
                    sp.dma_start(W["router"][:, :, :], router).then_inc(moe_loaded, 16)
                    sp.dma_start(W["gate_up"][:, :, :, :], gate_up).then_inc(moe_loaded, 16)
                    sp.wait_ge(zero_ready, 1)
                    load_down(sp, W["down"], moe_loaded)
                    for dst, src in ((Wqk, wqk), (Wv, wv)):
                        sp.dma_start(dst[:, :, :], src).then_inc(attention_loaded, 16)
                    sp.dma_start(Bqk[:, :], bqk).then_inc(attention_loaded, 16)
                    sp.dma_start(Bv[:, :], bv.to_broadcast([P, D])).then_inc(attention_loaded, 16)
                    sp.dma_start(Bo[:, :], bo.to_broadcast([P, D])).then_inc(attention_loaded, 16)

                @block.vector
                def _(dve):
                    nc.vector.memset(W["down"][I % P:P, I // P, :, :], 0.0)
                    nc.vector.memset(ones[:, :], 1.0)
                    dve.drain().then_inc(zero_ready, 1)

                @block.gpsimd
                def _(pool):
                    nc.gpsimd.memset(ident[:, :], 0.0).then_inc(ident_ready, 1)
                    pool.wait_ge(ident_ready, 1)
                    nc.gpsimd.affine_select(out=ident[:, :], in_=ident[:, :], compare_op=ALU.not_equal, fill=1.0,
                                            base=0, pattern=[[-1, P]], channel_multiplier=1).then_inc(ident_ready, 1)
                    pool.wait_ge(ident_ready, 2)
                    nc.gpsimd.tensor_copy(identb[:, :], ident[:, :])

            memory_phase(nc, "mem", X, x_loaded, stats, ident, ones, work, M0, W1, W2, (memory_loaded, 16 * 7), Rw, Rb, Gw, Gb)
            ffn_phase(nc, "moe1", X, stats, ident, ones, work, W, (moe_loaded, 16 * 4), xn_d, ys)

        attention_phase(nc, "att", X, stats, ident, identb, Wqk, Wv, Bqk, Bv, Bo, (attention_loaded, 16 * 5),
                        qk_d, v_d, work)

        second_half = ExitStack()
        with second_half:
            W["down"] = alloc(second_half, "W_down2", [P, KI, E + 1, D])
            W["gate_up"] = alloc(second_half, "W_gate_up2", [P, KD, E + 1, 2 * I]); Wo = alloc(second_half, "Wo", [P, KD, D])
            with nc.Block() as block:
                @block.vector
                def _(dve):
                    nc.vector.memset(W["down"][I % P:P, I // P, :, :], 0.0)
                    dve.drain().then_inc(zero_ready, 1)

                @block.sync
                def _(sp):
                    sp.dma_start(Wo[:, :, :], wo).then_inc(wo_loaded, 16)
                    sp.dma_start(W["gate_up"][:, :, :, :], gate_up).then_inc(experts_loaded, 16)
                    sp.wait_ge(zero_ready, 2)
                    load_down(sp, W["down"], experts_loaded)
            out_projection_phase(nc, "out", X, stats, ident, Wo, (wo_loaded, 16), work)
            ffn_phase(nc, "moe2", X, stats, ident, ones, work, W, (experts_loaded, 16 * 3), xn_d, ys, (out, stored))


def kernel(**inputs):
    import numpy as np
    import concourse.bacc as bacc
    from concourse.bass_utils import run_bass_kernel_spmd

    a = {name: np.asarray(v) for name, v in inputs.items()}
    mem = lambda n: a["L0_attn_a_" + n]
    att = lambda n: a["L0_attn_b_" + n]
    moe = lambda n: a["L0_ffn_" + n]
    tiles = lambda w: w.reshape(-1, P, w.shape[-1]).transpose(1, 0, 2)
    wqkv = att("Wqkv").reshape(HEADS, 3, HD, D)
    bqkv = att("bqkv").reshape(HEADS, 3, HD)
    experts = lambda n: np.concatenate([moe("w_" + n), moe("sw_" + n)[None]])
    gate_up = np.concatenate([experts("gate"), experts("up")], axis=2)
    down = experts("down")
    arrays = {
        "x": mem("x").reshape(NT, P, D).transpose(1, 0, 2),
        "m0T": tiles(mem("M_init").T), "w1T": tiles(mem("vg_w1").T), "w2T": tiles(mem("vg_w2").T),
        "rates_w": tiles(np.stack([mem("eta_w"), mem("alpha_w")], 1)),
        "rates_b": np.concatenate([mem("eta_b"), mem("alpha_b")]).reshape(2, 1),
        "gate_w": mem("gate_w").reshape(KD, P).T, "gate_b": mem("gate_b").reshape(1, 1),
        "gate_up": gate_up.reshape(E + 1, KD, P, 2 * I).transpose(2, 1, 0, 3),
        "down_a": down[:, :I // P * P].reshape(E + 1, I // P, P, D).transpose(2, 1, 0, 3),
        "down_b": down[:, I // P * P:].transpose(1, 0, 2),
        "router": tiles(np.concatenate([moe("gate_w"), moe("shared_gate_w")]).T),
        "wqk": tiles(wqkv[:, 0:2].transpose(3, 1, 0, 2).reshape(D, 2 * D)),
        "wv": tiles(wqkv[:, 2].transpose(2, 0, 1).reshape(D, D)), "wo": tiles(att("Wo").T),
        "bqk": bqkv[:, 0:2].transpose(1, 0, 2).reshape(2 * KD, P).T,
        "bv": bqkv[:, 2].reshape(1, D), "bo": att("bo").reshape(1, D),
    }
    nc = bacc.Bacc("TRN2", target_bir_lowering=False, num_devices=1)
    feeds, args = {}, []
    for name, v in arrays.items():
        v = np.ascontiguousarray(v)
        feeds[f"in_{name}_dram"] = v
        args.append(nc.dram_tensor(f"in_{name}_dram", v.shape, mybir.dt.from_np(v.dtype), kind="ExternalInput").ap())
    args.append(nc.dram_tensor("out_0_dram", (P, NT, D), F32, kind="ExternalOutput").ap())
    memory_moe_attention_moe_kernel(nc, *args)
    r = run_bass_kernel_spmd(nc, [feeds], core_ids=[0])
    return r.results[0]["out_0_dram"].transpose(1, 0, 2).reshape(B, S, D)
```
